# Optimizing a Trainium2 kernel written in Bass

```python
import numpy as np
import jax
import jax.numpy as jnp

def _softmax(x, axis=-1):
    return jax.nn.softmax(x, axis=axis)

def _gelu(x):
    return jax.nn.gelu(x, approximate=True)

def _silu(x):
    return jax.nn.silu(x)

def _sigmoid(x):
    return jax.nn.sigmoid(x)

def _layernorm(x, axis=-1, eps=1e-05):
    m = jnp.mean(x, axis=axis, keepdims=True)
    v = jnp.var(x, axis=axis, keepdims=True)
    return (x - m) / jnp.sqrt(v + eps)

def _scatter_add(tgt, idx, src, axis=0):
    return tgt.at[idx].add(src)

def _segment_sum(src, seg, n):
    return jax.ops.segment_sum(src, seg, n)
kernel_name = 'mk_vit_tower_cls_d1_tok_img768_r4_761983'

def setup_inputs(seed: int=0):
    np.random.seed(seed)
    _w = jnp.asarray

    def _rec_inputs():
        import jax
        import jax.numpy as jnp
        _rk = jax.random.key(seed)
        x = -0.000356955 + 1 * jax.random.normal(jax.random.fold_in(_rk, 1), (64, 3, 224, 224), jnp.float32)
        cls_tok = 0.02 * jax.random.normal(jax.random.fold_in(_rk, 5), (1, 1, 192), jnp.float32)
        return (x, cls_tok)
    x, cls_tok = _rec_inputs()

    def _L0_tok_setup():
        import jax, jax.numpy as jnp
        import numpy as np
        N_PATCHES = 14
        HIDDEN_D = 192
        N_HEADS = 12
        D_HEAD = HIDDEN_D // N_HEADS
        SEQ = N_PATCHES ** 2 + 1
        INPUT_D = 3 * 16 * 16
        LN_EPS = 1e-05

        def positional_embeddings(seq_len, d):
            i = jnp.arange(seq_len, dtype=jnp.float32)[:, None]
            j = jnp.arange(d, dtype=jnp.float32)[None, :]
            even = (jnp.arange(d) % 2 == 0)[None, :]
            denom_even = jnp.power(10000.0, j / d)
            denom_odd = jnp.power(10000.0, (j - 1.0) / d)
            return jnp.where(even, jnp.sin(i / denom_even), jnp.cos(i / denom_odd))

        def _forward(images, W_map, b_map, class_token, ln_w, ln_b, Wq, bq, Wk, bk, Wv, bv):
            n = images.shape[0]
            patches = images.reshape(n, N_PATCHES ** 2, INPUT_D)
            tokens = jnp.einsum('npi,di->npd', patches, W_map) + b_map
            cls = jnp.broadcast_to(class_token[None], (n, 1, HIDDEN_D))
            tokens = jnp.concatenate([cls, tokens], axis=1)
            tokens = tokens + positional_embeddings(SEQ, HIDDEN_D)[None]
            mean = jnp.mean(tokens, axis=(-2, -1), keepdims=True)
            var = jnp.var(tokens, axis=(-2, -1), keepdims=True)
            x = (tokens - mean) / jnp.sqrt(var + LN_EPS) * ln_w + ln_b
            xh = x.reshape(n, SEQ, N_HEADS, D_HEAD)
            q = jnp.einsum('bshd,hed->bshe', xh, Wq) + bq[None, None]
            k = jnp.einsum('bshd,hed->bshe', xh, Wk) + bk[None, None]
            v = jnp.einsum('bshd,hed->bshe', xh, Wv) + bv[None, None]
            att = jax.nn.softmax(jnp.einsum('bshd,bthd->bhst', q, k) / jnp.sqrt(jnp.float32(D_HEAD)), axis=-1)
            msa = jnp.einsum('bhst,bthd->bshd', att, v).reshape(n, SEQ, HIDDEN_D)
            return tokens + msa
        key = jax.random.key(seed)
        ks = jax.random.split(key, 12)
        s = 0.02
        return {'images': jax.random.normal(ks[0], (128, 3, 224, 224), dtype=jnp.float32), 'W_map': jax.random.normal(ks[1], (HIDDEN_D, INPUT_D), dtype=jnp.float32) * s, 'b_map': jax.random.normal(ks[2], (HIDDEN_D,), dtype=jnp.float32) * s, 'class_token': jax.random.uniform(ks[3], (1, HIDDEN_D), dtype=jnp.float32), 'ln_w': jnp.ones((SEQ, HIDDEN_D), dtype=jnp.float32), 'ln_b': jnp.zeros((SEQ, HIDDEN_D), dtype=jnp.float32), 'Wq': jax.random.normal(ks[4], (N_HEADS, D_HEAD, D_HEAD), dtype=jnp.float32) * s, 'bq': jax.random.normal(ks[5], (N_HEADS, D_HEAD), dtype=jnp.float32) * s, 'Wk': jax.random.normal(ks[6], (N_HEADS, D_HEAD, D_HEAD), dtype=jnp.float32) * s, 'bk': jax.random.normal(ks[7], (N_HEADS, D_HEAD), dtype=jnp.float32) * s, 'Wv': jax.random.normal(ks[8], (N_HEADS, D_HEAD, D_HEAD), dtype=jnp.float32) * s, 'bv': jax.random.normal(ks[9], (N_HEADS, D_HEAD), dtype=jnp.float32) * s}
    _L0_tok_all = _L0_tok_setup()
    _L0_tok_in = {k: v for k, v in _L0_tok_all.items() if k in ('W_map', 'b_map', 'class_token', 'ln_w', 'ln_b', 'Wq', 'bq', 'Wk', 'bk', 'Wv', 'bv')}
    del _L0_tok_all

    def _L0_attn_setup():
        import jax, jax.numpy as jnp
        import numpy as np
        DIM, H = (192, 12)
        DHEAD = DIM // H
        DATA_W, DATA_F = (32, 16)
        WQ = WK = WV = WP = (16, 8)
        BQ = BK = BV = BP = (16, 8)
        DQ = DK = DV = DS = DZ = (16, 8)
        OUT_W, OUT_F = (32, 8)

        def qfix(x, width, frac):
            scale = jnp.float32(2.0 ** frac)
            lo = -2.0 ** (width - 1)
            hi = 2.0 ** (width - 1) - 1
            return jnp.clip(jnp.round(x * scale), lo, hi) / scale
        key = jax.random.key(seed)
        ks = jax.random.split(key, 5)
        return {'q_in': jax.random.normal(ks[0], (2, 512, DIM), dtype=jnp.float32), 'wqkv': jax.random.normal(ks[1], (3 * DIM, DIM), dtype=jnp.float32) * 0.05, 'bqkv': jax.random.normal(ks[2], (3 * DIM,), dtype=jnp.float32) * 0.05, 'wp': jax.random.normal(ks[3], (DIM, DIM), dtype=jnp.float32) * 0.05, 'bp': jax.random.normal(ks[4], (DIM,), dtype=jnp.float32) * 0.05}
    _L0_attn_all = _L0_attn_setup()
    _L0_attn_in = {k: v for k, v in _L0_attn_all.items() if k in ('wqkv', 'bqkv', 'wp', 'bp')}
    del _L0_attn_all

    def _L0_ffn_setup():
        import jax, jax.numpy as jnp
        import numpy as np
        B, S, H = (4, 2048, 192)
        E, K = (8, 2)
        key = jax.random.key(seed)
        ks = jax.random.split(key, 5)
        scale = 1.0 / np.sqrt(H)
        x = jax.random.normal(ks[0], (B, S, H), dtype=jnp.float32)
        router_w = jax.random.uniform(ks[1], (E, H), jnp.float32, -scale, scale)
        router_b = jax.random.uniform(ks[2], (E,), jnp.float32, -scale, scale)
        expert_w = jax.random.uniform(ks[3], (E, H, H), jnp.float32, -scale, scale)
        expert_b = jax.random.uniform(ks[4], (E, H), jnp.float32, -scale, scale)
        return {'x': x, 'router_w': router_w, 'router_b': router_b, 'expert_w': expert_w, 'expert_b': expert_b}
    _L0_ffn_all = _L0_ffn_setup()
    _L0_ffn_in = {k: v for k, v in _L0_ffn_all.items() if k in ('router_w', 'router_b', 'expert_w', 'expert_b')}
    del _L0_ffn_all
    return {'x': x, 'cls_tok': cls_tok, 'L0_tok_W_map': _L0_tok_in['W_map'], 'L0_tok_b_map': _L0_tok_in['b_map'], 'L0_tok_class_token': _L0_tok_in['class_token'], 'L0_tok_ln_w': _L0_tok_in['ln_w'], 'L0_tok_ln_b': _L0_tok_in['ln_b'], 'L0_tok_Wq': _L0_tok_in['Wq'], 'L0_tok_bq': _L0_tok_in['bq'], 'L0_tok_Wk': _L0_tok_in['Wk'], 'L0_tok_bk': _L0_tok_in['bk'], 'L0_tok_Wv': _L0_tok_in['Wv'], 'L0_tok_bv': _L0_tok_in['bv'], 'L0_attn_wqkv': _L0_attn_in['wqkv'], 'L0_attn_bqkv': _L0_attn_in['bqkv'], 'L0_attn_wp': _L0_attn_in['wp'], 'L0_attn_bp': _L0_attn_in['bp'], 'L0_ffn_router_w': _L0_ffn_in['router_w'], 'L0_ffn_router_b': _L0_ffn_in['router_b'], 'L0_ffn_expert_w': _L0_ffn_in['expert_w'], 'L0_ffn_expert_b': _L0_ffn_in['expert_b']}

def reference(x, cls_tok, L0_tok_W_map, L0_tok_b_map, L0_tok_class_token, L0_tok_ln_w, L0_tok_ln_b, L0_tok_Wq, L0_tok_bq, L0_tok_Wk, L0_tok_bk, L0_tok_Wv, L0_tok_bv, L0_attn_wqkv, L0_attn_bqkv, L0_attn_wp, L0_attn_bp, L0_ffn_router_w, L0_ffn_router_b, L0_ffn_expert_w, L0_ffn_expert_b):
    import jax
    import jax.numpy as jnp

    def _L0_tok_ref(images, W_map, b_map, class_token, ln_w, ln_b, Wq, bq, Wk, bk, Wv, bv):
        import jax, jax.numpy as jnp
        import numpy as np
        N_PATCHES = 14
        HIDDEN_D = 192
        N_HEADS = 12
        D_HEAD = HIDDEN_D // N_HEADS
        SEQ = N_PATCHES ** 2 + 1
        INPUT_D = 3 * 16 * 16
        LN_EPS = 1e-05

        def positional_embeddings(seq_len, d):
            i = jnp.arange(seq_len, dtype=jnp.float32)[:, None]
            j = jnp.arange(d, dtype=jnp.float32)[None, :]
            even = (jnp.arange(d) % 2 == 0)[None, :]
            denom_even = jnp.power(10000.0, j / d)
            denom_odd = jnp.power(10000.0, (j - 1.0) / d)
            return jnp.where(even, jnp.sin(i / denom_even), jnp.cos(i / denom_odd))

        def _forward(images, W_map, b_map, class_token, ln_w, ln_b, Wq, bq, Wk, bk, Wv, bv):
            n = images.shape[0]
            patches = images.reshape(n, N_PATCHES ** 2, INPUT_D)
            tokens = jnp.einsum('npi,di->npd', patches, W_map) + b_map
            cls = jnp.broadcast_to(class_token[None], (n, 1, HIDDEN_D))
            tokens = jnp.concatenate([cls, tokens], axis=1)
            tokens = tokens + positional_embeddings(SEQ, HIDDEN_D)[None]
            mean = jnp.mean(tokens, axis=(-2, -1), keepdims=True)
            var = jnp.var(tokens, axis=(-2, -1), keepdims=True)
            x = (tokens - mean) / jnp.sqrt(var + LN_EPS) * ln_w + ln_b
            xh = x.reshape(n, SEQ, N_HEADS, D_HEAD)
            q = jnp.einsum('bshd,hed->bshe', xh, Wq) + bq[None, None]
            k = jnp.einsum('bshd,hed->bshe', xh, Wk) + bk[None, None]
            v = jnp.einsum('bshd,hed->bshe', xh, Wv) + bv[None, None]
            att = jax.nn.softmax(jnp.einsum('bshd,bthd->bhst', q, k) / jnp.sqrt(jnp.float32(D_HEAD)), axis=-1)
            msa = jnp.einsum('bhst,bthd->bshd', att, v).reshape(n, SEQ, HIDDEN_D)
            return tokens + msa
        return _forward(images, W_map, b_map, class_token, ln_w, ln_b, Wq, bq, Wk, bk, Wv, bv)

    def _L0_attn_ref(q_in, wqkv, bqkv, wp, bp):
        import jax, jax.numpy as jnp
        import numpy as np
        DIM, H = (192, 12)
        DHEAD = DIM // H
        DATA_W, DATA_F = (32, 16)
        WQ = WK = WV = WP = (16, 8)
        BQ = BK = BV = BP = (16, 8)
        DQ = DK = DV = DS = DZ = (16, 8)
        OUT_W, OUT_F = (32, 8)

        def qfix(x, width, frac):
            scale = jnp.float32(2.0 ** frac)
            lo = -2.0 ** (width - 1)
            hi = 2.0 ** (width - 1) - 1
            return jnp.clip(jnp.round(x * scale), lo, hi) / scale
        B, N, _ = q_in.shape
        w = wqkv.reshape(H, 3 * DHEAD, DIM)
        b = bqkv.reshape(H, 3 * DHEAD)
        wq_, wk_, wv_ = (w[:, :DHEAD], w[:, DHEAD:2 * DHEAD], w[:, 2 * DHEAD:])
        bq_, bk_, bv_ = (b[:, :DHEAD], b[:, DHEAD:2 * DHEAD], b[:, 2 * DHEAD:])
        x = qfix(q_in, DATA_W, DATA_F)

        def qlin(wt, bt, wcfg, bcfg, ocfg):
            y = jnp.einsum('bnd,hed->bhne', x, qfix(wt, *wcfg)) + qfix(bt, *bcfg)[None, :, None, :]
            return qfix(y, *ocfg)
        q = qlin(wq_, bq_, WQ, BQ, DQ)
        k = qlin(wk_, bk_, WK, BK, DK)
        v = qlin(wv_, bv_, WV, BV, DV)
        s = qfix(jnp.einsum('bhne,bhme->bhnm', q, k), *DS)
        z = qfix(jnp.einsum('bhnm,bhme->bhne', s, v), *DZ)
        zc = z.transpose(0, 2, 1, 3).reshape(B, N, DIM)
        out = jnp.einsum('bnd,ed->bne', qfix(zc, *DZ), qfix(wp, *WP)) + qfix(bp, *BP)
        return qfix(out, OUT_W, OUT_F)

    def _L0_ffn_ref(x, router_w, router_b, expert_w, expert_b):
        import jax, jax.numpy as jnp
        import numpy as np
        B, S, H = (4, 2048, 192)
        E, K = (8, 2)
        scores = jnp.einsum('bsh,eh->bse', x, router_w) + router_b
        probs = jax.nn.softmax(scores, axis=-1)
        top_probs, expert_ids = jax.lax.top_k(probs, K)
        y = jnp.einsum('bsh,edh->bsed', x, expert_w) + expert_b
        out_k = jnp.take_along_axis(y, expert_ids[..., None], axis=2)
        w = top_probs / (jnp.sum(top_probs, axis=-1, keepdims=True) + 1e-09)
        out = jnp.einsum('bsk,bskh->bsh', w, out_k)
        return out
    h = _L0_tok_ref(x, L0_tok_W_map, L0_tok_b_map, L0_tok_class_token, L0_tok_ln_w, L0_tok_ln_b, L0_tok_Wq, L0_tok_bq, L0_tok_Wk, L0_tok_bk, L0_tok_Wv, L0_tok_bv)
    h = jnp.concatenate([jnp.broadcast_to(cls_tok, (h.shape[0], 1, h.shape[2])), h], axis=1)
    h = h + _L0_attn_ref(_layernorm(h, axis=-1), L0_attn_wqkv, L0_attn_bqkv, L0_attn_wp, L0_attn_bp)
    h = h + _L0_ffn_ref(_layernorm(h, axis=-1), L0_ffn_router_w, L0_ffn_router_b, L0_ffn_expert_w, L0_ffn_expert_b)
    return h

_drawn_inputs = setup_inputs


def setup_inputs(seed=0):
    import zlib

    import numpy as np

    out = dict(_drawn_inputs(seed))
    spreads = {'L0_tok_ln_w': (1.0, 0.6), 'L0_tok_ln_b': (0.0, 0.8)}
    factors = {'L0_tok_Wq': 8.0,
     'L0_tok_bq': 8.0,
     'L0_tok_Wk': 8.0,
     'L0_tok_bk': 64.0,
     'L0_attn_bp': 46.686,
     'L0_ffn_router_w': 6.237,
     'L0_ffn_router_b': 40.236,
     'L0_ffn_expert_w': 5.688,
     'L0_ffn_expert_b': 64.0}
    for name, (base, spread) in spreads.items():
        noise = np.random.default_rng([zlib.crc32(name.encode()), seed]).standard_normal(out[name].shape)
        drawn = base * np.exp(spread * noise) if base else spread * noise
        out[name] = jnp.asarray(drawn.astype(out[name].dtype))
    for name, factor in factors.items():
        out[name] = (out[name] * factor).astype(out[name].dtype)
    return out
```

```python
from contextlib import ExitStack

import numpy as np

import concourse.bass as bass
from concourse import mybir

F32 = mybir.dt.float32
BF16 = mybir.dt.bfloat16
I16 = mybir.dt.int16
I32 = mybir.dt.int32
ALU = mybir.AluOpType
ACT = mybir.ActivationFunctionType
AX = mybir.AxisListType

D = 192
HEADS = 12
DH = D // HEADS
ROWS = 198
T = ROWS // 2
KD = 768
KC = KD // 128
HC = D // 2
PARTS = 6
SK = PARTS * DH
PAIRS = HEADS // 2
GROUPS = HEADS // 4
E = 8
EPS = 1e-5
ROUND = 1.5 * 2.0 ** 23
I16MAX, I16MIN = 32767.0, -32768.0
NTOK = (ROWS - 1) * D

LAG = {"A": 0, "B": 1, "C": 2}


def pe_order():
    order = [("A", "xt0", "G"), ("A", "xt1", "G"), ("A", "xt2", "G"), ("A", "tok", "G"),
             ("B", "xT", "G"), ("C", "xT", "G"), ("B", "qk0", "G"), ("B", "qk1", "G"),
             ("A", "sum", "G"), ("B", "v", "G"), ("A", "sq", "G"), ("C", "rt", "G"),
             ("C", "e0", "G"), ("A", "xT", "G"), ("C", "e1", "G"), ("A", "qk0", "G"),
             ("A", "qk1", "G"), ("A", "v", "G"), ("B", "st0", "T"), ("B", "sc0", "S"),
             ("C", "e2", "G"), ("A", "st0", "T"), ("A", "mx0", "S")]
    for p in range(PAIRS):
        if p + 1 < PAIRS:
            order += [("B", f"st{p + 1}", "T")]
        if 1 <= p < 5:
            order += [("C", f"e{p + 2}", "G")]
        order += [("A", f"nm{p}", "T")]
        if p + 1 < PAIRS:
            order += [("A", f"st{p + 1}", "T"), ("B", f"sc{p + 1}", "S")]
        if p in (2, 4):
            order += [("B", f"z{p // 2 - 1}", "Z")]
        if p + 1 < PAIRS:
            order += [("A", f"mx{p + 1}", "S")]
        order += [("A", f"sc{p}", "S")]
        if p in (3, 5):
            order += [("A", f"z{(p - 3) // 2}", "Z")]
        if p == 4:
            order += [("A", "zt0", "G")]
    return order + [("C", "e7", "G"), ("B", "z2", "Z"), ("A", "zt1", "G"), ("B", "out", "G"),
                    ("A", "z2", "Z"), ("A", "zt2", "G")]


class Turn:

    def __init__(self, t, images):
        self.t, self.images = t, images
        self.live = "ABC" if not isinstance(t, int) else "".join(
            s for s in "ABC" if 0 <= t - LAG[s] < images)

    def image(self, stage):
        return self.t - LAG[stage]

    def later(self, stage):
        return not isinstance(self.t, int) or self.t > LAG[stage]

    def previous(self):
        return Turn(self.t - 1, self.images)


class Steps:

    def __init__(self, sem, stage, names):
        self.sem, self.stage, self.names = sem, stage, names

    def at(self, turn, name, back=0):
        per, k, late = len(self.names), self.names.index(name) + 1, LAG[self.stage] + back
        return turn.t * per + (k - late * per)


class Banks:

    def __init__(self, kind, banks, reader, fresh):
        self.order = [(s, n) for s, n, k in pe_order() if k == kind]
        self.banks, self.reader, self.fresh = banks, reader, fresh

    def slot(self, use):
        return self.order.index(use) % len(self.banks)

    def __call__(self, stage, name):
        return self.banks[self.slot((stage, name))]

    def vacant(self, turn, stage, name):
        mine = [u for u in self.order if self.slot(u) == self.slot((stage, name))]
        before = mine[:mine.index((stage, name))]
        while True:
            live = [u for u in before if u[0] in turn.live]
            if live:
                steps, step = self.reader[live[-1]]
                return steps.sem, steps.at(turn, step)
            if isinstance(turn.t, int) and turn.t == 0:
                return self.fresh
            turn, before = turn.previous(), mine


def run_turns(engine, images, body):
    first = 3
    for t in range(first):
        body(Turn(t, images))
    with engine.Fori(first, images) as t:
        body(Turn(t, images))
    for t in range(images, images + 2):
        body(Turn(t, images))


def tower(nc, x, pos, base, ln_w, ln_b, wmap, w_a, w_b, w_p, b_p, w_r, w_e, cls, eye, out):
    images = x.shape[0]
    ctx = ExitStack()
    with ctx:
        def sb(name, shape, dt=F32):
            return ctx.enter_context(nc.sbuf_tensor(name, shape, dt))

        def ps(name, shape, dt=F32):
            return ctx.enter_context(nc.psum_tensor(name, shape, dt))

        def sem(name):
            return ctx.enter_context(nc.semaphore(name))

        W_map = sb("W_map", [128, KC, D])
        addend = sb("addend", [T, 2, D])
        base_sb = sb("base_sb", [T, 2, D])
        lnw = sb("lnw", [T, 2, D])
        lnb = sb("lnb", [T, 2, D])
        Wa = sb("Wa", [HC + 1, 2, 3, HC])
        Wb = sb("Wb", [HC + 1, 2, 3 * D])
        Wp = sb("Wp", [128, GROUPS, D])
        bp = sb("bp", [T, D])
        Wr = sb("Wr", [HC + 1, 2, E])
        We = sb("We", [HC + 1, 2, E * D])
        clsrow = sb("clsrow", [1, D])
        ident = sb("ident", [128, 128])
        identb = sb("identb", [128, 128], BF16)
        ones = sb("ones", [T, T])
        ones_not0 = sb("ones_not0", [T, T])
        not0 = sb("not0", [T, 1])
        halfneg = sb("halfneg", [T, 2])
        rank = sb("rank", [T, 2, E])
        zero4 = sb("zero4", [T, 4])
        dve_scrap = sb("dve_scrap", [1, 2])
        pool_scrap = sb("pool_scrap", [T, 2])
        X = sb("X", [T, 2, KD])
        XT = sb("XT", [128, KC, ROWS])
        tok = sb("tok", [T, 2, D])
        rowsum = sb("rowsum", [T, 1])
        negmean = sb("negmean", [T, 1])
        sqs = sb("sqs", [T, 2])
        sqtmp = sb("sqtmp", [T, 2, D])
        varA = sb("varA", [T, 1])
        rstdA = sb("rstdA", [T, 1])
        xn = sb("xn", [T, 2, D])
        xTA = sb("xTA", [HC + 1, 2, ROWS])
        qkA = sb("qkA", [T, 2, 2, D])
        resid = sb("resid", [T, 2, 2, D])
        vA = sb("vA", [T, 2, HEADS, 32])
        stackA = sb("stackA", [T, 2, 2 * HEADS, SK], BF16)
        stA = sb("stA", [SK + 3, 2, 2, 2, ROWS], BF16)
        nm = sb("nm", [T, 2, 4])
        nmr = sb("nmr", [T, 2, 4])
        nms = sb("nms", [T, 2, 4, 3], BF16)
        PA = sb("PA", [T, 4, 2, 2, ROWS])
        zA = sb("zA", [128, 2, ROWS])
        rden = sb("rden", [T, 2, 4])
        hm = sb("hm", [T, 2, D])
        H = sb("H", [T, 2, D])
        bnB = sb("bnB", [T, 2, 6])
        mvB = sb("mvB", [T, 2, 2])
        varB = sb("varB", [T, 2])
        rstdB = sb("rstdB", [T, 2])
        scaleB = sb("scaleB", [T, 2])
        x2 = sb("x2", [T, 2, D])
        xTB = sb("xTB", [HC + 1, 2, ROWS])
        qkB = sb("qkB", [T, 2, 2, D], I16)
        v16 = sb("v16", [T, 2, D], I16)
        vB = sb("vB", [T, 2, HEADS, 32])
        stackB = sb("stackB", [T, 2, 2 * HEADS, SK], BF16)
        stB = sb("stB", [SK, 2, 2, 2, ROWS], BF16)
        S16 = sb("S16", [T, 2, 2 * 2 * ROWS], I16)
        SB = sb("SB", [T, 4, 2, 2, ROWS])
        z16 = sb("z16", [128, 2, ROWS], I16)
        zB = sb("zB", [128, GROUPS, ROWS])
        o32 = sb("o32", [T, 2, D], I32)
        H2 = sb("H2", [T, 2, D])
        bnC = sb("bnC", [T, 2, 6])
        mvC = sb("mvC", [T, 2, 2])
        varC = sb("varC", [T, 2])
        rstdC = sb("rstdC", [T, 2])
        x3 = sb("x3", [T, 2, D])
        xTC = sb("xTC", [HC + 1, 2, ROWS])
        top = sb("top", [T, 2])
        sc = sb("sc", [T, 2, E])
        pr = sb("pr", [T, 2, E])
        eq = sb("eq", [T, 2, E])
        sel1 = sb("sel1", [T, 2, E])
        rest = sb("rest", [T, 2, E])
        r1 = sb("r1", [T, 2])
        r2 = sb("r2", [T, 2])
        p1 = sb("p1", [T, 2])
        p2 = sb("p2", [T, 2])
        gate = sb("gate", [T, 2, E])
        acc = sb("acc", [T, 2, D])

        Gt = [ps(f"G{i}", [128, 512]) for i in range(2)]
        St = [ps(f"S{i}", [128, 2, 512]) for i in range(2)]
        Tt = [ps("T0", [128, 1024], BF16)]
        Zt = [ps("Z0", [128, 512])]

        steps_p = range(PAIRS)
        act_a = ["xt0", "xt1", "xt2", "sq0", "sq1", "xT", "qk0", "qk1", "v0", "v1", "high"]
        act_b = ["xT", "qk0", "qk1", "v", "s0"]
        dve_a = ["tok", "negmean", "var", "xn", "resid", "mid", "lowq", "lowk", "st0", "mx0"]
        dve_b = ["bn0", "bn1", "mv0", "mv1", "var", "scale", "x2a", "x2b", "x2", "high", "mid", "v", "st0", "f0"]
        pool_a = ["rstd", "xw", "x", "qhigh", "khigh", "qmid", "kmid"]
        for p in steps_p:
            act_b += [f"s{p + 1}"] if p < 5 else []
            act_a += [f"p{p}"]
            act_b += [f"z{(p - 2) // 2}"] if p in (2, 4) else []
            act_a += [f"z{(p - 3) // 2}"] if p in (3, 5) else []
            dve_b += [f"st{p + 1}"] if p < 5 else []
            dve_a += [f"nmT{p}"] + ([f"st{p + 1}", f"mx{p + 1}"] if p < 5 else [])
            dve_b += [f"f{p + 1}"] if p < 5 else []
            dve_b += [f"z{(p - 3) // 2}"] if p in (3, 5) else []
            dve_a += ["rden0", "hm0"] if p == 4 else []
            pool_a += [f"n1_{p}", f"n2_{p}", f"n3_{p}", f"n4_{p}", f"n5_{p}"]
        act_b += ["z2"]
        act_a += ["z2"]
        dve_a += ["rden1", "hm1"]
        dve_b += ["z2", "o32", "H2"]
        dve_a += ["rden2", "hm2", "H"]
        pool_a += ["H"]
        act_a_done = Steps(sem("act_a_done"), "A", act_a)
        act_b_done = Steps(sem("act_b_done"), "B", act_b)
        act_c_done = Steps(sem("act_c_done"), "C", ["xT", "exp"])
        dve_a_done = Steps(sem("dve_a_done"), "A", dve_a)
        dve_b_done = Steps(sem("dve_b_done"), "B", dve_b)
        dve_c_done = Steps(sem("dve_c_done"), "C",
                           ["bn0", "bn1", "mv0", "mv1", "var", "x3a", "x3b", "top", "sc", "sum", "rsum", "pr",
                            "p1", "eq1", "key1", "r1", "sel1", "rest", "p2", "eq2", "key2", "r2",
                            "sel2", "sel", "chosen", "den", "den2", "rden", "gate"]
                           + [f"acc{u}{e}" for u in range(E) for e in range(2)])
        pool_a_done = Steps(sem("pool_a_done"), "A", pool_a)
        pool_b_done = Steps(sem("pool_b_done"), "B",
                            ["rstd", "qhigh", "khigh", "qmid", "kmid"])
        pool_c_done = Steps(sem("pool_c_done"), "C", ["rstd"])
        order = pe_order()
        pe_done = {s: Steps(sem(f"pe_{s.lower()}_done"), s, [n for st, n, _ in order if st == s])
                   for s in "ABC"}
        reader = {("A", n): (act_a_done, n) for n in ("xt0", "xt1", "xt2", "xT", "qk0", "qk1")}
        reader |= {("A", "tok"): (dve_a_done, "tok"), ("A", "sum"): (dve_a_done, "negmean"),
                   ("A", "sq"): (dve_a_done, "var"), ("A", "v"): (act_a_done, "v1"),
                   ("C", "xT"): (act_c_done, "xT"), ("C", "rt"): (dve_c_done, "sc")}
        reader |= {("B", n): (act_b_done, n) for n in ("xT", "qk0", "qk1", "v")}
        reader |= {("B", "out"): (dve_b_done, "o32")}
        for p in range(PAIRS):
            reader |= {("A", f"st{p}"): (dve_a_done, f"st{p}"), ("A", f"mx{p}"): (dve_a_done, f"mx{p}"),
                       ("A", f"nm{p}"): (dve_a_done, f"nmT{p}"), ("A", f"sc{p}"): (act_a_done, f"p{p}"),
                       ("B", f"st{p}"): (dve_b_done, f"st{p}"), ("B", f"sc{p}"): (act_b_done, f"s{p}")}
        for g in range(GROUPS):
            reader |= {("A", f"z{g}"): (act_a_done, f"z{g}"), ("B", f"z{g}"): (act_b_done, f"z{g}"),
                       ("A", f"zt{g}"): (dve_a_done, f"hm{g}")}
        reader |= {("C", f"e{u}"): (dve_c_done, f"acc{u}1") for u in range(E)}
        x_loaded = sem("x_loaded")
        weights_loaded = sem("weights_loaded")
        consts_made = sem("consts_made")
        quantised = sem("quantised")
        out_stored = sem("out_stored")
        LOADS = 13
        MEMSETS = 26
        QUANTS = 14
        fresh = (consts_made, MEMSETS)
        G, S, R, Z = (Banks(k, tiles, reader, fresh)
                      for k, tiles in (("G", Gt), ("S", St), ("T", Tt), ("Z", Zt)))

        block = ctx.enter_context(nc.Block())

        def in_tiles(ap):
            return ap.rearrange("(t p) d -> p t d", p=T)

        def part(stack, s, n, block_):
            return stack[:, s:s + n, :, block_ * DH:(block_ + 1) * DH].rearrange("p s h e -> p (s h) e")

        def all_heads(qk, s=0, n=2):
            return qk[:, s:s + n, :, :].rearrange("p s t (h e) -> p (s t h) e", h=HEADS)

        def dve_fence(k):
            nc.vector.memset(dve_scrap[:, k:k + 1], 0.0)

        def pool_fence(k):
            nc.gpsimd.tensor_tensor(pool_scrap[:, k:k + 1], not0[:], not0[:], ALU.add)

        @block.sync
        def _(sp):
            for dst, src in ((W_map[:], wmap), (addend[:], in_tiles(pos)), (base_sb[:], in_tiles(base)),
                             (lnw[:], in_tiles(ln_w)), (lnb[:], in_tiles(ln_b)), (Wa[:], w_a),
                             (Wb[:], w_b), (Wp[:], w_p), (bp[:], b_p), (Wr[:], w_r), (We[:], w_e),
                             (clsrow[:], cls), (ident[:], eye)):
                sp.dma_start(dst, src).then_inc(weights_loaded, 16)

            def body(turn):
                if "A" in turn.live:
                    i = turn.image("A")
                    if turn.later("A"):
                        sp.wait_ge(pe_done["A"].sem, pe_done["A"].at(turn, "xt2", back=1))
                    if isinstance(i, int) and i == 0:
                        sp.wait_ge(consts_made, MEMSETS)
                    sp.dma_start(X[2:T, 0, :], x[i, 0:T - 2, :]).then_inc(x_loaded, 16)
                    sp.dma_start(X[0:T, 1, :], x[i, T - 2:2 * T - 2, :]).then_inc(x_loaded, 16)
                if "C" in turn.live:
                    sp.wait_ge(dve_c_done.sem, dve_c_done.at(turn, f"acc{E - 1}1"))
                    sp.dma_start(in_tiles(out[turn.image("C")]), acc[:]).then_inc(out_stored, 16)

            run_turns(sp, images, body)
            sp.wait_ge(out_stored, 16 * images)

        @block.tensor
        def _(pe):
            mm = nc.tensor.matmul

            def flip(dst, src, eye_):
                return nc.tensor.transpose(dst, src, eye_)

            pe.wait_ge(weights_loaded, 16 * LOADS)
            pe.wait_ge(consts_made, MEMSETS)
            pe.wait_ge(quantised, QUANTS)

            def patches_turned(turn, k):
                n = ("A", f"xt{k}")
                if k == 0:
                    pe.wait_ge(x_loaded, (turn.image("A") + 1) * 32)
                pe.wait_ge(*G.vacant(turn, *n))
                bank = G(*n)
                for c in (0, 1):
                    for t in (0, 1):
                        o = c * ROWS + t * T
                        last = flip(bank[:, o:o + T], X[:, t, (2 * k + c) * 128:(2 * k + c + 1) * 128],
                                    ident[0:T, 0:T])
                last.then_inc(pe_done[n[0]].sem, 1)

            def tokens(turn):
                pe.wait_ge(act_a_done.sem, act_a_done.at(turn, "xt2"))
                pe.wait_ge(*G.vacant(turn, "A", "tok"))
                bank = G("A", "tok")
                for t in (0, 1):
                    for c in range(KC):
                        last = mm(bank[0:T, t * D:(t + 1) * D], XT[:, c, t * T:(t + 1) * T], W_map[:, c, :],
                                  start=(c == 0), stop=(c == KC - 1))
                last.then_inc(pe_done["A"].sem, 1)

            def rows_turned(turn, n, src):
                pe.wait_ge(*G.vacant(turn, *n))
                bank = G(*n)
                for c in (0, 1):
                    for t in (0, 1):
                        o = c * ROWS + t * T
                        last = flip(bank[0:HC, o:o + T], src[:, t, c * HC:(c + 1) * HC], ident[0:T, 0:T])
                last.then_inc(pe_done[n[0]].sem, 1)

            def sum_over_partitions(turn):
                pe.wait_ge(dve_a_done.sem, dve_a_done.at(turn, "tok"))
                pe.wait_ge(*G.vacant(turn, "A", "sum"))
                mm(G("A", "sum")[0:T, 0:1], ones[:], rowsum[:], start=True,
                   stop=True).then_inc(pe_done["A"].sem, 1)

            def squares_over_partitions(turn):
                pe.wait_ge(act_a_done.sem, act_a_done.at(turn, "sq1"))
                pe.wait_ge(*G.vacant(turn, "A", "sq"))
                bank = G("A", "sq")
                mm(bank[0:T, 0:1], ones_not0[:], sqs[:, 0:1], start=True, stop=False)
                mm(bank[0:T, 0:1], ones[:], sqs[:, 1:2], start=False, stop=True).then_inc(pe_done["A"].sem, 1)

            def qk_a(turn, t):
                n = ("A", f"qk{t}")
                pe.wait_ge(act_a_done.sem, act_a_done.at(turn, "xT"))
                pe.wait_ge(*G.vacant(turn, *n))
                o = G(*n)[0:T, 0:2 * D].rearrange("p (s d) -> p s d", s=2)
                for c in (0, 1):
                    last = mm(o[:, :, c * HC:(c + 1) * HC], xTA[:, c, t * T:(t + 1) * T], Wa[:, c, 0:2, :],
                              start=True, stop=True)
                last.then_inc(pe_done[n[0]].sem, 1)

            def v_a(turn):
                pe.wait_ge(*G.vacant(turn, "A", "v"))
                bank = G("A", "v")
                for kc in (0, 1):
                    for c in (0, 1):
                        last = mm(bank[0:T, kc * D + c * HC:kc * D + (c + 1) * HC],
                                  xTA[:, c, 1 + kc * (T - 1):1 + kc * (T - 1) + T], Wa[:, c, 2, :],
                                  start=True, stop=True)
                last.then_inc(pe_done["A"].sem, 1)

            def qkv_b(bank, t, cols, at):
                for c in (0, 1):
                    last = mm(bank[0:T, at:at + cols[1] - cols[0]], xTB[:, c, t * T:(t + 1) * T],
                              Wb[:, c, cols[0]:cols[1]], start=(c == 0), stop=(c == 1))
                return last

            def heads_turned(turn, n, stack, p):
                pe.wait_ge(*R.vacant(turn, *n))
                bank = R(*n)
                for s in (0, 1):
                    for h in (0, 1):
                        for t in (0, 1):
                            o = (s * 4 + h * 2 + t) * (T + 1)
                            last = flip(bank[0:SK, o:o + T], stack[:, s, t * HEADS + 2 * p + h, :],
                                        identb[0:T, 0:T])
                last.then_inc(pe_done[n[0]].sem, 1)

            def scores_for_max(turn, p):
                n = ("A", f"mx{p}")
                pe.wait_ge(dve_a_done.sem, dve_a_done.at(turn, f"st{p}"))
                pe.wait_ge(*S.vacant(turn, *n))
                for h in (0, 1):
                    for t in (0, 1):
                        last = mm(S(*n)[0:T, h, t * ROWS:t * ROWS + ROWS - 1],
                                  stA[0:SK, p % 2, 0, h, t * T:(t + 1) * T], stA[0:SK, p % 2, 1, h, 1:ROWS],
                                  start=True, stop=True)
                last.then_inc(pe_done[n[0]].sem, 1)

            def maxima_turned(turn, p):
                n = ("A", f"nm{p}")
                pe.wait_ge(pool_a_done.sem, pool_a_done.at(turn, f"n5_{p}"))
                pe.wait_ge(*R.vacant(turn, *n))
                for h in (0, 1):
                    for t in (0, 1):
                        o = (h * 2 + t) * (T + 1)
                        last = nc.tensor.transpose(R(*n)[SK:SK + 3, o:o + T], nms[:, p % 2, 2 * h + t, :],
                                                   identb[0:T, 0:T])
                last.then_inc(pe_done[n[0]].sem, 1)

            def scores_a(turn, p):
                n = ("A", f"sc{p}")
                pe.wait_ge(dve_a_done.sem, dve_a_done.at(turn, f"nmT{p}"))
                pe.wait_ge(*S.vacant(turn, *n))
                for h in (0, 1):
                    for kc in (0, 1):
                        k0 = 1 + kc * (T - 1)
                        last = mm(S(*n)[0:T, h, kc * ROWS:(kc + 1) * ROWS],
                                  stA[:, p % 2, 1, h, k0:k0 + T], stA[:, p % 2, 0, h, :], start=True, stop=True)
                last.then_inc(pe_done[n[0]].sem, 1)

            def scores_b(turn, p):
                n = ("B", f"sc{p}")
                pe.wait_ge(dve_b_done.sem, dve_b_done.at(turn, f"st{p}"))
                pe.wait_ge(*S.vacant(turn, *n))
                for h in (0, 1):
                    for kc in (0, 1):
                        last = mm(S(*n)[0:T, h, kc * ROWS:(kc + 1) * ROWS],
                                  stB[:, p % 2, 1, h, kc * T:(kc + 1) * T], stB[:, p % 2, 0, h, :],
                                  start=True, stop=True)
                last.then_inc(pe_done[n[0]].sem, 1)

            def times_v(turn, n, g, v, probs):
                pe.wait_ge(*Z.vacant(turn, *n))
                for j in range(4):
                    for kc in (0, 1):
                        last = mm(Z(*n)[32 * j:32 * j + 32, 0:ROWS], v[:, kc, 4 * g + j, :],
                                  probs[:, (2 * g + j // 2) % 4, j % 2, kc, :], start=(kc == 0), stop=(kc == 1))
                last.then_inc(pe_done[n[0]].sem, 1)

            def times_v_a(turn, g):
                pe.wait_ge(act_a_done.sem, act_a_done.at(turn, f"p{2 * g + 1}"))
                times_v(turn, ("A", f"z{g}"), g, vA, PA)

            def times_v_b(turn, g):
                pe.wait_ge(dve_b_done.sem, dve_b_done.at(turn, f"f{2 * g + 1}"))
                if g == 0:
                    pe.wait_ge(dve_b_done.sem, dve_b_done.at(turn, "v"))
                times_v(turn, ("B", f"z{g}"), g, vB, SB)

            def weighted_turned(turn, g):
                n = ("A", f"zt{g}")
                pe.wait_ge(act_a_done.sem, act_a_done.at(turn, f"z{g}"))
                pe.wait_ge(*G.vacant(turn, *n))
                for t in (0, 1):
                    last = flip(G(*n)[0:T, t * 128:(t + 1) * 128], zA[:, g % 2, t * T:(t + 1) * T], ident[:])
                last.then_inc(pe_done[n[0]].sem, 1)

            def project(turn):
                pe.wait_ge(dve_b_done.sem, dve_b_done.at(turn, "z2"))
                pe.wait_ge(*G.vacant(turn, "B", "out"))
                for t in (0, 1):
                    for g in range(GROUPS):
                        last = mm(G("B", "out")[0:T, t * D:(t + 1) * D], zB[:, g, t * T:(t + 1) * T],
                                  Wp[:, g, :], start=(g == 0), stop=(g == GROUPS - 1))
                last.then_inc(pe_done["B"].sem, 1)

            def expert_pair(turn, u):
                n = ("C", f"e{u}")
                t, q = u % 2, u // 2
                pe.wait_ge(*G.vacant(turn, *n))
                for c in (0, 1):
                    last = mm(G(*n)[0:T, 0:2 * D], xTC[:, c, t * T:(t + 1) * T],
                              We[:, c, 2 * q * D:(2 * q + 2) * D], start=(c == 0), stop=(c == 1))
                last.then_inc(pe_done[n[0]].sem, 1)

            def router(turn):
                pe.wait_ge(act_c_done.sem, act_c_done.at(turn, "xT"))
                pe.wait_ge(*G.vacant(turn, "C", "rt"))
                for t in (0, 1):
                    for c in (0, 1):
                        last = mm(G("C", "rt")[0:T, t * E:(t + 1) * E], xTC[:, c, t * T:(t + 1) * T],
                                  Wr[:, c, :], start=(c == 0), stop=(c == 1))
                last.then_inc(pe_done["C"].sem, 1)

            def body(turn):
                a, b, c = ("A" in turn.live), ("B" in turn.live), ("C" in turn.live)
                if a:
                    for k in range(3):
                        patches_turned(turn, k)
                    tokens(turn)
                if b:
                    pe.wait_ge(dve_b_done.sem, dve_b_done.at(turn, "x2"))
                    rows_turned(turn, ("B", "xT"), x2)
                if c:
                    pe.wait_ge(dve_c_done.sem, dve_c_done.at(turn, "x3b"))
                    rows_turned(turn, ("C", "xT"), x3)
                if b:
                    pe.wait_ge(act_b_done.sem, act_b_done.at(turn, "xT"))
                    for t in (0, 1):
                        pe.wait_ge(*G.vacant(turn, "B", f"qk{t}"))
                        qkv_b(G("B", f"qk{t}"), t, (0, 2 * D), 0).then_inc(pe_done["B"].sem, 1)
                if a:
                    sum_over_partitions(turn)
                if b:
                    pe.wait_ge(*G.vacant(turn, "B", "v"))
                    qkv_b(G("B", "v"), 0, (2 * D, 3 * D), 0)
                    qkv_b(G("B", "v"), 1, (2 * D, 3 * D), D).then_inc(pe_done["B"].sem, 1)
                if a:
                    squares_over_partitions(turn)
                if c:
                    router(turn)
                    expert_pair(turn, 0)
                if a:
                    pe.wait_ge(pool_a_done.sem, pool_a_done.at(turn, "x"))
                    rows_turned(turn, ("A", "xT"), xn)
                if c:
                    expert_pair(turn, 1)
                if a:
                    qk_a(turn, 0)
                    qk_a(turn, 1)
                    v_a(turn)
                if b:
                    pe.wait_ge(pool_b_done.sem, pool_b_done.at(turn, "kmid"))
                    pe.wait_ge(dve_b_done.sem, dve_b_done.at(turn, "mid"))
                    heads_turned(turn, ("B", "st0"), stackB, 0)
                    scores_b(turn, 0)
                if c:
                    expert_pair(turn, 2)
                if a:
                    pe.wait_ge(pool_a_done.sem, pool_a_done.at(turn, "kmid"))
                    pe.wait_ge(dve_a_done.sem, dve_a_done.at(turn, "lowk"))
                    heads_turned(turn, ("A", "st0"), stackA, 0)
                    scores_for_max(turn, 0)
                for p in range(PAIRS):
                    if b and p + 1 < PAIRS:
                        heads_turned(turn, ("B", f"st{p + 1}"), stackB, p + 1)
                    if c and 1 <= p < 5:
                        expert_pair(turn, p + 2)
                    if a:
                        maxima_turned(turn, p)
                        if p + 1 < PAIRS:
                            heads_turned(turn, ("A", f"st{p + 1}"), stackA, p + 1)
                    if b and p + 1 < PAIRS:
                        scores_b(turn, p + 1)
                    if b and p in (2, 4):
                        times_v_b(turn, (p - 2) // 2)
                    if a and p + 1 < PAIRS:
                        scores_for_max(turn, p + 1)
                    if a:
                        scores_a(turn, p)
                    if a and p in (3, 5):
                        times_v_a(turn, (p - 3) // 2)
                    if a and p == 4:
                        weighted_turned(turn, 0)
                if c:
                    expert_pair(turn, 7)
                if b:
                    times_v_b(turn, 2)
                if a:
                    weighted_turned(turn, 1)
                if b:
                    project(turn)
                if a:
                    times_v_a(turn, 2)
                    weighted_turned(turn, 2)

            run_turns(pe, images, body)

        @block.scalar
        def _(act):
            def copy(dst, src, scale=1.0):
                return nc.scalar.activation(dst, src, ACT.Copy, scale=scale)

            act.wait_ge(weights_loaded, 16 * LOADS)
            act.wait_ge(consts_made, MEMSETS)

            def turned_rows(turn, stage, dst, steps):
                act.wait_ge(pe_done[stage].sem, pe_done[stage].at(turn, "xT"))
                copy(dst[0:HC, :, :], G(stage, "xT")[0:HC, 0:2 * ROWS].rearrange("p (c r) -> p c r", c=2))\
                    .then_inc(steps.sem, 1)

            def rounded_scores(turn, p):
                act.wait_ge(pe_done["B"].sem, pe_done["B"].at(turn, f"sc{p}"))
                if p >= 2:
                    act.wait_ge(dve_b_done.sem, dve_b_done.at(turn, f"f{p - 2}"))
                copy(S16[:, p % 2, :].rearrange("p (h r) -> p h r", h=2), S("B", f"sc{p}")[0:T, :, 0:2 * ROWS],
                     scale=2.0 ** -8).then_inc(act_b_done.sem, 1)

            def weighted_b(turn, g):
                act.wait_ge(pe_done["B"].sem, pe_done["B"].at(turn, f"z{g}"))
                if g == 2:
                    act.wait_ge(dve_b_done.sem, dve_b_done.at(turn, "z0"))
                copy(z16[:, g % 2, :], Z("B", f"z{g}")[:, 0:ROWS], scale=2.0 ** -8).then_inc(act_b_done.sem, 1)

            def weighted_a(turn, g):
                act.wait_ge(pe_done["A"].sem, pe_done["A"].at(turn, f"z{g}"))
                copy(zA[:, g % 2, :], Z("A", f"z{g}")[:, 0:ROWS]).then_inc(act_a_done.sem, 1)

            def body(turn):
                a, b, c = ("A" in turn.live), ("B" in turn.live), ("C" in turn.live)
                if a:
                    for k in range(3):
                        act.wait_ge(pe_done["A"].sem, pe_done["A"].at(turn, f"xt{k}"))
                        copy(XT[:, 2 * k:2 * k + 2, :],
                             G("A", f"xt{k}")[:, 0:2 * ROWS].rearrange("p (c r) -> p c r", c=2))\
                            .then_inc(act_a_done.sem, 1)
                if b:
                    turned_rows(turn, "B", xTB, act_b_done)
                if c:
                    turned_rows(turn, "C", xTC, act_c_done)
                if b:
                    for t in (0, 1):
                        act.wait_ge(pe_done["B"].sem, pe_done["B"].at(turn, f"qk{t}"))
                        if t == 0:
                            if turn.later("B"):
                                act.wait_ge(dve_b_done.sem, dve_b_done.at(turn, "mid", back=1))
                        copy(qkB[:, :, t, :], G("B", f"qk{t}")[0:T, 0:2 * D].rearrange("p (s d) -> p s d", s=2),
                             scale=2.0 ** -16).then_inc(act_b_done.sem, 1)
                if a:
                    act.wait_ge(dve_a_done.sem, dve_a_done.at(turn, "negmean"))
                    for t in (0, 1):
                        nc.scalar.activation(sqtmp[:, t, :], tok[:, t, :], ACT.Square, bias=negmean[:],
                                             accum_out=sqs[:, t:t + 1]).then_inc(act_a_done.sem, 1)
                if b:
                    act.wait_ge(pe_done["B"].sem, pe_done["B"].at(turn, "v"))
                    if turn.later("B"):
                        act.wait_ge(dve_b_done.sem, dve_b_done.at(turn, "v", back=1))
                    copy(v16[:], G("B", "v")[0:T, 0:2 * D].rearrange("p (t d) -> p t d", t=2),
                         scale=2.0 ** -16).then_inc(act_b_done.sem, 1)
                if c:
                    act.wait_ge(dve_c_done.sem, dve_c_done.at(turn, "sc"))
                    nc.scalar.activation(pr[:], sc[:], ACT.Exp).then_inc(act_c_done.sem, 1)
                if a:
                    turned_rows(turn, "A", xTA, act_a_done)
                    for t in (0, 1):
                        act.wait_ge(pe_done["A"].sem, pe_done["A"].at(turn, f"qk{t}"))
                        copy(qkA[:, :, t, :], G("A", f"qk{t}")[0:T, 0:2 * D].rearrange("p (s d) -> p s d", s=2))\
                            .then_inc(act_a_done.sem, 1)
                    act.wait_ge(pe_done["A"].sem, pe_done["A"].at(turn, "v"))
                    if turn.later("A"):
                        act.wait_ge(pe_done["A"].sem, pe_done["A"].at(turn, "z2", back=1))
                    for kc in (0, 1):
                        copy(vA[:, kc, :, 0:DH],
                             G("A", "v")[0:T, kc * D:(kc + 1) * D].rearrange("p (h e) -> p h e", h=HEADS),
                             scale=(not0[:] if kc else 1.0)).then_inc(act_a_done.sem, 1)
                    act.wait_ge(act_a_done.sem, act_a_done.at(turn, "qk1"))
                    if turn.later("A"):
                        act.wait_ge(pe_done["A"].sem, pe_done["A"].at(turn, "st5", back=1))
                    copy(part(stackA, 0, 2, 2), all_heads(qkA)).then_inc(act_a_done.sem, 1)
                if b:
                    rounded_scores(turn, 0)
                for p in range(PAIRS):
                    if b and p + 1 < PAIRS:
                        rounded_scores(turn, p + 1)
                    if a:
                        act.wait_ge(pe_done["A"].sem, pe_done["A"].at(turn, f"sc{p}"))
                        nc.scalar.activation(PA[:, p % 4, :, :, :].rearrange("p h c r -> p h (c r)"),
                                             S("A", f"sc{p}")[0:T, :, 0:2 * ROWS], ACT.Exp,
                                             scale=DH ** -0.5).then_inc(act_a_done.sem, 1)
                    if b and p in (2, 4):
                        weighted_b(turn, p // 2 - 1)
                    if a and p in (3, 5):
                        weighted_a(turn, (p - 3) // 2)
                if b:
                    weighted_b(turn, 2)
                if a:
                    weighted_a(turn, 2)

            run_turns(act, images, body)

        @block.vector
        def _(dve):
            v = nc.vector
            dve.wait_ge(weights_loaded, 16 * LOADS)
            v.tensor_tensor(addend[:], addend[:], base_sb[:], ALU.add).then_inc(quantised, 1)
            done = 1
            for w, bias_scale in ((Wb[0:HC, :, :], 1.0), (Wb[HC:HC + 1, :, :], 2.0 ** 16), (Wp[:], 1.0),
                                  (bp[:], 1.0)):
                v.tensor_scalar(w, w, 256.0, I16MAX, ALU.mult, ALU.min).then_inc(quantised, 1)
                done += 1
                dve.wait_ge(quantised, done)
                v.tensor_scalar(w, w, I16MIN, ROUND, ALU.max, ALU.add).then_inc(quantised, 1)
                done += 1
                dve.wait_ge(quantised, done)
                v.tensor_scalar(w, w, ROUND, bias_scale, ALU.subtract, ALU.mult).then_inc(quantised, 1)
                done += 1
            v.memset(acc[:], 0.0).then_inc(quantised, 1)
            dve.wait_ge(quantised, QUANTS)
            dve.wait_ge(consts_made, MEMSETS)

            def norm_stats(turn, rows, bn, mv, var, steps):
                for t in (0, 1):
                    v.bn_stats(bn[:, t, :], rows[:, t, :]).then_inc(steps.sem, 1)
                dve.wait_ge(steps.sem, steps.at(turn, "bn1"))
                dve_fence(0 if steps is dve_b_done else 1)
                for t in (0, 1):
                    v.bn_aggr(mv[:, t, :], bn[:, t, :]).then_inc(steps.sem, 1)
                dve.wait_ge(steps.sem, steps.at(turn, "mv1"))
                v.tensor_scalar(var[:], mv[:, :, 1], EPS, None, ALU.add).then_inc(steps.sem, 1)

            def turned(bank, n):
                return bank[:, 0:n * (T + 1)].rearrange("p (n r) -> p n r", n=n)[:, :, 0:T]

            def operand_copied(turn, stage, p, dst, steps):
                dve.wait_ge(pe_done[stage].sem, pe_done[stage].at(turn, f"st{p}"))
                v.tensor_copy(dst[0:SK, p % 2, :, :, :].rearrange("p s h (t r) -> p (s h t) r", t=2),
                              turned(R(stage, f"st{p}")[0:SK], 8)).then_inc(steps.sem, 1)

            def float_scores(turn, p):
                dve.wait_ge(act_b_done.sem, act_b_done.at(turn, f"s{p}"))
                if p < 2:
                    if turn.later("B"):
                        dve.wait_ge(pe_done["B"].sem, pe_done["B"].at(turn, "z2", back=1))
                elif p >= 4:
                    dve.wait_ge(pe_done["B"].sem, pe_done["B"].at(turn, "z0"))
                v.tensor_copy(SB[:, p % 4, :, :, :].rearrange("p h c r -> p (h c r)"), S16[:, p % 2, :])\
                    .then_inc(dve_b_done.sem, 1)

            def float_weighted(turn, g):
                dve.wait_ge(act_b_done.sem, act_b_done.at(turn, f"z{g}"))
                v.tensor_copy(zB[:, g, :], z16[:, g % 2, :]).then_inc(dve_b_done.sem, 1)

            def row_maxima(turn, p):
                dve.wait_ge(pe_done["A"].sem, pe_done["A"].at(turn, f"mx{p}"))
                if p >= 2:
                    dve.wait_ge(pool_a_done.sem, pool_a_done.at(turn, f"n5_{p - 2}"))
                v.tensor_reduce(nm[:, p % 2, :].rearrange("p (h t) -> p h t", h=2),
                                S("A", f"mx{p}")[0:T, :, 0:2 * ROWS].rearrange("p h (t r) -> p h t r", t=2)
                                [:, :, :, 0:ROWS - 1], AX.X, ALU.max, negate=True).then_inc(dve_a_done.sem, 1)

            def softmax_rows(turn, g):
                dve.wait_ge(pe_done["A"].sem, pe_done["A"].at(turn, f"zt{g}"))
                w = G("A", f"zt{g}")[0:T, 0:256].rearrange("p (t j e) -> p t j e", t=2, j=4)
                v.reciprocal(rden[:], w[:, :, :, DH]).then_inc(dve_a_done.sem, 1)
                dve.wait_ge(dve_a_done.sem, dve_a_done.at(turn, f"rden{g}"))
                v.tensor_tensor(hm[:, :, g * 64:(g + 1) * 64].rearrange("p t (j e) -> p t j e", j=4),
                                w[:, :, :, 0:DH], rden[:].unsqueeze(3).to_broadcast([T, 2, 4, DH]), ALU.mult)\
                    .then_inc(dve_a_done.sem, 1)

            def experts_added(turn, u):
                dve.wait_ge(pe_done["C"].sem, pe_done["C"].at(turn, f"e{u}"))
                t, q = u % 2, u // 2
                for e in (0, 1):
                    if q or e:
                        dve.wait_ge(dve_c_done.sem, dve_c_done.at(turn, f"acc{u}0" if e else f"acc{u - 2}1"))
                    before = acc if q or e else H2
                    v.scalar_tensor_tensor(acc[:, t, :], G("C", f"e{u}")[0:T, e * D:(e + 1) * D],
                                           gate[:, t, 2 * q + e:2 * q + e + 1], before[:, t, :],
                                           ALU.mult, ALU.add).then_inc(dve_c_done.sem, 1)

            def per_expert(ap):
                return ap[:].unsqueeze(2).to_broadcast([T, 2, E])

            def route(turn):
                def tt(out_, a_, b_, op):
                    v.tensor_tensor(out_[:], a_, b_, op).then_inc(dve_c_done.sem, 1)

                def largest(out_, in_, op=ALU.max, **kw):
                    v.tensor_reduce(out_[:], in_, AX.X, op, **kw).then_inc(dve_c_done.sem, 1)

                logits = G("C", "rt")[0:T, 0:2 * E].rearrange("p (t e) -> p t e", t=2)
                dve.wait_ge(pe_done["C"].sem, pe_done["C"].at(turn, "rt"))
                largest(top, logits, negate=True)
                dve.wait_ge(dve_c_done.sem, dve_c_done.at(turn, "top"))
                tt(sc, logits, per_expert(top), ALU.add)
                dve.wait_ge(act_c_done.sem, act_c_done.at(turn, "exp"))
                largest(r1, pr[:], ALU.add)
                dve.wait_ge(dve_c_done.sem, dve_c_done.at(turn, "sum"))
                v.reciprocal(r2[:], r1[:]).then_inc(dve_c_done.sem, 1)
                dve.wait_ge(dve_c_done.sem, dve_c_done.at(turn, "rsum"))
                tt(pr, pr[:], per_expert(r2), ALU.mult)
                dve.wait_ge(dve_c_done.sem, dve_c_done.at(turn, "pr"))
                largest(p1, pr[:])
                dve.wait_ge(dve_c_done.sem, dve_c_done.at(turn, "p1"))
                tt(eq, pr[:], per_expert(p1), ALU.is_equal)
                dve.wait_ge(dve_c_done.sem, dve_c_done.at(turn, "eq1"))
                tt(eq, eq[:], rank[:], ALU.mult)
                dve.wait_ge(dve_c_done.sem, dve_c_done.at(turn, "key1"))
                largest(r1, eq[:])
                dve.wait_ge(dve_c_done.sem, dve_c_done.at(turn, "r1"))
                tt(sel1, eq[:], per_expert(r1), ALU.is_equal)
                dve.wait_ge(dve_c_done.sem, dve_c_done.at(turn, "sel1"))
                v.scalar_tensor_tensor(rest[:], sel1[:], -2.0, pr[:], ALU.mult, ALU.add)\
                    .then_inc(dve_c_done.sem, 1)
                dve.wait_ge(dve_c_done.sem, dve_c_done.at(turn, "rest"))
                largest(p2, rest[:])
                dve.wait_ge(dve_c_done.sem, dve_c_done.at(turn, "p2"))
                tt(eq, rest[:], per_expert(p2), ALU.is_equal)
                dve.wait_ge(dve_c_done.sem, dve_c_done.at(turn, "eq2"))
                tt(eq, eq[:], rank[:], ALU.mult)
                dve.wait_ge(dve_c_done.sem, dve_c_done.at(turn, "key2"))
                largest(r1, eq[:])
                dve.wait_ge(dve_c_done.sem, dve_c_done.at(turn, "r2"))
                tt(eq, eq[:], per_expert(r1), ALU.is_equal)
                dve.wait_ge(dve_c_done.sem, dve_c_done.at(turn, "sel2"))
                tt(sel1, sel1[:], eq[:], ALU.add)
                dve.wait_ge(dve_c_done.sem, dve_c_done.at(turn, "sel"))
                tt(sel1, sel1[:], pr[:], ALU.mult)
                tt(r2, p1[:], p2[:], ALU.add)
                dve.wait_ge(dve_c_done.sem, dve_c_done.at(turn, "den"))
                v.tensor_scalar(r2[:], r2[:], 1e-9, None, ALU.add).then_inc(dve_c_done.sem, 1)
                dve.wait_ge(dve_c_done.sem, dve_c_done.at(turn, "den2"))
                v.reciprocal(r2[:], r2[:]).then_inc(dve_c_done.sem, 1)
                dve.wait_ge(dve_c_done.sem, dve_c_done.at(turn, "rden"))
                tt(gate, sel1[:], per_expert(r2), ALU.mult)
                dve.wait_ge(dve_c_done.sem, dve_c_done.at(turn, "gate"))

            def body(turn):
                a, b, c = ("A" in turn.live), ("B" in turn.live), ("C" in turn.live)
                if b:
                    dve.wait_ge(pool_a_done.sem, pool_a_done.at(turn.previous(), "H"))
                    dve.wait_ge(dve_a_done.sem, dve_a_done.at(turn.previous(), "H"))
                    norm_stats(turn, H, bnB, mvB, varB, dve_b_done)
                if c:
                    dve.wait_ge(dve_b_done.sem, dve_b_done.at(turn.previous(), "H2"))
                    norm_stats(turn, H2, bnC, mvC, varC, dve_c_done)
                if b:
                    dve.wait_ge(pool_b_done.sem, pool_b_done.at(turn, "rstd"))
                    v.tensor_scalar(scaleB[:], rstdB[:], 2.0 ** 16, None, ALU.mult).then_inc(dve_b_done.sem, 1)
                    dve.wait_ge(dve_b_done.sem, dve_b_done.at(turn, "scale"))
                    for t in (0, 1):
                        v.tensor_scalar(x2[:, t, :], H[:, t, :], mvB[:, t, 0:1], scaleB[:, t:t + 1],
                                        ALU.subtract, ALU.mult).then_inc(dve_b_done.sem, 1)
                    dve.wait_ge(dve_b_done.sem, dve_b_done.at(turn, "x2b"))
                    v.tensor_scalar(x2[:], x2[:], ROUND, ROUND, ALU.add, ALU.subtract)\
                        .then_inc(dve_b_done.sem, 1)
                if c:
                    dve.wait_ge(pool_c_done.sem, pool_c_done.at(turn, "rstd"))
                    for t in (0, 1):
                        v.tensor_scalar(x3[:, t, :], H2[:, t, :], mvC[:, t, 0:1], rstdC[:, t:t + 1],
                                        ALU.subtract, ALU.mult).then_inc(dve_c_done.sem, 1)
                if a:
                    dve.wait_ge(pe_done["A"].sem, pe_done["A"].at(turn, "tok"))
                    v.scalar_tensor_tensor(tok[:].rearrange("p t d -> p (t d)"), G("A", "tok")[0:T, 0:2 * D], 0.0,
                                           addend[:].rearrange("p t d -> p (t d)"), ALU.add, ALU.add,
                                           accum_out=rowsum[:]).then_inc(dve_a_done.sem, 1)
                    dve.wait_ge(pe_done["A"].sem, pe_done["A"].at(turn, "sum"))
                    v.tensor_scalar(negmean[:], G("A", "sum")[0:T, 0:1], -1.0 / NTOK, None, ALU.mult)\
                        .then_inc(dve_a_done.sem, 1)
                    dve.wait_ge(pe_done["A"].sem, pe_done["A"].at(turn, "sq"))
                    v.tensor_scalar(varA[:], G("A", "sq")[0:T, 0:1], 1.0 / NTOK, EPS, ALU.mult, ALU.add)\
                        .then_inc(dve_a_done.sem, 1)
                if c:
                    route(turn)
                if a:
                    dve.wait_ge(pool_a_done.sem, pool_a_done.at(turn, "rstd"))
                    v.tensor_scalar(xn[:], tok[:], negmean[:], rstdA[:], ALU.add, ALU.mult)\
                        .then_inc(dve_a_done.sem, 1)
                if c:
                    out_count = 16 * turn.image("C")
                    if not isinstance(out_count, int) or out_count > 0:
                        dve.wait_ge(out_stored, out_count)
                    experts_added(turn, 0)
                    experts_added(turn, 1)
                if b:
                    dve.wait_ge(act_b_done.sem, act_b_done.at(turn, "qk1"))
                    if turn.later("B"):
                        dve.wait_ge(pe_done["B"].sem, pe_done["B"].at(turn, "st5", back=1))
                    v.tensor_copy(part(stackB, 0, 2, 2), all_heads(qkB)).then_inc(dve_b_done.sem, 1)
                    dve.wait_ge(dve_b_done.sem, dve_b_done.at(turn, "high"))
                    v.tensor_tensor(part(stackB, 0, 2, 5), all_heads(qkB), part(stackB, 0, 2, 2), ALU.subtract)\
                        .then_inc(dve_b_done.sem, 1)
                    dve.wait_ge(act_b_done.sem, act_b_done.at(turn, "v"))
                    if turn.later("B"):
                        dve.wait_ge(pe_done["B"].sem, pe_done["B"].at(turn, "z2", back=1))
                    v.tensor_copy(vB[:, :, :, 0:DH], v16[:].rearrange("p t (h e) -> p t h e", h=HEADS))\
                        .then_inc(dve_b_done.sem, 1)
                if a:
                    dve.wait_ge(act_a_done.sem, act_a_done.at(turn, "high"))
                    v.tensor_tensor(all_heads(resid), all_heads(qkA), part(stackA, 0, 2, 2), ALU.subtract)\
                        .then_inc(dve_a_done.sem, 1)
                    dve.wait_ge(dve_a_done.sem, dve_a_done.at(turn, "resid"))
                    v.tensor_copy(part(stackA, 0, 2, 5), all_heads(resid)).then_inc(dve_a_done.sem, 1)
                    dve.wait_ge(dve_a_done.sem, dve_a_done.at(turn, "mid"))
                    for s, low in ((0, 4), (1, 0)):
                        v.tensor_tensor(part(stackA, s, 1, low), all_heads(resid, s, 1),
                                        part(stackA, s, 1, 5), ALU.subtract).then_inc(dve_a_done.sem, 1)
                if b:
                    operand_copied(turn, "B", 0, stB, dve_b_done)
                if c:
                    experts_added(turn, 2)
                if a:
                    operand_copied(turn, "A", 0, stA, dve_a_done)
                    row_maxima(turn, 0)
                if b:
                    float_scores(turn, 0)
                for p in range(PAIRS):
                    if b and p + 1 < PAIRS:
                        operand_copied(turn, "B", p + 1, stB, dve_b_done)
                    if c and 1 <= p < 5:
                        experts_added(turn, p + 2)
                    if a:
                        dve.wait_ge(pe_done["A"].sem, pe_done["A"].at(turn, f"nm{p}"))
                        v.tensor_copy(stA[SK:SK + 3, p % 2, 0, :, :].rearrange("p h (t r) -> p (h t) r", t=2),
                                      turned(R("A", f"nm{p}")[SK:SK + 3], 4)).then_inc(dve_a_done.sem, 1)
                        if p + 1 < PAIRS:
                            operand_copied(turn, "A", p + 1, stA, dve_a_done)
                            row_maxima(turn, p + 1)
                    if b and p + 1 < PAIRS:
                        float_scores(turn, p + 1)
                    if b and p in (3, 5):
                        float_weighted(turn, (p - 3) // 2)
                    if a and p == 4:
                        softmax_rows(turn, 0)
                if c:
                    experts_added(turn, 7)
                if b:
                    float_weighted(turn, 2)
                if a:
                    softmax_rows(turn, 1)
                if b:
                    dve.wait_ge(pe_done["B"].sem, pe_done["B"].at(turn, "out"))
                    v.scalar_tensor_tensor(o32[:], G("B", "out")[0:T, 0:2 * D].rearrange("p (t d) -> p t d", t=2),
                                           2.0 ** -8, bp[:].unsqueeze(1).to_broadcast([T, 2, D]),
                                           ALU.mult, ALU.add).then_inc(dve_b_done.sem, 1)
                    dve.wait_ge(dve_b_done.sem, dve_b_done.at(turn, "o32"))
                    v.scalar_tensor_tensor(H2[:], o32[:], 2.0 ** -8, H[:], ALU.mult, ALU.add)\
                        .then_inc(dve_b_done.sem, 1)
                if a:
                    softmax_rows(turn, 2)
                    dve.wait_ge(pool_a_done.sem, pool_a_done.at(turn, "H"))
                    v.tensor_copy(H[0:1, 0, :], clsrow[:]).then_inc(dve_a_done.sem, 1)

            run_turns(dve, images, body)

        @block.gpsimd
        def _(pool):
            q = nc.gpsimd
            made = 0
            for ap, value in ((X[0:2, 0, :], 0.0), (xTA[HC:HC + 1], 1.0), (xTB[HC:HC + 1], 1.0),
                              (xTC[HC:HC + 1], 1.0), (ones[:], 1.0), (ones_not0[:], 1.0), (not0[:], 1.0),
                              (halfneg[:], -0.5), (zero4[:], 0.0), (vA[:, :, :, DH:32], 0.0), (vB[:], 0.0),
                              (stackB[:], 0.0), (stA[SK:SK + 3, :, 1, :, :], 1.0),
                              (ones_not0[0:1, :], 0.0), (not0[0:1, :], 0.0),
                              (vA[:, :, :, DH:DH + 1], 1.0), (vA[0:1, 1, :, DH:DH + 1], 0.0),
                              *((rank[:, :, e:e + 1], float(E - e)) for e in range(E))):
                q.memset(ap, value).then_inc(consts_made, 1)
                made += 1
                pool.wait_ge(consts_made, made)
            pool.wait_ge(weights_loaded, 16 * LOADS)
            q.tensor_copy(identb[:], ident[:]).then_inc(consts_made, 1)
            pool.wait_ge(consts_made, MEMSETS)

            def copies(turn, stack, steps, slots):
                pool_fence(0 if steps is pool_b_done else 1)
                for s, src, dst, n in slots:
                    q.tensor_copy(stack[:, s, :, dst * DH:(dst + n) * DH].rearrange("p h (n e) -> p h n e", n=n),
                                  stack[:, s, :, src * DH:(src + 1) * DH].unsqueeze(2)
                                  .to_broadcast([T, 2 * HEADS, n, DH])).then_inc(steps.sem, 1)

            def body(turn):
                a, b, c = ("A" in turn.live), ("B" in turn.live), ("C" in turn.live)
                if b:
                    pool.wait_ge(dve_b_done.sem, dve_b_done.at(turn, "var"))
                    q.tensor_tensor(rstdB[:], varB[:], halfneg[:], ALU.pow).then_inc(pool_b_done.sem, 1)
                if c:
                    pool.wait_ge(dve_c_done.sem, dve_c_done.at(turn, "var"))
                    q.tensor_tensor(rstdC[:], varC[:], halfneg[:], ALU.pow).then_inc(pool_c_done.sem, 1)
                if a:
                    pool.wait_ge(dve_a_done.sem, dve_a_done.at(turn, "var"))
                    q.tensor_tensor(rstdA[:], varA[:], halfneg[:, 0:1], ALU.pow).then_inc(pool_a_done.sem, 1)
                if a:
                    pool.wait_ge(dve_a_done.sem, dve_a_done.at(turn, "xn"))
                    q.tensor_tensor(xn[:], xn[:], lnw[:], ALU.mult).then_inc(pool_a_done.sem, 1)
                    pool.wait_ge(pool_a_done.sem, pool_a_done.at(turn, "xw"))
                    q.tensor_tensor(xn[:], xn[:], lnb[:], ALU.add).then_inc(pool_a_done.sem, 1)
                if b:
                    pool.wait_ge(dve_b_done.sem, dve_b_done.at(turn, "mid"))
                    copies(turn, stackB, pool_b_done, ((0, 2, 1, 1), (1, 2, 3, 1), (0, 5, 3, 1), (1, 5, 1, 1)))
                if a:
                    pool.wait_ge(dve_a_done.sem, dve_a_done.at(turn, "mid"))
                    copies(turn, stackA, pool_a_done, ((0, 2, 0, 2), (1, 2, 3, 2), (0, 5, 3, 1), (1, 5, 1, 1)))
                for p in range(PAIRS):
                    if a:
                        high, mid, low = (nms[:, p % 2, :, i] for i in range(3))
                        pool.wait_ge(dve_a_done.sem, dve_a_done.at(turn, f"mx{p}"))
                        q.tensor_tensor(high, nm[:, p % 2, :], zero4[:], ALU.add).then_inc(pool_a_done.sem, 1)
                        pool.wait_ge(pool_a_done.sem, pool_a_done.at(turn, f"n1_{p}"))
                        q.tensor_tensor(nmr[:, p % 2, :], nm[:, p % 2, :], high, ALU.subtract)\
                            .then_inc(pool_a_done.sem, 1)
                        pool.wait_ge(pool_a_done.sem, pool_a_done.at(turn, f"n2_{p}"))
                        q.tensor_tensor(mid, nmr[:, p % 2, :], zero4[:], ALU.add).then_inc(pool_a_done.sem, 1)
                        pool.wait_ge(pool_a_done.sem, pool_a_done.at(turn, f"n3_{p}"))
                        q.tensor_tensor(nmr[:, p % 2, :], nmr[:, p % 2, :], mid, ALU.subtract)\
                            .then_inc(pool_a_done.sem, 1)
                        pool.wait_ge(pool_a_done.sem, pool_a_done.at(turn, f"n4_{p}"))
                        q.tensor_tensor(low, nmr[:, p % 2, :], zero4[:], ALU.add).then_inc(pool_a_done.sem, 1)
                if a:
                    pool.wait_ge(dve_a_done.sem, dve_a_done.at(turn, "hm2"))
                    pool.wait_ge(dve_b_done.sem, dve_b_done.at(turn, "H2"))
                    q.tensor_tensor(H[:], hm[:], tok[:], ALU.add).then_inc(pool_a_done.sem, 1)

            run_turns(pool, images, body)


def positions():
    seq = ROWS - 1
    i = np.arange(seq, dtype=np.float32)[:, None]
    j = np.arange(D, dtype=np.float32)[None, :]
    even = (np.arange(D) % 2 == 0)[None, :]
    base = np.float32(10000.0)
    one = np.float32(1.0)
    angle = i / np.where(even, base ** (j / np.float32(D)), base ** ((j - one) / np.float32(D)))
    table = np.zeros((ROWS, D), np.float32)
    table[1:] = np.where(even, np.sin(angle), np.cos(angle))
    return table


def kernel(**inputs):
    import concourse.bacc as bacc
    from concourse.bass_utils import run_bass_kernel_spmd as run

    def get(name):
        return np.asarray(inputs[name])

    x = np.ascontiguousarray(get("x"))
    images = x.shape[0]
    arrays = {"x": x.reshape(images, 196, KD), "pos": positions()}
    base = np.zeros((ROWS, D), np.float32)
    base[1] = get("L0_tok_class_token")[0]
    base[2:] = get("L0_tok_b_map")
    arrays["base"] = base
    for name, key in (("ln_w", "L0_tok_ln_w"), ("ln_b", "L0_tok_ln_b")):
        arrays[name] = np.zeros((ROWS, D), np.float32)
        arrays[name][1:] = get(key)
    arrays["wmap"] = get("L0_tok_W_map").T.reshape(KC, 128, D).transpose(1, 0, 2)
    w_a = np.zeros((HC + 1, 2, 3, HC), np.float32)
    for s, (w, bias) in enumerate((("L0_tok_Wq", "L0_tok_bq"), ("L0_tok_Wk", "L0_tok_bk"),
                                   ("L0_tok_Wv", "L0_tok_bv"))):
        for h in range(HEADS):
            c, o = h // 6, (h % 6) * DH
            w_a[o:o + DH, c, s, o:o + DH] = get(w)[h].T
            w_a[HC, c, s, o:o + DH] = get(bias)[h]
    arrays["w_a"] = w_a
    w = get("L0_attn_wqkv").reshape(HEADS, 3, DH, D).transpose(3, 1, 0, 2).reshape(D, 3 * D)
    w_b = np.zeros((HC + 1, 2, 3 * D), np.float32)
    w_b[0:HC] = w.reshape(2, HC, 3 * D).transpose(1, 0, 2)
    w_b[HC, 0] = get("L0_attn_bqkv").reshape(HEADS, 3, DH).transpose(1, 0, 2).reshape(3 * D)
    arrays["w_b"] = w_b
    w_p = np.zeros((4, 32, GROUPS, D), np.float32)
    w_p[:, 0:DH] = get("L0_attn_wp").T.reshape(GROUPS, 4, DH, D).transpose(1, 2, 0, 3)
    arrays["w_p"] = w_p.reshape(128, GROUPS, D)
    arrays["b_p"] = np.broadcast_to(get("L0_attn_bp"), (T, D))
    w_r = np.zeros((HC + 1, 2, E), np.float32)
    w_r[0:HC] = get("L0_ffn_router_w").T.reshape(2, HC, E).transpose(1, 0, 2)
    w_r[HC, 0] = get("L0_ffn_router_b")
    arrays["w_r"] = w_r
    w_e = np.zeros((HC + 1, 2, E * D), np.float32)
    w_e[0:HC] = get("L0_ffn_expert_w").transpose(2, 0, 1).reshape(2, HC, E * D).transpose(1, 0, 2)
    w_e[HC, 0] = get("L0_ffn_expert_b").reshape(E * D)
    arrays["w_e"] = w_e
    arrays["cls"] = get("cls_tok").reshape(1, D)
    arrays["eye"] = np.eye(128, dtype=np.float32)
    arrays = {f"{n}_dram": np.ascontiguousarray(a) for n, a in arrays.items()}

    nc = bacc.Bacc("TRN2", target_bir_lowering=False, num_devices=1)
    args = [nc.dram_tensor(n, a.shape, mybir.dt.from_np(a.dtype), kind="ExternalInput").ap()
            for n, a in arrays.items()]
    out = nc.dram_tensor("out_dram", (images, ROWS, D), F32, kind="ExternalOutput").ap()
    tower(nc, *args, out)
    r = run(nc, [arrays], core_ids=[0])
    return r.results[0]["out_dram"]
```

```python
from contextlib import ExitStack

import numpy as np

import concourse.bass as bass
from concourse import mybir

F32 = mybir.dt.float32
BF16 = mybir.dt.bfloat16
I16 = mybir.dt.int16
I32 = mybir.dt.int32
ALU = mybir.AluOpType
ACT = mybir.ActivationFunctionType
AX = mybir.AxisListType

W = 192
HEADS = 12
DH = W // HEADS
ROWS = 198
T = ROWS // 2
TP = T + 1
KD = 768
KC = KD // 128
HC = W // 2
SK = 6 * DH
PAIRS = HEADS // 2
GROUPS = HEADS // 4
NE = 8
EPS = 1e-5
ROUND = 1.5 * 2.0 ** 23
I16MAX, I16MIN = 32767.0, -32768.0
NTOK = (ROWS - 1) * W
STAGES = ("load", "embed", "soft", "qkv", "fixed", "route", "experts")
LAG = {s: i for i, s in enumerate(STAGES)}


def pe_order():
    g = lambda *uses: [(u.split(".")[0], u.split(".")[1], "G") for u in uses]
    order = [("fixed", "st0", "T"), *g("experts.e0"), ("soft", "st0", "T"), ("soft", "st1", "T"),
             ("soft", "mx0", "S"), *g("experts.e1", "embed.tok")]
    first = [[], [], g("qkv.qk1"), g("embed.xT"), g("embed.qk0"), []]
    second = [g("qkv.xT", "experts.e2", "embed.sum"), g("qkv.qk0", "experts.e3", "embed.sq"),
              g("experts.e4", "fixed.z0"), g("qkv.v", "soft.z0", "experts.e5"),
              g("fixed.z1", "soft.zt0", "embed.qk1", "experts.e6"), g("experts.e7", "route.xT", "soft.z1")]
    for p in range(PAIRS):
        order += [("soft", f"nm{p}", "T")] + ([("soft", f"st{p + 2}", "T")] if p + 2 < PAIRS else [])
        order += [("fixed", f"sc{p}", "S")] + first[p]
        order += [("soft", f"mx{p + 1}", "S"), ("fixed", f"st{p + 1}", "T")] if p + 1 < PAIRS else []
        order += [("soft", f"sc{p}", "S")] + second[p]
    return order + g("fixed.z2", "route.rt", "load.xt0", "soft.z2", "soft.zt1", "load.xt1", "embed.v",
                     "load.xt2", "fixed.out", "soft.zt2")


class Turn:

    def __init__(self, t, images):
        self.t, self.images = t, images
        self.live = STAGES if not isinstance(t, int) else tuple(
            s for s in STAGES if 0 <= t - LAG[s] < images)

    def image(self, stage):
        return self.t - LAG[stage]

    def later(self, stage):
        return not isinstance(self.t, int) or self.t > LAG[stage]

    def previous(self):
        return Turn(self.t - 1, self.images)


class Steps:

    def __init__(self, sem, stage, names):
        self.sem, self.stage, self.names = sem, stage, names

    def at(self, turn, name, back=0):
        per, k, late = len(self.names), self.names.index(name) + 1, LAG[self.stage] + back
        return turn.t * per + (k - late * per)


class Banks:

    def __init__(self, kind, banks, reader, fresh):
        self.order = [(s, n) for s, n, k in pe_order() if k == kind]
        self.banks, self.reader, self.fresh = banks, reader, fresh

    def slot(self, use):
        return self.order.index(use) % len(self.banks)

    def __call__(self, stage, name):
        return self.banks[self.slot((stage, name))]

    def vacant(self, turn, stage, name):
        mine = [u for u in self.order if self.slot(u) == self.slot((stage, name))]
        before = mine[:mine.index((stage, name))]
        while True:
            live = [u for u in before if u[0] in turn.live]
            if live:
                steps, step = self.reader[live[-1]]
                return steps.sem, steps.at(turn, step)
            if isinstance(turn.t, int) and turn.t == 0:
                return self.fresh
            turn, before = turn.previous(), mine


def run_turns(engine, images, body):
    first = len(STAGES)
    for t in range(first):
        body(Turn(t, images))
    with engine.Fori(first, images) as t:
        body(Turn(t, images))
    for t in range(images, images + len(STAGES) - 1):
        body(Turn(t, images))


def tower(nc, x, pos, base, ln_w, ln_b, wmap, w_a, w_b, w_p, b_p, w_r, w_e, cls, eye, out):
    images = x.shape[0]
    ctx = ExitStack()
    with ctx:
        def sb(name, shape, dt=F32):
            return ctx.enter_context(nc.sbuf_tensor(name, shape, dt))

        def ps(name, shape, dt=F32):
            return ctx.enter_context(nc.psum_tensor(name, shape, dt))

        def sem(name):
            return ctx.enter_context(nc.semaphore(name))

        W_map = sb("W_map", [128, KC, W])
        addend = sb("addend", [T, 2, W])
        base_sb = sb("base_sb", [T, 2, W])
        lnw = sb("lnw", [T, 2, W])
        lnb = sb("lnb", [T, 2, W])
        Wa = sb("Wa", [HC + 1, 2, 3, HC])
        Wb = sb("Wb", [HC + 1, 2, 3 * W])
        Wp = sb("Wp", [128, GROUPS, W])
        bp = sb("bp", [T, W])
        Wr = sb("Wr", [HC + 1, 2, NE])
        We = sb("We", [HC + 1, 2, NE * W])
        clsrow = sb("clsrow", [1, W])
        ident = sb("ident", [128, 128])
        identb = sb("identb", [128, 128], BF16)
        ones = sb("ones", [T, T])
        ones_not0 = sb("ones_not0", [T, T])
        not0 = sb("not0", [T, 1])
        halfneg = sb("halfneg", [T, 2])
        rank = sb("rank", [T, 2, NE])
        dve_scrap = sb("dve_scrap", [1, 2])
        X = sb("X", [T, 2, KD])
        XT = sb("XT", [128, KC, ROWS])
        tok = sb("tok", [T, 2, W])
        rowsum = sb("rowsum", [T, 1])
        negmean = sb("negmean", [T, 1])
        sqs = sb("sqs", [T, 2])
        sqtmp = sb("sqtmp", [T, 2, W])
        varA = sb("varA", [T, 1])
        rstdA = sb("rstdA", [T, 1])
        xn = sb("xn", [T, 2, W])
        xTA = sb("xTA", [HC + 1, 2, ROWS])
        qkA = sb("qkA", [T, 2, 2, W])
        resid = sb("resid", [T, 2, 2, W])
        stackA = sb("stackA", [TP, 2, 2 * HEADS, 6, DH], BF16)
        vA = sb("vA", [T, 2, HEADS, 32])
        tokres = sb("tokres", [T, 2, W])
        stA = sb("stA", [SK + 3, 3, 2, 2, 2 * TP], BF16)
        nm = sb("nm", [T, 2, 4])
        nmr = sb("nmr", [T, 2, 4])
        nms = sb("nms", [TP, 2, 4, 3], BF16)
        PA = sb("PA", [T, 4, 2, 2, 2 * TP])
        zA = sb("zA", [128, 2, 2 * TP])
        rden = sb("rden", [T, 2, 4])
        hm = sb("hm", [T, 2, W])
        H = sb("H", [T, 2, W])
        bnB = sb("bnB", [T, 2, 6])
        mvB = sb("mvB", [T, 2, 2])
        varB = sb("varB", [T, 2])
        rstdB = sb("rstdB", [T, 2])
        scaleB = sb("scaleB", [T, 2])
        x2 = sb("x2", [T, 2, W])
        xTB = sb("xTB", [HC + 1, 2, ROWS])
        qkB = sb("qkB", [T, 2, 2, W], I16)
        v16 = sb("v16", [T, 2, W], I16)
        stackB = sb("stackB", [TP, 2, 2 * HEADS, 6, DH], BF16)
        vB = sb("vB", [T, 2, HEADS, 32])
        Hres = sb("Hres", [T, 2, W])
        stB = sb("stB", [SK, 2, 2, 2, 2 * TP], BF16)
        S16 = sb("S16", [T, 2, 8 * TP], I16)
        SB = sb("SB", [T, 4, 2, 2, 2 * TP])
        z16 = sb("z16", [128, 2, 2 * TP], I16)
        zB = sb("zB", [128, GROUPS, 2 * TP])
        o32 = sb("o32", [T, 2, W], I32)
        H2 = sb("H2", [T, 2, W])
        H2res = sb("H2res", [T, 2, W])
        bnC = sb("bnC", [T, 2, 6])
        mvC = sb("mvC", [T, 2, 2])
        varC = sb("varC", [T, 2])
        rstdC = sb("rstdC", [T, 2])
        x3 = sb("x3", [T, 2, W])
        xTC = sb("xTC", [HC + 1, 2, ROWS])
        top = sb("top", [T, 2])
        sc = sb("sc", [T, 2, NE])
        pr = sb("pr", [T, 2, NE])
        eq = sb("eq", [T, 2, NE])
        sel1 = sb("sel1", [T, 2, NE])
        rest = sb("rest", [T, 2, NE])
        r1 = sb("r1", [T, 2])
        r2 = sb("r2", [T, 2])
        p1 = sb("p1", [T, 2])
        p2 = sb("p2", [T, 2])
        gate = sb("gate", [T, 2, NE])
        acc = sb("acc", [T, 2, W])

        Gt = [ps(f"G{i}", [128, 512]) for i in range(2)]
        St = [ps(f"S{i}", [128, 2, 512]) for i in range(2)]
        Tt = [ps(f"T{i}", [128, 1024], BF16) for i in range(2)]

        act_embed = ["sq0", "sq1", "xT", "xT0", "qk0", "qk1", "hq", "hk", "v0", "v1"]
        act_soft = ["tok", "p0", "p1", "p2", "p3", "z0", "p4", "p5", "z1", "z2"]
        act_qkv = ["xT", "qk0", "qk1", "v", "kept", "hq", "hk"]
        act_fixed = ["st0", "s0", "st1", "s1", "st2", "s2", "st3", "z0", "s3", "st4", "H2", "s4", "st5", "z1",
                     "s5", "z2"]
        act_route = ["xT", "exp"]
        dve_embed = ["tok", "negmean", "var", "xn", "resid", "mid", "mid2"]
        dve_qkv = ["bn0", "bn1", "mv0", "mv1", "var", "scale", "x2a", "x2b", "x2", "mid", "v"]
        dve_soft = ["st0", "st1", "mx0", "n1_0", "n2_0", "n3_0", "n4_0"]
        dve_fixed = []
        for p in range(PAIRS):
            dve_soft += [f"nmT{p}"]
            if p + 2 < PAIRS:
                dve_soft += [f"st{p + 2}"]
            if p + 1 < PAIRS:
                dve_soft += [f"mx{p + 1}"] + [f"n{i}_{p + 1}" for i in (1, 2, 3, 4)]
            dve_fixed += [f"f{p}"] + {3: ["z0"], 4: ["z1"]}.get(p, [])
            dve_soft += ["rden0", "hm0"] if p == 4 else []
        dve_soft += ["rden1", "hm1", "rden2", "hm2", "H"]
        dve_fixed += ["z2", "o32", "H2"]
        dve_route = ["bn0", "bn1", "mv0", "mv1", "var", "x3a", "x3b", "kept", "top", "sc", "sum", "rsum",
                     "pr", "p1", "eq1", "key1", "r1", "sel1", "rest", "p2", "eq2", "key2", "r2", "sel2",
                     "sel", "chosen", "den", "den2", "rden", "gate"]
        act_load_done = Steps(sem("act_load_done"), "load", ["xt0", "xt1", "xt2"])
        act_embed_done = Steps(sem("act_embed_done"), "embed", act_embed)
        act_soft_done = Steps(sem("act_soft_done"), "soft", act_soft)
        act_qkv_done = Steps(sem("act_qkv_done"), "qkv", act_qkv)
        act_fixed_done = Steps(sem("act_fixed_done"), "fixed", act_fixed)
        act_route_done = Steps(sem("act_route_done"), "route", act_route)
        dve_embed_done = Steps(sem("dve_embed_done"), "embed", dve_embed)
        dve_soft_done = Steps(sem("dve_soft_done"), "soft", dve_soft)
        dve_qkv_done = Steps(sem("dve_qkv_done"), "qkv", dve_qkv)
        dve_fixed_done = Steps(sem("dve_fixed_done"), "fixed", dve_fixed)
        dve_route_done = Steps(sem("dve_route_done"), "route", dve_route)
        dve_experts_done = Steps(sem("dve_experts_done"), "experts",
                                 [f"acc{u}{e}" for u in range(NE) for e in range(2)])
        pool_embed_done = Steps(sem("pool_embed_done"), "embed", ["rstd", "xw", "x", "low"])
        pool_soft_done = Steps(sem("pool_soft_done"), "soft", ["H"])
        pool_qkv_done = Steps(sem("pool_qkv_done"), "qkv", ["rstd", "mid2"])
        pool_route_done = Steps(sem("pool_route_done"), "route", ["rstd"])
        order = pe_order()
        pe_done = {s: Steps(sem(f"pe_{s}_done"), s, [n for st, n, _ in order if st == s]) for s in STAGES}
        reader = {("load", n): (act_load_done, n) for n in ("xt0", "xt1", "xt2")}
        reader |= {("embed", "xT"): (act_embed_done, "xT0"), ("embed", "tok"): (dve_embed_done, "tok"),
                   ("embed", "sum"): (dve_embed_done, "negmean"), ("embed", "sq"): (dve_embed_done, "var"),
                   ("embed", "qk0"): (act_embed_done, "qk0"), ("embed", "qk1"): (act_embed_done, "qk1"),
                   ("embed", "v"): (act_embed_done, "v1"), ("route", "xT"): (act_route_done, "xT"),
                   ("route", "rt"): (dve_route_done, "sc"), ("fixed", "out"): (dve_fixed_done, "o32")}
        reader |= {("qkv", n): (act_qkv_done, n) for n in ("xT", "qk0", "qk1", "v")}
        for p in range(PAIRS):
            reader |= {("soft", f"st{p}"): (dve_soft_done, f"st{p}"), ("soft", f"mx{p}"): (dve_soft_done, f"mx{p}"),
                       ("soft", f"nm{p}"): (dve_soft_done, f"nmT{p}"), ("soft", f"sc{p}"): (act_soft_done, f"p{p}"),
                       ("fixed", f"st{p}"): (act_fixed_done, f"st{p}"),
                       ("fixed", f"sc{p}"): (act_fixed_done, f"s{p}")}
        for g in range(GROUPS):
            reader |= {("soft", f"z{g}"): (act_soft_done, f"z{g}"), ("fixed", f"z{g}"): (act_fixed_done, f"z{g}"),
                       ("soft", f"zt{g}"): (dve_soft_done, f"hm{g}")}
        reader |= {("experts", f"e{u}"): (dve_experts_done, f"acc{u}1") for u in range(NE)}
        x_loaded = sem("x_loaded")
        weights_loaded = sem("weights_loaded")
        consts_made = sem("consts_made")
        quantised = sem("quantised")
        out_stored = sem("out_stored")
        LOADS = 13
        QUANTS = 14

        fills = [(X[0:2, 0, :], 0.0), (xTA[HC:HC + 1], 1.0), (xTB[HC:HC + 1], 1.0), (xTC[HC:HC + 1], 1.0),
                 (ones[:], 1.0), (ones_not0[:], 1.0), (not0[:], 1.0), (halfneg[:], -0.5),
                 (vA[:, :, :, DH:32], 0.0), (vB[:], 0.0), (stackA[:], 0.0), (stackB[:], 0.0),
                 (nms[:], 0.0), (stA[SK:SK + 3, :, 1, :, :], 1.0), (ones_not0[0:1, :], 0.0),
                 (not0[0:1, :], 0.0), (vA[:, :, :, DH:DH + 1], 1.0), (vA[0:1, 0, :, DH:DH + 1], 0.0),
                 *((rank[:, :, e:e + 1], float(NE - e)) for e in range(NE))]
        MEMSETS = len(fills) + 1
        fresh = (consts_made, MEMSETS)
        G, S, R = (Banks(k, tiles, reader, fresh) for k, tiles in (("G", Gt), ("S", St), ("T", Tt)))

        block = ctx.enter_context(nc.Block())

        def in_tiles(ap):
            return ap.rearrange("(t p) d -> p t d", p=T)

        def part(stack, slot_q, slot_k):
            a = stack[0:T, 0, :, slot_q, :]
            s_step = stack[:].ap[1][0] + (slot_k - slot_q) * DH
            return bass.AP(a.tensor, a.offset, [a.ap[0], [s_step, 2], a.ap[1], a.ap[2]])

        def all_heads(qk):
            return qk[:].rearrange("p s t (h e) -> p s (t h) e", h=HEADS)

        def dve_fence(k):
            nc.vector.memset(dve_scrap[:, k:k + 1], 0.0)

        @block.sync
        def _(sp):
            for dst, src in ((W_map[:], wmap), (addend[:], in_tiles(pos)), (base_sb[:], in_tiles(base)),
                             (lnw[:], in_tiles(ln_w)), (lnb[:], in_tiles(ln_b)), (Wa[:], w_a),
                             (Wb[:], w_b), (Wp[:], w_p), (bp[:], b_p), (Wr[:], w_r), (We[:], w_e),
                             (clsrow[:], cls), (ident[:], eye)):
                sp.dma_start(dst, src).then_inc(weights_loaded, 16)

            def body(turn):
                if "load" in turn.live:
                    i = turn.image("load")
                    if turn.later("load"):
                        sp.wait_ge(pe_done["load"].sem, pe_done["load"].at(turn, "xt2", back=1))
                    else:
                        sp.wait_ge(consts_made, MEMSETS)
                    sp.dma_start(X[2:T, 0, :], x[i, 0:T - 2, :]).then_inc(x_loaded, 16)
                    sp.dma_start(X[0:T, 1, :], x[i, T - 2:2 * T - 2, :]).then_inc(x_loaded, 16)
                if "experts" in turn.live:
                    sp.wait_ge(dve_experts_done.sem, dve_experts_done.at(turn, f"acc{NE - 1}1"))
                    sp.dma_start(in_tiles(out[turn.image("experts")]), acc[:]).then_inc(out_stored, 16)

            run_turns(sp, images, body)
            sp.wait_ge(out_stored, 16 * images)

        @block.tensor
        def _(pe):
            mm = nc.tensor.matmul

            def flip(dst, src, eye_):
                return nc.tensor.matmul(dst, src, eye_, start=True, stop=True, is_transpose=True)

            pe.wait_ge(weights_loaded, 16 * LOADS)
            pe.wait_ge(consts_made, MEMSETS)
            pe.wait_ge(quantised, QUANTS)

            def patches_turned(turn, k):
                if k == 0:
                    pe.wait_ge(x_loaded, (turn.image("load") + 1) * 32)
                pe.wait_ge(*G.vacant(turn, "load", f"xt{k}"))
                bank = G("load", f"xt{k}")
                for c in (0, 1):
                    for t in (0, 1):
                        o = c * ROWS + t * T
                        last = flip(bank[:, o:o + T], X[:, t, (2 * k + c) * 128:(2 * k + c + 1) * 128],
                                    ident[0:T, 0:T])
                last.then_inc(pe_done["load"].sem, 1)

            def tokens(turn):
                pe.wait_ge(act_load_done.sem, act_load_done.at(turn.previous(), "xt2"))
                pe.wait_ge(*G.vacant(turn, "embed", "tok"))
                bank = G("embed", "tok")
                for t in (0, 1):
                    for c in range(KC):
                        last = mm(bank[0:T, t * W:(t + 1) * W], XT[:, c, t * T:(t + 1) * T], W_map[:, c, :],
                                  start=(c == 0), stop=(c == KC - 1))
                last.then_inc(pe_done["embed"].sem, 1)

            def rows_turned(turn, stage, src):
                pe.wait_ge(*G.vacant(turn, stage, "xT"))
                bank = G(stage, "xT")
                for c in (0, 1):
                    for t in (0, 1):
                        o = c * ROWS + t * T
                        last = flip(bank[0:HC, o:o + T], src[:, t, c * HC:(c + 1) * HC], ident[0:T, 0:T])
                last.then_inc(pe_done[stage].sem, 1)

            def sum_over_partitions(turn):
                pe.wait_ge(dve_embed_done.sem, dve_embed_done.at(turn, "tok"))
                pe.wait_ge(*G.vacant(turn, "embed", "sum"))
                mm(G("embed", "sum")[0:T, 0:1], ones[:], rowsum[:], start=True,
                   stop=True).then_inc(pe_done["embed"].sem, 1)

            def squares_over_partitions(turn):
                pe.wait_ge(act_embed_done.sem, act_embed_done.at(turn, "sq1"))
                pe.wait_ge(*G.vacant(turn, "embed", "sq"))
                bank = G("embed", "sq")
                mm(bank[0:T, 0:1], ones_not0[:], sqs[:, 0:1], start=True, stop=False)
                mm(bank[0:T, 0:1], ones[:], sqs[:, 1:2], start=False,
                   stop=True).then_inc(pe_done["embed"].sem, 1)

            def qk_float(turn, t):
                pe.wait_ge(act_embed_done.sem, act_embed_done.at(turn, "xT0"))
                pe.wait_ge(*G.vacant(turn, "embed", f"qk{t}"))
                o = G("embed", f"qk{t}")[0:T, 0:2 * W].rearrange("p (s d) -> p s d", s=2)
                for c in (0, 1):
                    last = mm(o[:, :, c * HC:(c + 1) * HC], xTA[:, c, t * T:(t + 1) * T], Wa[:, c, 0:2, :],
                              start=True, stop=True)
                last.then_inc(pe_done["embed"].sem, 1)

            def v_float(turn):
                pe.wait_ge(*G.vacant(turn, "embed", "v"))
                bank = G("embed", "v")
                for t in (0, 1):
                    for c in (0, 1):
                        last = mm(bank[0:T, t * W + c * HC:t * W + (c + 1) * HC],
                                  xTA[:, c, t * T:(t + 1) * T], Wa[:, c, 2, :], start=True, stop=True)
                last.then_inc(pe_done["embed"].sem, 1)

            def fixed_product(bank, t, first, n, at):
                for c in (0, 1):
                    last = mm(bank[0:T, at:at + n], xTB[:, c, t * T:(t + 1) * T], Wb[:, c, first:first + n],
                              start=(c == 0), stop=(c == 1))
                return last

            def qk_fixed(turn, t):
                pe.wait_ge(act_qkv_done.sem, act_qkv_done.at(turn, "xT"))
                pe.wait_ge(*G.vacant(turn, "qkv", f"qk{t}"))
                fixed_product(G("qkv", f"qk{t}"), t, 0, 2 * W, 0).then_inc(pe_done["qkv"].sem, 1)

            def v_fixed(turn):
                pe.wait_ge(*G.vacant(turn, "qkv", "v"))
                fixed_product(G("qkv", "v"), 0, 2 * W, W, 0)
                fixed_product(G("qkv", "v"), 1, 2 * W, W, W).then_inc(pe_done["qkv"].sem, 1)

            def heads_turned(turn, stage, p):
                pe.wait_ge(*R.vacant(turn, stage, f"st{p}"))
                bank = R(stage, f"st{p}")
                for s in (0, 1):
                    for h in (0, 1):
                        for t in (0, 1):
                            o = (s * 4 + h * 2 + t) * TP
                            th = t * HEADS + 2 * p + h
                            src = (stackA if stage == "soft" else stackB)[:, s, th, :, :]
                            last = flip(bank[0:SK, o:o + TP], src.rearrange("r j e -> r (j e)"),
                                        identb[0:TP, 0:TP])
                last.then_inc(pe_done[stage].sem, 1)

            def scores_for_max(turn, p):
                pe.wait_ge(dve_soft_done.sem, dve_soft_done.at(turn, f"st{p}"))
                pe.wait_ge(*S.vacant(turn, "soft", f"mx{p}"))
                for h in (0, 1):
                    keys = stA[0:SK, p % 3, 1, h, :].rearrange("k (t r) -> k t r", t=2)[:, :, 0:T]
                    for t in (0, 1):
                        last = mm(S("soft", f"mx{p}")[0:T, h, t * ROWS:(t + 1) * ROWS],
                                  stA[0:SK, p % 3, 0, h, t * TP:t * TP + T], keys, start=True, stop=True)
                last.then_inc(pe_done["soft"].sem, 1)

            def maxima_turned(turn, p):
                pe.wait_ge(dve_soft_done.sem, dve_soft_done.at(turn, f"n4_{p}"))
                pe.wait_ge(*R.vacant(turn, "soft", f"nm{p}"))
                for n in range(4):
                    last = flip(R("soft", f"nm{p}")[SK:SK + 3, n * TP:(n + 1) * TP], nms[:, p % 2, n, :],
                                identb[0:TP, 0:TP])
                last.then_inc(pe_done["soft"].sem, 1)

            def scores_soft(turn, p):
                pe.wait_ge(dve_soft_done.sem, dve_soft_done.at(turn, f"nmT{p}"))
                pe.wait_ge(*S.vacant(turn, "soft", f"sc{p}"))
                for h in (0, 1):
                    for t in (0, 1):
                        last = mm(S("soft", f"sc{p}")[0:T, h, t * 2 * TP:(t + 1) * 2 * TP],
                                  stA[:, p % 3, 1, h, t * TP:t * TP + T], stA[:, p % 3, 0, h, :],
                                  start=True, stop=True)
                last.then_inc(pe_done["soft"].sem, 1)

            def scores_fixed(turn, p):
                pe.wait_ge(act_fixed_done.sem, act_fixed_done.at(turn, f"st{p}"))
                pe.wait_ge(*S.vacant(turn, "fixed", f"sc{p}"))
                for h in (0, 1):
                    for t in (0, 1):
                        last = mm(S("fixed", f"sc{p}")[0:T, h, t * 2 * TP:(t + 1) * 2 * TP],
                                  stB[:, p % 2, 1, h, t * TP:t * TP + T], stB[:, p % 2, 0, h, :],
                                  start=True, stop=True)
                last.then_inc(pe_done["fixed"].sem, 1)

            def times_v(bank, g, v, weights):
                for j in range(4):
                    for t in (0, 1):
                        last = mm(bank[32 * j:32 * j + 32, 0:2 * TP], v[:, t, 4 * g + j, :],
                                  weights[:, (2 * g + j // 2) % 4, j % 2, t, :], start=(t == 0), stop=(t == 1))
                return last

            def weighted_soft(turn, g):
                pe.wait_ge(act_soft_done.sem, act_soft_done.at(turn, f"p{2 * g + 1}"))
                pe.wait_ge(*G.vacant(turn, "soft", f"z{g}"))
                times_v(G("soft", f"z{g}"), g, vA, PA).then_inc(pe_done["soft"].sem, 1)

            def weighted_fixed(turn, g):
                pe.wait_ge(dve_fixed_done.sem, dve_fixed_done.at(turn, f"f{2 * g + 1}"))
                pe.wait_ge(*G.vacant(turn, "fixed", f"z{g}"))
                times_v(G("fixed", f"z{g}"), g, vB, SB).then_inc(pe_done["fixed"].sem, 1)

            def weighted_turned(turn, g):
                pe.wait_ge(act_soft_done.sem, act_soft_done.at(turn, f"z{g}"))
                pe.wait_ge(*G.vacant(turn, "soft", f"zt{g}"))
                for t in (0, 1):
                    last = flip(G("soft", f"zt{g}")[0:T, t * 128:(t + 1) * 128],
                                zA[:, g % 2, t * TP:t * TP + T], ident[:])
                last.then_inc(pe_done["soft"].sem, 1)

            def project(turn):
                pe.wait_ge(dve_fixed_done.sem, dve_fixed_done.at(turn, "z2"))
                pe.wait_ge(*G.vacant(turn, "fixed", "out"))
                for t in (0, 1):
                    for g in range(GROUPS):
                        last = mm(G("fixed", "out")[0:T, t * W:(t + 1) * W], zB[:, g, t * TP:t * TP + T],
                                  Wp[:, g, :], start=(g == 0), stop=(g == GROUPS - 1))
                last.then_inc(pe_done["fixed"].sem, 1)

            def expert_pair(turn, u):
                t, q = u % 2, u // 2
                if u == 0:
                    pe.wait_ge(act_route_done.sem, act_route_done.at(turn.previous(), "xT"))
                pe.wait_ge(*G.vacant(turn, "experts", f"e{u}"))
                for c in (0, 1):
                    last = mm(G("experts", f"e{u}")[0:T, 0:2 * W], xTC[:, c, t * T:(t + 1) * T],
                              We[:, c, 2 * q * W:(2 * q + 2) * W], start=(c == 0), stop=(c == 1))
                last.then_inc(pe_done["experts"].sem, 1)

            def router(turn):
                pe.wait_ge(act_route_done.sem, act_route_done.at(turn, "xT"))
                pe.wait_ge(*G.vacant(turn, "route", "rt"))
                for t in (0, 1):
                    for c in (0, 1):
                        last = mm(G("route", "rt")[0:T, t * NE:(t + 1) * NE], xTC[:, c, t * T:(t + 1) * T],
                                  Wr[:, c, :], start=(c == 0), stop=(c == 1))
                last.then_inc(pe_done["route"].sem, 1)

            def body(turn):
                load, embed, soft, qkv, fixed, route, experts = (s in turn.live for s in STAGES)
                if fixed:
                    pe.wait_ge(dve_qkv_done.sem, dve_qkv_done.at(turn.previous(), "mid"))
                    pe.wait_ge(pool_qkv_done.sem, pool_qkv_done.at(turn.previous(), "mid2"))
                    heads_turned(turn, "fixed", 0)
                if experts:
                    expert_pair(turn, 0)
                if soft:
                    pe.wait_ge(dve_embed_done.sem, dve_embed_done.at(turn.previous(), "mid2"))
                    pe.wait_ge(pool_embed_done.sem, pool_embed_done.at(turn.previous(), "low"))
                    heads_turned(turn, "soft", 0)
                    heads_turned(turn, "soft", 1)
                if soft:
                    scores_for_max(turn, 0)
                if experts:
                    expert_pair(turn, 1)
                if embed:
                    tokens(turn)
                for p in range(PAIRS):
                    if soft:
                        maxima_turned(turn, p)
                        if p + 2 < PAIRS:
                            heads_turned(turn, "soft", p + 2)
                    if fixed:
                        scores_fixed(turn, p)
                    if p == 2 and qkv:
                        qk_fixed(turn, 1)
                    if p == 3 and embed:
                        pe.wait_ge(pool_embed_done.sem, pool_embed_done.at(turn, "x"))
                        rows_turned(turn, "embed", xn)
                    if p == 4 and embed:
                        qk_float(turn, 0)
                    if p + 1 < PAIRS:
                        if soft:
                            scores_for_max(turn, p + 1)
                        if fixed:
                            heads_turned(turn, "fixed", p + 1)
                    if soft:
                        scores_soft(turn, p)
                    if p == 0:
                        if qkv:
                            pe.wait_ge(dve_qkv_done.sem, dve_qkv_done.at(turn, "x2"))
                            rows_turned(turn, "qkv", x2)
                        if experts:
                            expert_pair(turn, 2)
                        if embed:
                            sum_over_partitions(turn)
                    if p == 1:
                        if qkv:
                            qk_fixed(turn, 0)
                        if experts:
                            expert_pair(turn, 3)
                        if embed:
                            squares_over_partitions(turn)
                    if p == 2:
                        if experts:
                            expert_pair(turn, 4)
                        if fixed:
                            weighted_fixed(turn, 0)
                    if p == 3:
                        if qkv:
                            v_fixed(turn)
                        if soft:
                            weighted_soft(turn, 0)
                        if experts:
                            expert_pair(turn, 5)
                    if p == 4:
                        if fixed:
                            weighted_fixed(turn, 1)
                        if soft:
                            weighted_turned(turn, 0)
                        if embed:
                            qk_float(turn, 1)
                        if experts:
                            expert_pair(turn, 6)
                    if p == 5:
                        if experts:
                            expert_pair(turn, 7)
                        if route:
                            pe.wait_ge(dve_route_done.sem, dve_route_done.at(turn, "x3b"))
                            rows_turned(turn, "route", x3)
                        if soft:
                            weighted_soft(turn, 1)
                if fixed:
                    weighted_fixed(turn, 2)
                if route:
                    router(turn)
                if load:
                    patches_turned(turn, 0)
                if soft:
                    weighted_soft(turn, 2)
                    weighted_turned(turn, 1)
                if load:
                    patches_turned(turn, 1)
                if embed:
                    v_float(turn)
                if load:
                    patches_turned(turn, 2)
                if fixed:
                    project(turn)
                if soft:
                    weighted_turned(turn, 2)

            run_turns(pe, images, body)

        @block.scalar
        def _(act):
            def copy(dst, src, scale=1.0):
                return nc.scalar.activation(dst, src, ACT.Copy, scale=scale)

            act.wait_ge(weights_loaded, 16 * LOADS)
            act.wait_ge(consts_made, MEMSETS)

            def patches_kept(turn, k):
                act.wait_ge(pe_done["load"].sem, pe_done["load"].at(turn, f"xt{k}"))
                copy(XT[:, 2 * k:2 * k + 2, :],
                     G("load", f"xt{k}")[:, 0:2 * ROWS].rearrange("p (c r) -> p c r", c=2))\
                    .then_inc(act_load_done.sem, 1)

            def operand_copied(turn, p):
                act.wait_ge(pe_done["fixed"].sem, pe_done["fixed"].at(turn, f"st{p}"))
                copy(stB[0:SK, p % 2, :, :, :].rearrange("p s h r -> p (s h r)"),
                     R("fixed", f"st{p}")[0:SK, 0:8 * TP]).then_inc(act_fixed_done.sem, 1)

            def turned(stage):
                return G(stage, "xT")[0:HC, 0:2 * ROWS].rearrange("p (c r) -> p c r", c=2)

            def rounded_scores(turn, p):
                act.wait_ge(pe_done["fixed"].sem, pe_done["fixed"].at(turn, f"sc{p}"))
                if p >= 2:
                    act.wait_ge(dve_fixed_done.sem, dve_fixed_done.at(turn, f"f{p - 2}"))
                copy(S16[:, p % 2, :].rearrange("p (h r) -> p h r", h=2),
                     S("fixed", f"sc{p}")[0:T, :, 0:4 * TP], scale=2.0 ** -8).then_inc(act_fixed_done.sem, 1)

            def exponentials(turn, p):
                act.wait_ge(pe_done["soft"].sem, pe_done["soft"].at(turn, f"sc{p}"))
                if p in (0, 1) and turn.later("soft"):
                    act.wait_ge(pe_done["soft"].sem, pe_done["soft"].at(turn, "z2", back=1))
                if p >= 4:
                    act.wait_ge(pe_done["soft"].sem, pe_done["soft"].at(turn, "z0"))
                nc.scalar.activation(PA[:, p % 4, :, :, :].rearrange("p h c r -> p h (c r)"),
                                     S("soft", f"sc{p}")[0:T, :, 0:4 * TP], ACT.Exp,
                                     scale=DH ** -0.5).then_inc(act_soft_done.sem, 1)

            def weighted_rounded(turn, g):
                act.wait_ge(pe_done["fixed"].sem, pe_done["fixed"].at(turn, f"z{g}"))
                if g == 2:
                    act.wait_ge(dve_fixed_done.sem, dve_fixed_done.at(turn, "z0"))
                copy(z16[:, g % 2, :], G("fixed", f"z{g}")[:, 0:2 * TP],
                     scale=2.0 ** -8).then_inc(act_fixed_done.sem, 1)

            def weighted_kept(turn, g):
                act.wait_ge(pe_done["soft"].sem, pe_done["soft"].at(turn, f"z{g}"))
                copy(zA[:, g % 2, :], G("soft", f"z{g}")[:, 0:2 * TP]).then_inc(act_soft_done.sem, 1)

            def qk_fixed_rounded(turn, t):
                act.wait_ge(pe_done["qkv"].sem, pe_done["qkv"].at(turn, f"qk{t}"))
                if t == 0 and turn.later("qkv"):
                    act.wait_ge(dve_qkv_done.sem, dve_qkv_done.at(turn, "mid", back=1))
                copy(qkB[:, :, t, :], G("qkv", f"qk{t}")[0:T, 0:2 * W].rearrange("p (s d) -> p s d", s=2),
                     scale=2.0 ** -16).then_inc(act_qkv_done.sem, 1)

            def float_high_part(turn, s):
                act.wait_ge(act_embed_done.sem, act_embed_done.at(turn, "qk1"))
                if turn.later("embed"):
                    act.wait_ge(pe_done["soft"].sem, pe_done["soft"].at(turn, "st5"))
                slots = slice(1, 6, 2) if s else slice(0, 3)
                copy(stackA[0:T, s, :, slots, :],
                     all_heads(qkA)[:, s, :, :].unsqueeze(2).to_broadcast([T, 2 * HEADS, 3, DH]))\
                    .then_inc(act_embed_done.sem, 1)

            def fixed_high_part(turn, s):
                act.wait_ge(act_qkv_done.sem, act_qkv_done.at(turn, "qk1"))
                if turn.later("qkv"):
                    act.wait_ge(pe_done["fixed"].sem, pe_done["fixed"].at(turn, "st5"))
                slots = slice(0, 3, 2) if s else slice(0, 2)
                copy(stackB[0:T, s, :, slots, :],
                     all_heads(qkB)[:, s, :, :].unsqueeze(2).to_broadcast([T, 2 * HEADS, 2, DH]))\
                    .then_inc(act_qkv_done.sem, 1)

            def qk_kept(turn, t):
                act.wait_ge(pe_done["embed"].sem, pe_done["embed"].at(turn, f"qk{t}"))
                if t == 0 and turn.later("embed"):
                    act.wait_ge(dve_embed_done.sem, dve_embed_done.at(turn, "resid", back=1))
                copy(qkA[:, :, t, :], G("embed", f"qk{t}")[0:T, 0:2 * W].rearrange("p (s d) -> p s d", s=2))\
                    .then_inc(act_embed_done.sem, 1)

            def body(turn):
                load, embed, soft, qkv, fixed, route, experts = (s in turn.live for s in STAGES)
                if fixed:
                    operand_copied(turn, 0)
                if soft:
                    if turn.later("soft"):
                        act.wait_ge(pool_soft_done.sem, pool_soft_done.at(turn, "H", back=1))
                    act.wait_ge(dve_embed_done.sem, dve_embed_done.at(turn.previous(), "tok"))
                    copy(tokres[:], tok[:]).then_inc(act_soft_done.sem, 1)
                for p in range(PAIRS):
                    if fixed:
                        rounded_scores(turn, p)
                    if p == 1 and embed:
                        act.wait_ge(dve_embed_done.sem, dve_embed_done.at(turn, "negmean"))
                        for t in (0, 1):
                            nc.scalar.activation(sqtmp[:, t, :], tok[:, t, :], ACT.Square, bias=negmean[:],
                                                 accum_out=sqs[:, t:t + 1]).then_inc(act_embed_done.sem, 1)
                    if p == 2 and qkv:
                        qk_fixed_rounded(turn, 1)
                    if p == 3 and embed:
                        act.wait_ge(pe_done["embed"].sem, pe_done["embed"].at(turn, "xT"))
                        copy(xTA[0:HC, :, 1:ROWS], turned("embed")[:, :, 1:ROWS]).then_inc(act_embed_done.sem, 1)
                        copy(xTA[0:HC, :, 0:1], turned("embed")[:, :, 1:2]).then_inc(act_embed_done.sem, 1)
                    if p == 4 and embed:
                        qk_kept(turn, 0)
                    if p + 1 < PAIRS and fixed:
                        operand_copied(turn, p + 1)
                    if soft:
                        exponentials(turn, p)
                    if p == 0:
                        if qkv:
                            act.wait_ge(pe_done["qkv"].sem, pe_done["qkv"].at(turn, "xT"))
                            copy(xTB[0:HC, :, :], turned("qkv")).then_inc(act_qkv_done.sem, 1)
                    if p == 1 and qkv:
                        qk_fixed_rounded(turn, 0)
                    if p == 2 and fixed:
                        weighted_rounded(turn, 0)
                    if p == 3:
                        if qkv:
                            act.wait_ge(pe_done["qkv"].sem, pe_done["qkv"].at(turn, "v"))
                            if turn.later("qkv"):
                                act.wait_ge(dve_qkv_done.sem, dve_qkv_done.at(turn, "v", back=1))
                            copy(v16[:], G("qkv", "v")[0:T, 0:2 * W].rearrange("p (t d) -> p t d", t=2),
                                 scale=2.0 ** -16).then_inc(act_qkv_done.sem, 1)
                        if soft:
                            weighted_kept(turn, 0)
                        if fixed:
                            if route:
                                act.wait_ge(dve_route_done.sem, dve_route_done.at(turn, "kept"))
                            act.wait_ge(act_qkv_done.sem, act_qkv_done.at(turn.previous(), "kept"))
                            copy(H2[:], Hres[:]).then_inc(act_fixed_done.sem, 1)
                        if qkv:
                            act.wait_ge(dve_soft_done.sem, dve_soft_done.at(turn.previous(), "H"))
                            if fixed:
                                act.wait_ge(act_fixed_done.sem, act_fixed_done.at(turn, "H2"))
                            copy(Hres[:], H[:]).then_inc(act_qkv_done.sem, 1)
                    if p == 4:
                        if fixed:
                            weighted_rounded(turn, 1)
                        if embed:
                            qk_kept(turn, 1)
                        if qkv:
                            fixed_high_part(turn, 0)
                if qkv:
                    fixed_high_part(turn, 1)
                if route:
                    act.wait_ge(pe_done["route"].sem, pe_done["route"].at(turn, "xT"))
                    copy(xTC[0:HC, :, :], turned("route")).then_inc(act_route_done.sem, 1)
                if soft:
                    weighted_kept(turn, 1)
                if embed:
                    float_high_part(turn, 0)
                if fixed:
                    weighted_rounded(turn, 2)
                if embed:
                    float_high_part(turn, 1)
                if load:
                    patches_kept(turn, 0)
                if route:
                    act.wait_ge(dve_route_done.sem, dve_route_done.at(turn, "sc"))
                    nc.scalar.activation(pr[:], sc[:], ACT.Exp).then_inc(act_route_done.sem, 1)
                if soft:
                    weighted_kept(turn, 2)
                if load:
                    patches_kept(turn, 1)
                if embed:
                    act.wait_ge(pe_done["embed"].sem, pe_done["embed"].at(turn, "v"))
                    for t in (0, 1):
                        copy(vA[:, t, :, 0:DH],
                             G("embed", "v")[0:T, t * W:(t + 1) * W].rearrange("p (h e) -> p h e", h=HEADS),
                             scale=(1.0 if t else not0[:])).then_inc(act_embed_done.sem, 1)
                if load:
                    patches_kept(turn, 2)

            run_turns(act, images, body)

        @block.vector
        def _(dve):
            v = nc.vector
            dve.wait_ge(weights_loaded, 16 * LOADS)
            v.tensor_tensor(addend[:], addend[:], base_sb[:], ALU.add).then_inc(quantised, 1)
            done = 1
            for w, bias_scale in ((Wb[0:HC, :, :], 1.0), (Wb[HC:HC + 1, :, :], 2.0 ** 16), (Wp[:], 1.0),
                                  (bp[:], 1.0)):
                v.tensor_scalar(w, w, 256.0, I16MAX, ALU.mult, ALU.min).then_inc(quantised, 1)
                done += 1
                dve.wait_ge(quantised, done)
                v.tensor_scalar(w, w, I16MIN, ROUND, ALU.max, ALU.add).then_inc(quantised, 1)
                done += 1
                dve.wait_ge(quantised, done)
                v.tensor_scalar(w, w, ROUND, bias_scale, ALU.subtract, ALU.mult).then_inc(quantised, 1)
                done += 1
            v.memset(acc[:], 0.0).then_inc(quantised, 1)
            dve.wait_ge(quantised, QUANTS)
            dve.wait_ge(consts_made, MEMSETS)

            def norm_stats(turn, rows, bn, mv, var, steps):
                for t in (0, 1):
                    v.bn_stats(bn[:, t, :], rows[:, t, :]).then_inc(steps.sem, 1)
                dve.wait_ge(steps.sem, steps.at(turn, "bn1"))
                dve_fence(0 if steps is dve_qkv_done else 1)
                for t in (0, 1):
                    v.bn_aggr(mv[:, t, :], bn[:, t, :]).then_inc(steps.sem, 1)
                dve.wait_ge(steps.sem, steps.at(turn, "mv1"))
                v.tensor_scalar(var[:], mv[:, :, 1], EPS, None, ALU.add).then_inc(steps.sem, 1)

            def operand_copied(turn, p):
                dve.wait_ge(pe_done["soft"].sem, pe_done["soft"].at(turn, f"st{p}"))
                v.tensor_copy(stA[0:SK, p % 3, :, :, :].rearrange("p s h r -> p (s h r)"),
                              R("soft", f"st{p}")[0:SK, 0:8 * TP]).then_inc(dve_soft_done.sem, 1)

            def float_scores(turn, p):
                dve.wait_ge(act_fixed_done.sem, act_fixed_done.at(turn, f"s{p}"))
                if p < 2 and turn.later("fixed"):
                    dve.wait_ge(pe_done["fixed"].sem, pe_done["fixed"].at(turn, "z2", back=1))
                if p >= 4:
                    dve.wait_ge(pe_done["fixed"].sem, pe_done["fixed"].at(turn, "z0"))
                v.tensor_copy(SB[:, p % 4, :, :, :].rearrange("p h c r -> p (h c r)"), S16[:, p % 2, :])\
                    .then_inc(dve_fixed_done.sem, 1)

            def float_weighted(turn, g):
                dve.wait_ge(act_fixed_done.sem, act_fixed_done.at(turn, f"z{g}"))
                v.tensor_copy(zB[:, g, :], z16[:, g % 2, :]).then_inc(dve_fixed_done.sem, 1)

            def row_maxima(turn, p):
                dve.wait_ge(pe_done["soft"].sem, pe_done["soft"].at(turn, f"mx{p}"))
                v.tensor_reduce(nm[:, p % 2, :].rearrange("p (h t) -> p h t", h=2),
                                S("soft", f"mx{p}")[0:T, :, 0:2 * ROWS].rearrange("p h (t r) -> p h t r", t=2),
                                AX.X, ALU.max, negate=True).then_inc(dve_soft_done.sem, 1)
                high, middle, low = (nms[0:T, p % 2, :, i] for i in range(3))
                dve.wait_ge(dve_soft_done.sem, dve_soft_done.at(turn, f"mx{p}"))
                v.tensor_copy(high, nm[:, p % 2, :]).then_inc(dve_soft_done.sem, 1)
                dve.wait_ge(dve_soft_done.sem, dve_soft_done.at(turn, f"n1_{p}"))
                v.tensor_tensor(nmr[:, p % 2, :], nm[:, p % 2, :], high, ALU.subtract)\
                    .then_inc(dve_soft_done.sem, 1)
                dve.wait_ge(dve_soft_done.sem, dve_soft_done.at(turn, f"n2_{p}"))
                v.tensor_copy(middle, nmr[:, p % 2, :]).then_inc(dve_soft_done.sem, 1)
                dve.wait_ge(dve_soft_done.sem, dve_soft_done.at(turn, f"n3_{p}"))
                v.tensor_tensor(low, nmr[:, p % 2, :], middle, ALU.subtract).then_inc(dve_soft_done.sem, 1)

            def softmax_rows(turn, g):
                dve.wait_ge(pe_done["soft"].sem, pe_done["soft"].at(turn, f"zt{g}"))
                w = G("soft", f"zt{g}")[0:T, 0:256].rearrange("p (t j e) -> p t j e", t=2, j=4)
                v.reciprocal(rden[:], w[:, :, :, DH]).then_inc(dve_soft_done.sem, 1)
                dve.wait_ge(dve_soft_done.sem, dve_soft_done.at(turn, f"rden{g}"))
                v.tensor_tensor(hm[:, :, g * 64:(g + 1) * 64].rearrange("p t (j e) -> p t j e", j=4),
                                w[:, :, :, 0:DH], rden[:].unsqueeze(3).to_broadcast([T, 2, 4, DH]), ALU.mult)\
                    .then_inc(dve_soft_done.sem, 1)

            def experts_added(turn, u):
                dve.wait_ge(pe_done["experts"].sem, pe_done["experts"].at(turn, f"e{u}"))
                t, q = u % 2, u // 2
                for e in (0, 1):
                    if q or e:
                        dve.wait_ge(dve_experts_done.sem, dve_experts_done.at(turn, f"acc{u}0" if e else f"acc{u - 2}1"))
                    before = acc if q or e else H2res
                    v.scalar_tensor_tensor(acc[:, t, :], G("experts", f"e{u}")[0:T, e * W:(e + 1) * W],
                                           gate[:, t, 2 * q + e:2 * q + e + 1], before[:, t, :],
                                           ALU.mult, ALU.add).then_inc(dve_experts_done.sem, 1)

            def per_expert(ap):
                return ap[:].unsqueeze(2).to_broadcast([T, 2, NE])

            def tt(out_, a_, b_, op):
                v.tensor_tensor(out_[:], a_, b_, op).then_inc(dve_route_done.sem, 1)

            def largest(out_, in_, op=ALU.max, **kw):
                v.tensor_reduce(out_[:], in_, AX.X, op, **kw).then_inc(dve_route_done.sem, 1)

            def router_read(turn):
                logits = G("route", "rt")[0:T, 0:2 * NE].rearrange("p (t e) -> p t e", t=2)
                dve.wait_ge(pe_done["route"].sem, pe_done["route"].at(turn, "rt"))
                largest(top, logits, negate=True)
                dve.wait_ge(dve_route_done.sem, dve_route_done.at(turn, "top"))
                tt(sc, logits, per_expert(top), ALU.add)

            def gates(turn):
                dve.wait_ge(act_route_done.sem, act_route_done.at(turn, "exp"))
                largest(r1, pr[:], ALU.add)
                dve.wait_ge(dve_route_done.sem, dve_route_done.at(turn, "sum"))
                v.reciprocal(r2[:], r1[:]).then_inc(dve_route_done.sem, 1)
                dve.wait_ge(dve_route_done.sem, dve_route_done.at(turn, "rsum"))
                tt(pr, pr[:], per_expert(r2), ALU.mult)
                dve.wait_ge(dve_route_done.sem, dve_route_done.at(turn, "pr"))
                largest(p1, pr[:])
                dve.wait_ge(dve_route_done.sem, dve_route_done.at(turn, "p1"))
                tt(eq, pr[:], per_expert(p1), ALU.is_equal)
                dve.wait_ge(dve_route_done.sem, dve_route_done.at(turn, "eq1"))
                tt(eq, eq[:], rank[:], ALU.mult)
                dve.wait_ge(dve_route_done.sem, dve_route_done.at(turn, "key1"))
                largest(r1, eq[:])
                dve.wait_ge(dve_route_done.sem, dve_route_done.at(turn, "r1"))
                tt(sel1, eq[:], per_expert(r1), ALU.is_equal)
                dve.wait_ge(dve_route_done.sem, dve_route_done.at(turn, "sel1"))
                v.scalar_tensor_tensor(rest[:], sel1[:], -2.0, pr[:], ALU.mult, ALU.add)\
                    .then_inc(dve_route_done.sem, 1)
                dve.wait_ge(dve_route_done.sem, dve_route_done.at(turn, "rest"))
                largest(p2, rest[:])
                dve.wait_ge(dve_route_done.sem, dve_route_done.at(turn, "p2"))
                tt(eq, rest[:], per_expert(p2), ALU.is_equal)
                dve.wait_ge(dve_route_done.sem, dve_route_done.at(turn, "eq2"))
                tt(eq, eq[:], rank[:], ALU.mult)
                dve.wait_ge(dve_route_done.sem, dve_route_done.at(turn, "key2"))
                largest(r1, eq[:])
                dve.wait_ge(dve_route_done.sem, dve_route_done.at(turn, "r2"))
                tt(eq, eq[:], per_expert(r1), ALU.is_equal)
                dve.wait_ge(dve_route_done.sem, dve_route_done.at(turn, "sel2"))
                tt(sel1, sel1[:], eq[:], ALU.add)
                dve.wait_ge(dve_route_done.sem, dve_route_done.at(turn, "sel"))
                tt(sel1, sel1[:], pr[:], ALU.mult)
                tt(r2, p1[:], p2[:], ALU.add)
                dve.wait_ge(dve_route_done.sem, dve_route_done.at(turn, "den"))
                v.tensor_scalar(r2[:], r2[:], 1e-9, None, ALU.add).then_inc(dve_route_done.sem, 1)
                dve.wait_ge(dve_route_done.sem, dve_route_done.at(turn, "den2"))
                v.reciprocal(r2[:], r2[:]).then_inc(dve_route_done.sem, 1)
                dve.wait_ge(dve_route_done.sem, dve_route_done.at(turn, "rden"))
                tt(gate, sel1[:], per_expert(r2), ALU.mult)

            def body(turn):
                load, embed, soft, qkv, fixed, route, experts = (s in turn.live for s in STAGES)
                if soft:
                    operand_copied(turn, 0)
                if experts:
                    if turn.later("experts"):
                        dve.wait_ge(out_stored, 16 * turn.image("experts"))
                    dve.wait_ge(dve_route_done.sem, dve_route_done.at(turn.previous(), "gate"))
                    experts_added(turn, 0)
                if soft:
                    operand_copied(turn, 1)
                    row_maxima(turn, 0)
                if qkv:
                    dve.wait_ge(pool_soft_done.sem, pool_soft_done.at(turn.previous(), "H"))
                    dve.wait_ge(dve_soft_done.sem, dve_soft_done.at(turn.previous(), "H"))
                    norm_stats(turn, H, bnB, mvB, varB, dve_qkv_done)
                if experts:
                    experts_added(turn, 1)
                if qkv:
                    dve.wait_ge(pool_qkv_done.sem, pool_qkv_done.at(turn, "rstd"))
                    v.tensor_scalar(scaleB[:], rstdB[:], 2.0 ** 16, None, ALU.mult)\
                        .then_inc(dve_qkv_done.sem, 1)
                    dve.wait_ge(dve_qkv_done.sem, dve_qkv_done.at(turn, "scale"))
                    for t in (0, 1):
                        v.tensor_scalar(x2[:, t, :], H[:, t, :], mvB[:, t, 0:1], scaleB[:, t:t + 1],
                                        ALU.subtract, ALU.mult).then_inc(dve_qkv_done.sem, 1)
                    dve.wait_ge(dve_qkv_done.sem, dve_qkv_done.at(turn, "x2b"))
                    v.tensor_scalar(x2[:], x2[:], ROUND, ROUND, ALU.add, ALU.subtract)\
                        .then_inc(dve_qkv_done.sem, 1)
                for p in range(PAIRS):
                    if soft:
                        dve.wait_ge(pe_done["soft"].sem, pe_done["soft"].at(turn, f"nm{p}"))
                        v.tensor_copy(stA[SK:SK + 3, p % 3, 0, :, :].rearrange("p h r -> p (h r)"),
                                      R("soft", f"nm{p}")[SK:SK + 3, 0:4 * TP]).then_inc(dve_soft_done.sem, 1)
                        if p + 2 < PAIRS:
                            operand_copied(turn, p + 2)
                    if p == 0 and embed:
                        dve.wait_ge(pe_done["embed"].sem, pe_done["embed"].at(turn, "tok"))
                        if soft:
                            dve.wait_ge(act_soft_done.sem, act_soft_done.at(turn, "tok"))
                        v.scalar_tensor_tensor(tok[:].rearrange("p t d -> p (t d)"), G("embed", "tok")[0:T, 0:2 * W],
                                               0.0, addend[:].rearrange("p t d -> p (t d)"), ALU.add, ALU.add,
                                               accum_out=rowsum[:]).then_inc(dve_embed_done.sem, 1)
                    if p == 1 and embed:
                        dve.wait_ge(pe_done["embed"].sem, pe_done["embed"].at(turn, "sum"))
                        v.tensor_scalar(negmean[:], G("embed", "sum")[0:T, 0:1], -1.0 / NTOK, None, ALU.mult)\
                            .then_inc(dve_embed_done.sem, 1)
                    if p == 2 and embed:
                        dve.wait_ge(pe_done["embed"].sem, pe_done["embed"].at(turn, "sq"))
                        v.tensor_scalar(varA[:], G("embed", "sq")[0:T, 0:1], 1.0 / NTOK, EPS, ALU.mult, ALU.add)\
                            .then_inc(dve_embed_done.sem, 1)
                    if fixed:
                        float_scores(turn, p)
                    if p == 2 and embed:
                        dve.wait_ge(pool_embed_done.sem, pool_embed_done.at(turn, "rstd"))
                        v.tensor_scalar(xn[:], tok[:], negmean[:], rstdA[:], ALU.add, ALU.mult)\
                            .then_inc(dve_embed_done.sem, 1)
                    if p == 3 and fixed:
                        float_weighted(turn, 0)
                    if p + 1 < PAIRS and soft:
                        row_maxima(turn, p + 1)
                    if p == 0 and experts:
                        experts_added(turn, 2)
                    if p == 1:
                        if experts:
                            experts_added(turn, 3)
                        if route:
                            dve.wait_ge(dve_fixed_done.sem, dve_fixed_done.at(turn.previous(), "H2"))
                            norm_stats(turn, H2, bnC, mvC, varC, dve_route_done)
                    if p == 2:
                        if experts:
                            experts_added(turn, 4)
                        if route:
                            dve.wait_ge(pool_route_done.sem, pool_route_done.at(turn, "rstd"))
                            for t in (0, 1):
                                v.tensor_scalar(x3[:, t, :], H2[:, t, :], mvC[:, t, 0:1], rstdC[:, t:t + 1],
                                                ALU.subtract, ALU.mult).then_inc(dve_route_done.sem, 1)
                            v.tensor_copy(H2res[:], H2[:]).then_inc(dve_route_done.sem, 1)
                    if p == 3 and experts:
                        experts_added(turn, 5)
                    if p == 4:
                        if fixed:
                            float_weighted(turn, 1)
                        if soft:
                            softmax_rows(turn, 0)
                        if experts:
                            experts_added(turn, 6)
                    if p == 5 and experts:
                        experts_added(turn, 7)
                if qkv:
                    dve.wait_ge(act_qkv_done.sem, act_qkv_done.at(turn, "hk"))
                    v.tensor_tensor(part(stackB, 2, 1), all_heads(qkB), part(stackB, 0, 0), ALU.subtract)\
                        .then_inc(dve_qkv_done.sem, 1)
                if embed:
                    dve.wait_ge(act_embed_done.sem, act_embed_done.at(turn, "hk"))
                    v.tensor_tensor(all_heads(resid), all_heads(qkA), part(stackA, 1, 1), ALU.subtract)\
                        .then_inc(dve_embed_done.sem, 1)
                    dve.wait_ge(dve_embed_done.sem, dve_embed_done.at(turn, "resid"))
                    v.tensor_copy(part(stackA, 4, 4), all_heads(resid)).then_inc(dve_embed_done.sem, 1)
                    v.tensor_copy(part(stackA, 3, 2), all_heads(resid)).then_inc(dve_embed_done.sem, 1)
                if fixed:
                    float_weighted(turn, 2)
                if route:
                    router_read(turn)
                if qkv:
                    if fixed:
                        dve.wait_ge(pe_done["fixed"].sem, pe_done["fixed"].at(turn, "z2"))
                    dve.wait_ge(act_qkv_done.sem, act_qkv_done.at(turn, "v"))
                    v.tensor_copy(vB[:, :, :, 0:DH], v16[:].rearrange("p t (h e) -> p t h e", h=HEADS))\
                        .then_inc(dve_qkv_done.sem, 1)
                if soft:
                    softmax_rows(turn, 1)
                if route:
                    gates(turn)
                if fixed:
                    dve.wait_ge(pe_done["fixed"].sem, pe_done["fixed"].at(turn, "out"))
                    v.scalar_tensor_tensor(o32[:], G("fixed", "out")[0:T, 0:2 * W].rearrange("p (t d) -> p t d", t=2),
                                           2.0 ** -8, bp[:].unsqueeze(1).to_broadcast([T, 2, W]),
                                           ALU.mult, ALU.add).then_inc(dve_fixed_done.sem, 1)
                    dve.wait_ge(dve_fixed_done.sem, dve_fixed_done.at(turn, "o32"))
                    dve.wait_ge(act_fixed_done.sem, act_fixed_done.at(turn, "H2"))
                    v.scalar_tensor_tensor(H2[:], o32[:], 2.0 ** -8, H2[:], ALU.mult, ALU.add)\
                        .then_inc(dve_fixed_done.sem, 1)
                if soft:
                    softmax_rows(turn, 2)
                    dve.wait_ge(pool_soft_done.sem, pool_soft_done.at(turn, "H"))
                    v.tensor_copy(H[0:1, 0, :], clsrow[:]).then_inc(dve_soft_done.sem, 1)

            run_turns(dve, images, body)

        @block.gpsimd
        def _(pool):
            q = nc.gpsimd
            for made, (ap, value) in enumerate(fills):
                q.memset(ap, value).then_inc(consts_made, 1)
                pool.wait_ge(consts_made, made + 1)
            pool.wait_ge(weights_loaded, 16 * LOADS)
            q.tensor_copy(identb[:], ident[:]).then_inc(consts_made, 1)
            pool.wait_ge(consts_made, MEMSETS)

            def body(turn):
                load, embed, soft, qkv, fixed, route, experts = (s in turn.live for s in STAGES)
                if qkv:
                    pool.wait_ge(dve_qkv_done.sem, dve_qkv_done.at(turn, "var"))
                    q.tensor_tensor(rstdB[:], varB[:], halfneg[:], ALU.pow).then_inc(pool_qkv_done.sem, 1)
                if route:
                    pool.wait_ge(dve_route_done.sem, dve_route_done.at(turn, "var"))
                    q.tensor_tensor(rstdC[:], varC[:], halfneg[:], ALU.pow).then_inc(pool_route_done.sem, 1)
                if embed:
                    pool.wait_ge(dve_embed_done.sem, dve_embed_done.at(turn, "var"))
                    q.tensor_tensor(rstdA[:], varA[:], halfneg[:, 0:1], ALU.pow).then_inc(pool_embed_done.sem, 1)
                    pool.wait_ge(dve_embed_done.sem, dve_embed_done.at(turn, "xn"))
                    q.tensor_tensor(xn[:], xn[:], lnw[:], ALU.mult).then_inc(pool_embed_done.sem, 1)
                    pool.wait_ge(pool_embed_done.sem, pool_embed_done.at(turn, "xw"))
                    q.tensor_tensor(xn[:], xn[:], lnb[:], ALU.add).then_inc(pool_embed_done.sem, 1)
                if qkv:
                    pool.wait_ge(dve_qkv_done.sem, dve_qkv_done.at(turn, "mid"))
                    q.tensor_tensor(part(stackB, 3, 3), part(stackB, 2, 1), part(stackB, 4, 4), ALU.add)\
                        .then_inc(pool_qkv_done.sem, 1)
                if embed:
                    pool.wait_ge(dve_embed_done.sem, dve_embed_done.at(turn, "mid"))
                    q.tensor_tensor(part(stackA, 5, 0), all_heads(resid), part(stackA, 4, 4), ALU.subtract)\
                        .then_inc(pool_embed_done.sem, 1)
                if soft:
                    pool.wait_ge(dve_soft_done.sem, dve_soft_done.at(turn, "hm2"))
                    if qkv:
                        pool.wait_ge(act_qkv_done.sem, act_qkv_done.at(turn, "kept"))
                    q.tensor_tensor(H[:], hm[:], tokres[:], ALU.add).then_inc(pool_soft_done.sem, 1)

            run_turns(pool, images, body)


def positions():
    seq = ROWS - 1
    i = np.arange(seq, dtype=np.float32)[:, None]
    j = np.arange(W, dtype=np.float32)[None, :]
    even = (np.arange(W) % 2 == 0)[None, :]
    base = np.float32(10000.0)
    one = np.float32(1.0)
    angle = i / np.where(even, base ** (j / np.float32(W)), base ** ((j - one) / np.float32(W)))
    table = np.zeros((ROWS, W), np.float32)
    table[1:] = np.where(even, np.sin(angle), np.cos(angle))
    return table


def kernel(**inputs):
    import concourse.bacc as bacc
    from concourse.bass_utils import run_bass_kernel_spmd as run

    def get(name):
        return np.asarray(inputs[name])

    x = np.ascontiguousarray(get("x"))
    images = x.shape[0]
    arrays = {"x": x.reshape(images, 196, KD), "pos": positions()}
    base = np.zeros((ROWS, W), np.float32)
    base[1] = get("L0_tok_class_token")[0]
    base[2:] = get("L0_tok_b_map")
    arrays["base"] = base
    for name, key in (("ln_w", "L0_tok_ln_w"), ("ln_b", "L0_tok_ln_b")):
        arrays[name] = np.zeros((ROWS, W), np.float32)
        arrays[name][1:] = get(key)
    arrays["wmap"] = get("L0_tok_W_map").T.reshape(KC, 128, W).transpose(1, 0, 2)
    w_a = np.zeros((HC + 1, 2, 3, HC), np.float32)
    for s, (w, bias) in enumerate((("L0_tok_Wq", "L0_tok_bq"), ("L0_tok_Wk", "L0_tok_bk"),
                                   ("L0_tok_Wv", "L0_tok_bv"))):
        for h in range(HEADS):
            c, o = h // 6, (h % 6) * DH
            w_a[o:o + DH, c, s, o:o + DH] = get(w)[h].T
            w_a[HC, c, s, o:o + DH] = get(bias)[h]
    arrays["w_a"] = w_a
    w = get("L0_attn_wqkv").reshape(HEADS, 3, DH, W).transpose(3, 1, 0, 2).reshape(W, 3 * W)
    w_b = np.zeros((HC + 1, 2, 3 * W), np.float32)
    w_b[0:HC] = w.reshape(2, HC, 3 * W).transpose(1, 0, 2)
    w_b[HC, 0] = get("L0_attn_bqkv").reshape(HEADS, 3, DH).transpose(1, 0, 2).reshape(3 * W)
    arrays["w_b"] = w_b
    w_p = np.zeros((4, 32, GROUPS, W), np.float32)
    w_p[:, 0:DH] = get("L0_attn_wp").T.reshape(GROUPS, 4, DH, W).transpose(1, 2, 0, 3)
    arrays["w_p"] = w_p.reshape(128, GROUPS, W)
    arrays["b_p"] = np.broadcast_to(get("L0_attn_bp"), (T, W))
    w_r = np.zeros((HC + 1, 2, NE), np.float32)
    w_r[0:HC] = get("L0_ffn_router_w").T.reshape(2, HC, NE).transpose(1, 0, 2)
    w_r[HC, 0] = get("L0_ffn_router_b")
    arrays["w_r"] = w_r
    w_e = np.zeros((HC + 1, 2, NE * W), np.float32)
    w_e[0:HC] = get("L0_ffn_expert_w").transpose(2, 0, 1).reshape(2, HC, NE * W).transpose(1, 0, 2)
    w_e[HC, 0] = get("L0_ffn_expert_b").reshape(NE * W)
    arrays["w_e"] = w_e
    arrays["cls"] = get("cls_tok").reshape(1, W)
    arrays["eye"] = np.eye(128, dtype=np.float32)
    arrays = {f"{n}_dram": np.ascontiguousarray(a) for n, a in arrays.items()}

    nc = bacc.Bacc("TRN2", target_bir_lowering=False, num_devices=1)
    args = [nc.dram_tensor(n, a.shape, mybir.dt.from_np(a.dtype), kind="ExternalInput").ap()
            for n, a in arrays.items()]
    out = nc.dram_tensor("out_dram", (images, ROWS, W), F32, kind="ExternalOutput").ap()
    tower(nc, *args, out)
    r = run(nc, [arrays], core_ids=[0])
    return r.results[0]["out_dram"]
```

```python
from contextlib import ExitStack

import numpy as np

import concourse.bass as bass
from concourse import mybir

F32 = mybir.dt.float32
F32R = mybir.dt.float32r
BF16 = mybir.dt.bfloat16
I16 = mybir.dt.int16
I32 = mybir.dt.int32
ALU = mybir.AluOpType
ACT = mybir.ActivationFunctionType
AX = mybir.AxisListType

W = 192
HEADS = 12
DH = W // HEADS
ROWS = 198
T = ROWS // 2
TP = T + 1
KD = 768
KC = KD // 128
HC = W // 2
SK = 6 * DH
PAIRS = HEADS // 2
GROUPS = HEADS // 4
NE = 8
EPS = 1e-5
ROUND = 1.5 * 2.0 ** 23
I16MAX, I16MIN = 32767.0, -32768.0
NTOK = (ROWS - 1) * W
STAGES = ("load", "embed", "soft", "qkv", "fixed", "route", "experts")
LAG = {s: i for i, s in enumerate(STAGES)}


def pe_order():
    g = lambda *uses: [(u.split(".")[0], u.split(".")[1], "G") for u in uses]
    order = [("fixed", "st0", "T"), ("soft", "st0", "T"), *g("experts.e0"), ("soft", "st1", "T"),
             ("soft", "mx0", "S"), *g("experts.e1", "embed.tok")]
    first = [g("qkv.xT"), g("qkv.qk0"), g("qkv.qk1"), g("embed.xT"), g("embed.qk0"), g("soft.zt0")]
    second = [g("load.xt0", "embed.sum", "experts.e2"), g("route.xT", "embed.sq", "experts.e3", "load.xt1"),
              g("fixed.z0", "route.rt", "experts.e4"), g("qkv.v", "soft.z0", "experts.e5"),
              g("fixed.z1", "embed.qk1", "experts.e6"), g("soft.z1", "load.xt2", "experts.e7")]
    for p in range(PAIRS):
        order += [("soft", f"nm{p}", "T")] + ([("soft", f"st{p + 2}", "T")] if p + 2 < PAIRS else [])
        order += [("fixed", f"sc{p}", "S")] + first[p]
        order += [("soft", f"mx{p + 1}", "S"), ("fixed", f"st{p + 1}", "T")] if p + 1 < PAIRS else []
        order += [("soft", f"sc{p}", "S")] + second[p]
    return order + [*g("fixed.z2"), ("soft", "z2", "S"), *g("soft.zt1"), ("embed", "v", "S"),
                    *g("fixed.out", "soft.zt2")]


class Turn:

    def __init__(self, t, images):
        self.t, self.images = t, images
        self.live = STAGES if not isinstance(t, int) else tuple(
            s for s in STAGES if 0 <= t - LAG[s] < images)

    def image(self, stage):
        return self.t - LAG[stage]

    def later(self, stage):
        return not isinstance(self.t, int) or self.t > LAG[stage]

    def previous(self):
        return Turn(self.t - 1, self.images)


class Steps:

    def __init__(self, sem, stage, names):
        self.sem, self.stage, self.names = sem, stage, names

    def at(self, turn, name, back=0):
        per, k, late = len(self.names), self.names.index(name) + 1, LAG[self.stage] + back
        return turn.t * per + (k - late * per)


class Banks:

    def __init__(self, kind, banks, reader, fresh):
        self.order = [(s, n) for s, n, k in pe_order() if k == kind]
        self.banks, self.reader, self.fresh = banks, reader, fresh

    def slot(self, use):
        return self.order.index(use) % len(self.banks)

    def __call__(self, stage, name):
        return self.banks[self.slot((stage, name))]

    def vacant(self, turn, stage, name):
        mine = [u for u in self.order if self.slot(u) == self.slot((stage, name))]
        before = mine[:mine.index((stage, name))]
        while True:
            live = [u for u in before if u[0] in turn.live]
            if live:
                steps, step = self.reader[live[-1]]
                return steps.sem, steps.at(turn, step)
            if isinstance(turn.t, int) and turn.t == 0:
                return self.fresh
            turn, before = turn.previous(), mine


def run_turns(engine, images, body):
    first = len(STAGES)
    for t in range(first):
        body(Turn(t, images))
    with engine.Fori(first, images) as t:
        body(Turn(t, images))
    for t in range(images, images + len(STAGES) - 1):
        body(Turn(t, images))


def tower(nc, x, pos, base, ln_w, ln_b, wmap, w_a, w_b, w_p, b_p, w_r, w_e, cls, eye, out):
    images = x.shape[0]
    ctx = ExitStack()
    with ctx:
        def sb(name, shape, dt=F32):
            return ctx.enter_context(nc.sbuf_tensor(name, shape, dt))

        def ps(name, shape, dt=F32):
            return ctx.enter_context(nc.psum_tensor(name, shape, dt))

        def sem(name):
            return ctx.enter_context(nc.semaphore(name))

        W_map = sb("W_map", [128, KC, W])
        addend = sb("addend", [T, 2, W])
        base_sb = sb("base_sb", [T, 2, W])
        lnw = sb("lnw", [T, 2, W])
        lnb = sb("lnb", [T, 2, W])
        Wa = sb("Wa", [HC + 1, 2, 3, HC])
        Wb = sb("Wb", [HC + 1, 2, 3 * W])
        Wp = sb("Wp", [128, GROUPS, W])
        bp = sb("bp", [T, W])
        Wr = sb("Wr", [HC + 1, 2, NE])
        We = sb("We", [HC + 1, 2, NE * W])
        W_map_high, W_map_low = (sb(f"W_map_{n}", [128, KC, W], F32R) for n in ("high", "low"))
        Wb_high, Wb_low = (sb(f"Wb_{n}", [HC + 1, 2, 3 * W], F32R) for n in ("high", "low"))
        We_high, We_low = (sb(f"We_{n}", [HC + 1, 2, NE * W], F32R) for n in ("high", "low"))
        clsrow = sb("clsrow", [1, 2, W])
        ident = sb("ident", [128, 128])
        identb = sb("identb", [128, 128], BF16)
        ones = sb("ones", [T, T])
        ones_not0 = sb("ones_not0", [T, T])
        not0 = sb("not0", [T, 1])
        halfneg = sb("halfneg", [T, 2])
        rank = sb("rank", [T, 2, NE])
        dve_scrap = sb("dve_scrap", [1, 2])
        X = sb("X", [T, 2, KD])
        XT = sb("XT", [128, KC, ROWS])
        XT_high, XT_low = (sb(f"XT_{n}", [128, KC, ROWS], F32R) for n in ("high", "low"))
        tok = sb("tok", [T, 2, W])
        rowsum = sb("rowsum", [T, 1])
        negmean = sb("negmean", [T, 1])
        sqs = sb("sqs", [T, 2])
        sqtmp = sb("sqtmp", [T, 2, W])
        varA = sb("varA", [T, 1])
        rstdA = sb("rstdA", [T, 1])
        xn = sb("xn", [T, 2, W])
        xTA = sb("xTA", [HC + 1, 2, ROWS])
        qkA = sb("qkA", [T, 2, 2, W])
        resid = sb("resid", [T, 2, 2, W])
        stackA = sb("stackA", [TP, 2, 2 * HEADS, 6, DH], BF16)
        vA = sb("vA", [T, 2, HEADS, 32])
        tokres = sb("tokres", [T, 2, W])
        stA = sb("stA", [SK + 3, 3, 2, 2, 2 * TP], BF16)
        nm = sb("nm", [T, 2, 4])
        nmr = sb("nmr", [T, 2, 4])
        nms = sb("nms", [TP, 2, 4, 3], BF16)
        PA = sb("PA", [T, 4, 2, 2, 2 * TP])
        zA = sb("zA", [128, 2, 2 * TP])
        rden = sb("rden", [T, GROUPS, 2, 4])
        hm = sb("hm", [T, 2, W])
        H = sb("H", [T, 2, W])
        bnB = sb("bnB", [T, 2, 6])
        mvB = sb("mvB", [T, 2, 2])
        varB = sb("varB", [T, 2])
        rstdB = sb("rstdB", [T, 2])
        scaleB = sb("scaleB", [T, 2])
        x2 = sb("x2", [T, 2, W])
        xTB = sb("xTB", [HC + 1, 2, ROWS])
        xTB_high, xTB_low = (sb(f"xTB_{n}", [HC + 1, 2, ROWS], F32R) for n in ("high", "low"))
        qkB = sb("qkB", [T, 2, 2, W], I16)
        v16 = sb("v16", [T, 2, W], I16)
        stackB = sb("stackB", [TP, 2, 2 * HEADS, 6, DH], BF16)
        vB = sb("vB", [T, 2, HEADS, 32])
        Hres = sb("Hres", [T, 2, W])
        stB = sb("stB", [SK, 2, 2, 2, 2 * TP], BF16)
        S16 = sb("S16", [T, 2, 8 * TP], I16)
        SB = sb("SB", [T, 4, 2, 2, 2 * TP])
        z16 = sb("z16", [128, 2, 2 * TP], I16)
        zB = sb("zB", [128, GROUPS, 2 * TP])
        o32 = sb("o32", [T, 2, W], I32)
        H2 = sb("H2", [T, 2, W])
        H2res = sb("H2res", [T, 2, W])
        xTC_high, xTC_low = (sb(f"xTC_{n}", [HC + 1, 2, ROWS], F32R) for n in ("high", "low"))
        gate = sb("gate", [T, 2, NE])
        bnC = sb("bnC", [T, 2, 6])
        mvC = sb("mvC", [T, 2, 2])
        varC = sb("varC", [T, 2])
        rstdC = sb("rstdC", [T, 2])
        x3 = sb("x3", [T, 2, W])
        xTR = sb("xTR", [HC + 1, 2, ROWS])
        top = sb("top", [T, 2])
        sc = sb("sc", [T, 2, NE])
        pr = sb("pr", [T, 2, NE])
        total = sb("total", [T, 2])
        den = sb("den", [T, 2])
        first = sb("first", [T, 2])
        second = sb("second", [T, 2])
        eq = sb("eq", [T, 2, NE])
        sel1 = sb("sel1", [T, 2, NE])
        rest = sb("rest", [T, 2, NE])
        newgate = sb("newgate", [T, 2, NE])
        acc = sb("acc", [T, 2, W])

        Gt = [ps(f"G{i}", [128, 512]) for i in range(2)]
        St = [ps(f"S{i}", [128, 2, 512]) for i in range(2)]
        Tt = [ps(f"T{i}", [128, 1024], BF16) for i in range(2)]

        act_embed = ["sq0", "sq1", "xT", "xT0", "qk0", "qk1", "hq", "hk", "v0", "v1"]
        act_soft = ["st1", "tok", "p0", "p1", "p2", "p3", "z0", "p4", "z1", "p5", "z2"]
        act_qkv = ["xT", "qk0", "qk1", "v", "kept", "hq", "hk", "vB"]
        act_fixed = ["st0", "s0", "st1", "s1", "st2", "s2", "st3", "z0", "s3", "st4", "H2", "s4", "st5", "z1",
                     "s5", "z2"]
        act_route = ["xT", "exp"]
        dve_embed = ["tok", "negmean", "var", "xn", "resid", "mid", "mid2"]
        dve_qkv = ["bn0", "bn1", "mv0", "mv1", "var", "scale", "x2a", "x2b", "x2", "xT", "mid"]
        dve_soft = ["st0", "mx0", "n1_0", "n2_0", "n3_0", "n4_0"]
        dve_fixed = []
        for p in range(PAIRS):
            dve_soft += [f"nmT{p}"]
            if p + 2 < PAIRS:
                dve_soft += [f"st{p + 2}"]
            if p + 1 < PAIRS:
                dve_soft += [f"mx{p + 1}"] + [f"n{i}_{p + 1}" for i in (1, 2, 3, 4)]
            dve_fixed += {3: ["z0"], 5: ["z1"]}.get(p, []) + ([f"f{p - 1}"] if p else [])
            dve_soft += ["rden0", "hm0"] if p == 5 else []
        dve_soft += ["rden1", "hm1", "rden2", "hm2"]
        dve_fixed += [f"f{PAIRS - 1}", "z2", "o32", "H2"]
        dve_route = ["bn0", "bn1", "mv0", "mv1", "var", "x3a", "x3b", "kept", "top", "sc"]
        gate_steps = ["sum", "rsum", "pr", "p1", "eq1", "key1", "r1", "sel1", "rest", "p2", "eq2", "key2", "r2",
                      "sel2", "sel", "chosen", "den", "den2", "rden", "gate"]
        dve_route += gate_steps[:13] + ["xT"] + gate_steps[13:]
        act_load_done = Steps(sem("act_load_done"), "load", ["xt0", "xh0", "xt1", "xh1", "xt2", "xh2"])
        act_embed_done = Steps(sem("act_embed_done"), "embed", act_embed)
        act_soft_done = Steps(sem("act_soft_done"), "soft", act_soft)
        act_qkv_done = Steps(sem("act_qkv_done"), "qkv", act_qkv)
        act_fixed_done = Steps(sem("act_fixed_done"), "fixed", act_fixed)
        act_route_done = Steps(sem("act_route_done"), "route", act_route)
        dve_embed_done = Steps(sem("dve_embed_done"), "embed", dve_embed)
        dve_soft_done = Steps(sem("dve_soft_done"), "soft", dve_soft)
        dve_qkv_done = Steps(sem("dve_qkv_done"), "qkv", dve_qkv)
        dve_fixed_done = Steps(sem("dve_fixed_done"), "fixed", dve_fixed)
        dve_route_done = Steps(sem("dve_route_done"), "route", dve_route)
        dve_experts_done = Steps(sem("dve_experts_done"), "experts",
                                 ["gate"] + [f"acc{u}{e}" for u in range(NE) for e in range(2)])
        pool_load_done = Steps(sem("pool_load_done"), "load", ["low0", "low1", "low2"])
        pool_embed_done = Steps(sem("pool_embed_done"), "embed", ["rstd", "xw", "x", "low"])
        pool_soft_done = Steps(sem("pool_soft_done"), "soft", ["H", "H0"])
        pool_qkv_done = Steps(sem("pool_qkv_done"), "qkv", ["rstd", "xT", "mid2"])
        pool_route_done = Steps(sem("pool_route_done"), "route", ["rstd", "xT"])
        order = pe_order()
        pe_done = {s: Steps(sem(f"pe_{s}_done"), s, [n for st, n, _ in order if st == s]) for s in STAGES}
        reader = {("load", f"xt{k}"): (act_load_done, f"xt{k}") for k in range(3)}
        reader |= {("embed", "xT"): (act_embed_done, "xT0"), ("embed", "tok"): (dve_embed_done, "tok"),
                   ("embed", "sum"): (dve_embed_done, "negmean"), ("embed", "sq"): (dve_embed_done, "var"),
                   ("embed", "qk0"): (act_embed_done, "qk0"), ("embed", "qk1"): (act_embed_done, "qk1"),
                   ("embed", "v"): (act_embed_done, "v1"), ("route", "xT"): (act_route_done, "xT"),
                   ("route", "rt"): (dve_route_done, "sc"), ("fixed", "out"): (dve_fixed_done, "o32")}
        reader |= {("qkv", n): (act_qkv_done, n) for n in ("xT", "qk0", "qk1", "v")}
        for p in range(PAIRS):
            reader |= {("soft", f"st{p}"): (act_soft_done if p == 1 else dve_soft_done, f"st{p}"), ("soft", f"mx{p}"): (dve_soft_done, f"mx{p}"),
                       ("soft", f"nm{p}"): (dve_soft_done, f"nmT{p}"), ("soft", f"sc{p}"): (act_soft_done, f"p{p}"),
                       ("fixed", f"st{p}"): (act_fixed_done, f"st{p}"),
                       ("fixed", f"sc{p}"): (act_fixed_done, f"s{p}")}
        for g in range(GROUPS):
            reader |= {("soft", f"z{g}"): (act_soft_done, f"z{g}"), ("fixed", f"z{g}"): (act_fixed_done, f"z{g}"),
                       ("soft", f"zt{g}"): (dve_soft_done, f"hm{g}")}
        reader |= {("experts", f"e{u}"): (dve_experts_done, f"acc{u}1") for u in range(NE)}
        x_loaded = sem("x_loaded")
        weights_loaded = sem("weights_loaded")
        consts_made = sem("consts_made")
        quantised = sem("quantised")
        out_stored = sem("out_stored")
        high_parts = sem("high_parts")
        low_parts = sem("low_parts")
        stacks_zeroed = sem("stacks_zeroed")
        LOADS = 13
        QUANTS = 14

        fills = [(X[0:2, 0, :], 0.0), (xTA[HC:HC + 1], 1.0), (xTB[HC:HC + 1], 1.0),
                 (ones[:], 1.0), (ones_not0[:], 1.0), (not0[:], 1.0), (halfneg[:], -0.5),
                 (clsrow[:, 1, :], 0.0), (xTR[HC:HC + 1], 1.0),
                 (vA[:, :, :, DH:32], 0.0), (vB[:], 0.0),
                 (nms[:], 0.0), (stA[SK:SK + 3, :, 1, :, :], 1.0), (ones_not0[0:1, :], 0.0),
                 (not0[0:1, :], 0.0), (vA[:, :, :, DH:DH + 1], 1.0), (vA[0:1, 0, :, DH:DH + 1], 0.0),
                 *((rank[:, :, e:e + 1], float(NE - e)) for e in range(NE))]
        MEMSETS = len(fills) + 1
        fresh = (consts_made, MEMSETS)
        G, S, R = (Banks(k, tiles, reader, fresh) for k, tiles in (("G", Gt), ("S", St), ("T", Tt)))

        block = ctx.enter_context(nc.Block())

        def in_tiles(ap):
            return ap.rearrange("(t p) d -> p t d", p=T)

        def part(stack, slot_q, slot_k):
            a = stack[0:T, 0, :, slot_q, :]
            s_step = stack[:].ap[1][0] + (slot_k - slot_q) * DH
            return bass.AP(a.tensor, a.offset, [a.ap[0], [s_step, 2], a.ap[1], a.ap[2]])

        def all_heads(qk):
            return qk[:].rearrange("p s t (h e) -> p s (t h) e", h=HEADS)

        def high_part(dst, src):
            return nc.vector.tensor_copy(dst, src)

        def low_part(dst, src, high):
            return nc.gpsimd.tensor_tensor(dst, src, high, ALU.subtract)

        def soft_weighted(g):
            return S("soft", f"z{g}")[:, 0, :] if g == 2 else G("soft", f"z{g}")

        def dve_fence(k):
            nc.vector.memset(dve_scrap[:, k:k + 1], 0.0)

        @block.sync
        def _(sp):
            for dst, src in ((W_map[:], wmap), (addend[:], in_tiles(pos)), (base_sb[:], in_tiles(base)),
                             (lnw[:], in_tiles(ln_w)), (lnb[:], in_tiles(ln_b)), (Wa[:], w_a),
                             (Wb[:], w_b), (Wp[:], w_p), (bp[:], b_p), (Wr[:], w_r), (We[:], w_e),
                             (clsrow[:, 0, :], cls), (ident[:], eye)):
                sp.dma_start(dst, src).then_inc(weights_loaded, 16)

            def body(turn):
                if "load" in turn.live:
                    i = turn.image("load")
                    if turn.later("load"):
                        sp.wait_ge(pe_done["load"].sem, pe_done["load"].at(turn, "xt2", back=1))
                    else:
                        sp.wait_ge(consts_made, 1)
                    sp.dma_start(X[2:T, 0, :], x[i, 0:T - 2, :]).then_inc(x_loaded, 16)
                    sp.dma_start(X[0:T, 1, :], x[i, T - 2:2 * T - 2, :]).then_inc(x_loaded, 16)
                if "experts" in turn.live:
                    sp.wait_ge(dve_experts_done.sem, dve_experts_done.at(turn, f"acc{NE - 1}1"))
                    sp.dma_start(in_tiles(out[turn.image("experts")]), acc[:]).then_inc(out_stored, 16)

            run_turns(sp, images, body)
            sp.wait_ge(out_stored, 16 * images)

        @block.tensor
        def _(pe):
            mm = nc.tensor.matmul

            def flip(dst, src, eye_):
                return nc.tensor.matmul(dst, src, eye_, start=True, stop=True, is_transpose=True)

            pe.wait_ge(weights_loaded, 16 * LOADS)
            pe.wait_ge(consts_made, MEMSETS)
            pe.wait_ge(stacks_zeroed, 2)

            def patches_turned(turn, k):
                if k == 0:
                    pe.wait_ge(x_loaded, (turn.image("load") + 1) * 32)
                pe.wait_ge(*G.vacant(turn, "load", f"xt{k}"))
                bank = G("load", f"xt{k}")
                for c in (0, 1):
                    for t in (0, 1):
                        o = c * ROWS + t * T
                        last = flip(bank[:, o:o + T], X[:, t, (2 * k + c) * 128:(2 * k + c + 1) * 128],
                                    ident[0:T, 0:T])
                last.then_inc(pe_done["load"].sem, 1)

            def three_passes(dst, x_high, x_low, w_high, w_low, rows, columns, chunks=2):
                for c in range(chunks):
                    mm(dst, x_high[:, c, rows], w_high[:, c, columns], start=(c == 0), stop=False)
                    mm(dst, x_high[:, c, rows], w_low[:, c, columns], start=False, stop=False)
                    last = mm(dst, x_low[:, c, rows], w_high[:, c, columns], start=False, stop=(c == chunks - 1))
                return last

            def tokens(turn):
                pe.wait_ge(pool_load_done.sem, pool_load_done.at(turn.previous(), "low2"))
                pe.wait_ge(*G.vacant(turn, "embed", "tok"))
                bank = G("embed", "tok")
                for t in (0, 1):
                    last = three_passes(bank[0:T, t * W:(t + 1) * W], XT_high, XT_low, W_map_high, W_map_low,
                                        slice(t * T, (t + 1) * T), slice(0, W), KC)
                last.then_inc(pe_done["embed"].sem, 1)

            def rows_turned(turn, stage, src):
                pe.wait_ge(*G.vacant(turn, stage, "xT"))
                bank = G(stage, "xT")
                for c in (0, 1):
                    for t in (0, 1):
                        o = c * ROWS + t * T
                        last = flip(bank[0:HC, o:o + T], src[:, t, c * HC:(c + 1) * HC], ident[0:T, 0:T])
                last.then_inc(pe_done[stage].sem, 1)

            def sum_over_partitions(turn):
                pe.wait_ge(dve_embed_done.sem, dve_embed_done.at(turn, "tok"))
                pe.wait_ge(*G.vacant(turn, "embed", "sum"))
                mm(G("embed", "sum")[0:T, 0:1], ones[:], rowsum[:], start=True,
                   stop=True).then_inc(pe_done["embed"].sem, 1)

            def squares_over_partitions(turn):
                pe.wait_ge(act_embed_done.sem, act_embed_done.at(turn, "sq1"))
                pe.wait_ge(*G.vacant(turn, "embed", "sq"))
                bank = G("embed", "sq")
                mm(bank[0:T, 0:1], ones_not0[:], sqs[:, 0:1], start=True, stop=False)
                mm(bank[0:T, 0:1], ones[:], sqs[:, 1:2], start=False,
                   stop=True).then_inc(pe_done["embed"].sem, 1)

            def qk_float(turn, t):
                pe.wait_ge(act_embed_done.sem, act_embed_done.at(turn, "xT0"))
                pe.wait_ge(*G.vacant(turn, "embed", f"qk{t}"))
                o = G("embed", f"qk{t}")[0:T, 0:2 * W].rearrange("p (s d) -> p s d", s=2)
                for c in (0, 1):
                    last = mm(o[:, :, c * HC:(c + 1) * HC], xTA[:, c, t * T:(t + 1) * T], Wa[:, c, 0:2, :],
                              start=True, stop=True)
                last.then_inc(pe_done["embed"].sem, 1)

            def v_float(turn):
                pe.wait_ge(*S.vacant(turn, "embed", "v"))
                bank = S("embed", "v")[:, 0, :]
                for t in (0, 1):
                    for c in (0, 1):
                        last = mm(bank[0:T, t * W + c * HC:t * W + (c + 1) * HC],
                                  xTA[:, c, t * T:(t + 1) * T], Wa[:, c, 2, :], start=True, stop=True)
                last.then_inc(pe_done["embed"].sem, 1)

            def fixed_product(bank, t, first, n, at):
                return three_passes(bank[0:T, at:at + n], xTB_high, xTB_low, Wb_high, Wb_low,
                                    slice(t * T, (t + 1) * T), slice(first, first + n))

            def qk_fixed(turn, t):
                pe.wait_ge(pool_qkv_done.sem, pool_qkv_done.at(turn, "xT"))
                pe.wait_ge(*G.vacant(turn, "qkv", f"qk{t}"))
                fixed_product(G("qkv", f"qk{t}"), t, 0, 2 * W, 0).then_inc(pe_done["qkv"].sem, 1)

            def v_fixed(turn):
                pe.wait_ge(*G.vacant(turn, "qkv", "v"))
                fixed_product(G("qkv", "v"), 0, 2 * W, W, 0)
                fixed_product(G("qkv", "v"), 1, 2 * W, W, W).then_inc(pe_done["qkv"].sem, 1)

            def heads_turned(turn, stage, p):
                pe.wait_ge(*R.vacant(turn, stage, f"st{p}"))
                bank = R(stage, f"st{p}")
                for s in (0, 1):
                    for h in (0, 1):
                        for t in (0, 1):
                            o = (s * 4 + h * 2 + t) * TP
                            th = t * HEADS + 2 * p + h
                            src = (stackA if stage == "soft" else stackB)[:, s, th, :, :]
                            last = flip(bank[0:SK, o:o + TP], src.rearrange("r j e -> r (j e)"),
                                        identb[0:TP, 0:TP])
                last.then_inc(pe_done[stage].sem, 1)

            def scores_for_max(turn, p):
                copied = act_soft_done if p == 1 else dve_soft_done
                pe.wait_ge(copied.sem, copied.at(turn, f"st{p}"))
                pe.wait_ge(*S.vacant(turn, "soft", f"mx{p}"))
                for h in (0, 1):
                    keys = stA[0:SK, p % 3, 1, h, :].rearrange("k (t r) -> k t r", t=2)[:, :, 0:T]
                    for t in (0, 1):
                        last = mm(S("soft", f"mx{p}")[0:T, h, t * ROWS:(t + 1) * ROWS],
                                  stA[0:SK, p % 3, 0, h, t * TP:t * TP + T], keys, start=True, stop=True)
                last.then_inc(pe_done["soft"].sem, 1)

            def maxima_turned(turn, p):
                pe.wait_ge(dve_soft_done.sem, dve_soft_done.at(turn, f"n4_{p}"))
                pe.wait_ge(*R.vacant(turn, "soft", f"nm{p}"))
                for n in range(4):
                    last = flip(R("soft", f"nm{p}")[SK:SK + 3, n * TP:(n + 1) * TP], nms[:, p % 2, n, :],
                                identb[0:TP, 0:TP])
                last.then_inc(pe_done["soft"].sem, 1)

            def scores_soft(turn, p):
                pe.wait_ge(dve_soft_done.sem, dve_soft_done.at(turn, f"nmT{p}"))
                pe.wait_ge(*S.vacant(turn, "soft", f"sc{p}"))
                for h in (0, 1):
                    for t in (0, 1):
                        last = mm(S("soft", f"sc{p}")[0:T, h, t * 2 * TP:(t + 1) * 2 * TP],
                                  stA[:, p % 3, 1, h, t * TP:t * TP + T], stA[:, p % 3, 0, h, :],
                                  start=True, stop=True)
                last.then_inc(pe_done["soft"].sem, 1)

            def scores_fixed(turn, p):
                pe.wait_ge(act_fixed_done.sem, act_fixed_done.at(turn, f"st{p}"))
                pe.wait_ge(*S.vacant(turn, "fixed", f"sc{p}"))
                for h in (0, 1):
                    for t in (0, 1):
                        last = mm(S("fixed", f"sc{p}")[0:T, h, t * 2 * TP:(t + 1) * 2 * TP],
                                  stB[:, p % 2, 1, h, t * TP:t * TP + T], stB[:, p % 2, 0, h, :],
                                  start=True, stop=True)
                last.then_inc(pe_done["fixed"].sem, 1)

            def times_v(bank, g, v, weights):
                for j in range(4):
                    for t in (0, 1):
                        last = mm(bank[32 * j:32 * j + 32, 0:2 * TP], v[:, t, 4 * g + j, :],
                                  weights[:, (2 * g + j // 2) % 4, j % 2, t, :], start=(t == 0), stop=(t == 1))
                return last

            def weighted_soft(turn, g):
                pe.wait_ge(act_soft_done.sem, act_soft_done.at(turn, f"p{2 * g + 1}"))
                pe.wait_ge(*(S if g == 2 else G).vacant(turn, "soft", f"z{g}"))
                times_v(soft_weighted(g), g, vA, PA).then_inc(pe_done["soft"].sem, 1)

            def weighted_fixed(turn, g):
                pe.wait_ge(dve_fixed_done.sem, dve_fixed_done.at(turn, f"f{2 * g + 1}"))
                pe.wait_ge(*G.vacant(turn, "fixed", f"z{g}"))
                times_v(G("fixed", f"z{g}"), g, vB, SB).then_inc(pe_done["fixed"].sem, 1)

            def weighted_turned(turn, g):
                pe.wait_ge(act_soft_done.sem, act_soft_done.at(turn, f"z{g}"))
                pe.wait_ge(*G.vacant(turn, "soft", f"zt{g}"))
                for t in (0, 1):
                    last = flip(G("soft", f"zt{g}")[0:T, t * 128:(t + 1) * 128],
                                zA[:, g % 2, t * TP:t * TP + T], ident[:])
                last.then_inc(pe_done["soft"].sem, 1)

            def project(turn):
                pe.wait_ge(dve_fixed_done.sem, dve_fixed_done.at(turn, "z2"))
                pe.wait_ge(*G.vacant(turn, "fixed", "out"))
                for t in (0, 1):
                    for g in range(GROUPS):
                        last = mm(G("fixed", "out")[0:T, t * W:(t + 1) * W], zB[:, g, t * TP:t * TP + T],
                                  Wp[:, g, :], start=(g == 0), stop=(g == GROUPS - 1))
                last.then_inc(pe_done["fixed"].sem, 1)

            def expert_pair(turn, u):
                t, q = u % 2, u // 2
                if u == 0:
                    pe.wait_ge(pool_route_done.sem, pool_route_done.at(turn.previous(), "xT"))
                pe.wait_ge(*G.vacant(turn, "experts", f"e{u}"))
                last = three_passes(G("experts", f"e{u}")[0:T, 0:2 * W], xTC_high, xTC_low, We_high, We_low,
                                    slice(t * T, (t + 1) * T), slice(2 * q * W, (2 * q + 2) * W))
                last.then_inc(pe_done["experts"].sem, 1)

            def router(turn):
                pe.wait_ge(act_route_done.sem, act_route_done.at(turn, "xT"))
                pe.wait_ge(*G.vacant(turn, "route", "rt"))
                for t in (0, 1):
                    for c in (0, 1):
                        last = mm(G("route", "rt")[0:T, t * NE:(t + 1) * NE], xTR[:, c, t * T:(t + 1) * T],
                                  Wr[:, c, :], start=(c == 0), stop=(c == 1))
                last.then_inc(pe_done["route"].sem, 1)

            def body(turn):
                load, embed, soft, qkv, fixed, route, experts = (s in turn.live for s in STAGES)
                for live, stage, split in ((embed, "embed", 1), (qkv, "qkv", 3)):
                    if live and not turn.later(stage):
                        pe.wait_ge(quantised, QUANTS)
                        pe.wait_ge(low_parts, split)
                if fixed:
                    pe.wait_ge(dve_qkv_done.sem, dve_qkv_done.at(turn.previous(), "mid"))
                    pe.wait_ge(pool_qkv_done.sem, pool_qkv_done.at(turn.previous(), "mid2"))
                    heads_turned(turn, "fixed", 0)
                if soft:
                    pe.wait_ge(dve_embed_done.sem, dve_embed_done.at(turn.previous(), "mid2"))
                    pe.wait_ge(pool_embed_done.sem, pool_embed_done.at(turn.previous(), "low"))
                    heads_turned(turn, "soft", 0)
                if experts:
                    expert_pair(turn, 0)
                if soft:
                    heads_turned(turn, "soft", 1)
                    scores_for_max(turn, 0)
                if experts:
                    expert_pair(turn, 1)
                if embed:
                    tokens(turn)
                for p in range(PAIRS):
                    if soft:
                        maxima_turned(turn, p)
                        if p + 2 < PAIRS:
                            heads_turned(turn, "soft", p + 2)
                    if fixed:
                        scores_fixed(turn, p)
                    if p == 0 and qkv:
                        pe.wait_ge(dve_qkv_done.sem, dve_qkv_done.at(turn, "x2"))
                        rows_turned(turn, "qkv", x2)
                    if p in (1, 2) and qkv:
                        qk_fixed(turn, p - 1)
                    if p == 3 and embed:
                        pe.wait_ge(pool_embed_done.sem, pool_embed_done.at(turn, "x"))
                        rows_turned(turn, "embed", xn)
                    if p == 4 and embed:
                        qk_float(turn, 0)
                    if p == 5 and soft:
                        weighted_turned(turn, 0)
                    if p + 1 < PAIRS:
                        if soft:
                            scores_for_max(turn, p + 1)
                        if fixed:
                            heads_turned(turn, "fixed", p + 1)
                    if soft:
                        scores_soft(turn, p)
                    if p == 0:
                        if load:
                            patches_turned(turn, 0)
                        if embed:
                            sum_over_partitions(turn)
                        if experts:
                            expert_pair(turn, 2)
                    if p == 1:
                        if route:
                            pe.wait_ge(dve_route_done.sem, dve_route_done.at(turn, "x3b"))
                            rows_turned(turn, "route", x3)
                        if embed:
                            squares_over_partitions(turn)
                        if experts:
                            expert_pair(turn, 3)
                        if load:
                            patches_turned(turn, 1)
                    if p == 2:
                        if fixed:
                            weighted_fixed(turn, 0)
                        if route:
                            router(turn)
                        if experts:
                            expert_pair(turn, 4)
                    if p == 3:
                        if qkv:
                            v_fixed(turn)
                        if soft:
                            weighted_soft(turn, 0)
                        if experts:
                            expert_pair(turn, 5)
                    if p == 4:
                        if fixed:
                            weighted_fixed(turn, 1)
                        if embed:
                            qk_float(turn, 1)
                        if experts:
                            expert_pair(turn, 6)
                    if p == 5:
                        if soft:
                            weighted_soft(turn, 1)
                        if load:
                            patches_turned(turn, 2)
                        if experts:
                            expert_pair(turn, 7)
                if fixed:
                    weighted_fixed(turn, 2)
                if soft:
                    weighted_soft(turn, 2)
                if soft:
                    weighted_turned(turn, 1)
                if embed:
                    v_float(turn)
                if fixed:
                    project(turn)
                if soft:
                    weighted_turned(turn, 2)

            run_turns(pe, images, body)

        @block.scalar
        def _(act):
            def copy(dst, src, scale=1.0):
                return nc.scalar.activation(dst, src, ACT.Copy, scale=scale)

            act.wait_ge(weights_loaded, 16 * LOADS)
            act.wait_ge(consts_made, MEMSETS)
            act.wait_ge(stacks_zeroed, 2)

            def patches_kept(turn, k):
                act.wait_ge(pe_done["load"].sem, pe_done["load"].at(turn, f"xt{k}"))
                if turn.later("load"):
                    act.wait_ge(pool_load_done.sem, pool_load_done.at(turn, f"low{k}", back=1))
                copy(XT[:, 2 * k:2 * k + 2, :],
                     G("load", f"xt{k}")[:, 0:2 * ROWS].rearrange("p (c r) -> p c r", c=2))\
                    .then_inc(act_load_done.sem, 1)

            def patches_high(turn, k):
                act.wait_ge(act_load_done.sem, act_load_done.at(turn, f"xt{k}"))
                copy(XT_high[:, 2 * k:2 * k + 2, :], XT[:, 2 * k:2 * k + 2, :]).then_inc(act_load_done.sem, 1)

            def operand_copied(turn, stage, p, dst, steps):
                act.wait_ge(pe_done[stage].sem, pe_done[stage].at(turn, f"st{p}"))
                copy(dst.rearrange("p s h r -> p (s h r)"), R(stage, f"st{p}")[0:SK, 0:8 * TP])\
                    .then_inc(steps.sem, 1)

            def turned(stage):
                return G(stage, "xT")[0:HC, 0:2 * ROWS].rearrange("p (c r) -> p c r", c=2)

            def rounded_scores(turn, p):
                act.wait_ge(pe_done["fixed"].sem, pe_done["fixed"].at(turn, f"sc{p}"))
                if p >= 2:
                    act.wait_ge(dve_fixed_done.sem, dve_fixed_done.at(turn, f"f{p - 2}"))
                copy(S16[:, p % 2, :].rearrange("p (h r) -> p h r", h=2),
                     S("fixed", f"sc{p}")[0:T, :, 0:4 * TP], scale=2.0 ** -8).then_inc(act_fixed_done.sem, 1)

            def exponentials(turn, p):
                act.wait_ge(pe_done["soft"].sem, pe_done["soft"].at(turn, f"sc{p}"))
                if p in (0, 1) and turn.later("soft"):
                    act.wait_ge(pe_done["soft"].sem, pe_done["soft"].at(turn, "z2", back=1))
                if p >= 4:
                    act.wait_ge(pe_done["soft"].sem, pe_done["soft"].at(turn, "z0"))
                nc.scalar.activation(PA[:, p % 4, :, :, :].rearrange("p h c r -> p h (c r)"),
                                     S("soft", f"sc{p}")[0:T, :, 0:4 * TP], ACT.Exp,
                                     scale=DH ** -0.5).then_inc(act_soft_done.sem, 1)

            def weighted_rounded(turn, g):
                act.wait_ge(pe_done["fixed"].sem, pe_done["fixed"].at(turn, f"z{g}"))
                if g == 2:
                    act.wait_ge(dve_fixed_done.sem, dve_fixed_done.at(turn, "z0"))
                copy(z16[:, g % 2, :], G("fixed", f"z{g}")[:, 0:2 * TP],
                     scale=2.0 ** -8).then_inc(act_fixed_done.sem, 1)

            def weighted_kept(turn, g):
                act.wait_ge(pe_done["soft"].sem, pe_done["soft"].at(turn, f"z{g}"))
                copy(zA[:, g % 2, :], soft_weighted(g)[:, 0:2 * TP]).then_inc(act_soft_done.sem, 1)

            def qk_fixed_rounded(turn, t):
                act.wait_ge(pe_done["qkv"].sem, pe_done["qkv"].at(turn, f"qk{t}"))
                if t == 0 and turn.later("qkv"):
                    act.wait_ge(dve_qkv_done.sem, dve_qkv_done.at(turn, "mid", back=1))
                copy(qkB[:, :, t, :], G("qkv", f"qk{t}")[0:T, 0:2 * W].rearrange("p (s d) -> p s d", s=2),
                     scale=2.0 ** -16).then_inc(act_qkv_done.sem, 1)

            def float_high_part(turn, s):
                act.wait_ge(act_embed_done.sem, act_embed_done.at(turn, "qk1"))
                if turn.later("embed"):
                    act.wait_ge(pe_done["soft"].sem, pe_done["soft"].at(turn, "st5"))
                slots = slice(1, 6, 2) if s else slice(0, 3)
                copy(stackA[0:T, s, :, slots, :],
                     all_heads(qkA)[:, s, :, :].unsqueeze(2).to_broadcast([T, 2 * HEADS, 3, DH]))\
                    .then_inc(act_embed_done.sem, 1)

            def fixed_high_part(turn, s):
                act.wait_ge(act_qkv_done.sem, act_qkv_done.at(turn, "qk1"))
                if turn.later("qkv"):
                    act.wait_ge(pe_done["fixed"].sem, pe_done["fixed"].at(turn, "st5"))
                slots = slice(0, 3, 2) if s else slice(0, 2)
                copy(stackB[0:T, s, :, slots, :],
                     all_heads(qkB)[:, s, :, :].unsqueeze(2).to_broadcast([T, 2 * HEADS, 2, DH]))\
                    .then_inc(act_qkv_done.sem, 1)

            def qk_kept(turn, t):
                act.wait_ge(pe_done["embed"].sem, pe_done["embed"].at(turn, f"qk{t}"))
                if t == 0 and turn.later("embed"):
                    act.wait_ge(dve_embed_done.sem, dve_embed_done.at(turn, "resid", back=1))
                copy(qkA[:, :, t, :], G("embed", f"qk{t}")[0:T, 0:2 * W].rearrange("p (s d) -> p s d", s=2))\
                    .then_inc(act_embed_done.sem, 1)

            def body(turn):
                load, embed, soft, qkv, fixed, route, experts = (s in turn.live for s in STAGES)
                if fixed:
                    operand_copied(turn, "fixed", 0, stB[0:SK, 0], act_fixed_done)
                if soft:
                    operand_copied(turn, "soft", 1, stA[0:SK, 1], act_soft_done)
                    if turn.later("soft"):
                        act.wait_ge(pool_soft_done.sem, pool_soft_done.at(turn, "H0", back=1))
                    act.wait_ge(dve_embed_done.sem, dve_embed_done.at(turn.previous(), "tok"))
                    copy(tokres[:], tok[:]).then_inc(act_soft_done.sem, 1)
                for p in range(PAIRS):
                    if fixed:
                        rounded_scores(turn, p)
                    if p == 0 and qkv:
                        act.wait_ge(pe_done["qkv"].sem, pe_done["qkv"].at(turn, "xT"))
                        copy(xTB[0:HC, :, :], turned("qkv")).then_inc(act_qkv_done.sem, 1)
                    if p in (1, 2) and qkv:
                        qk_fixed_rounded(turn, p - 1)
                    if p == 3:
                        if route:
                            if turn.later("route"):
                                act.wait_ge(dve_route_done.sem, dve_route_done.at(turn, "gate", back=1))
                            act.wait_ge(dve_route_done.sem, dve_route_done.at(turn, "sc"))
                            nc.scalar.activation(pr[:], sc[:], ACT.Exp).then_inc(act_route_done.sem, 1)
                        if embed:
                            act.wait_ge(pe_done["embed"].sem, pe_done["embed"].at(turn, "xT"))
                            copy(xTA[0:HC, :, 1:ROWS], turned("embed")[:, :, 1:ROWS])\
                                .then_inc(act_embed_done.sem, 1)
                            copy(xTA[0:HC, :, 0:1], turned("embed")[:, :, 1:2]).then_inc(act_embed_done.sem, 1)
                    if p == 4 and embed:
                        qk_kept(turn, 0)
                    if p + 1 < PAIRS and fixed:
                        operand_copied(turn, "fixed", p + 1, stB[0:SK, (p + 1) % 2], act_fixed_done)
                    if p == 0 and load:
                        patches_kept(turn, 0)
                    if p == 1 and route:
                        if turn.later("route"):
                            act.wait_ge(pool_route_done.sem, pool_route_done.at(turn, "xT", back=1))
                        act.wait_ge(pe_done["route"].sem, pe_done["route"].at(turn, "xT"))
                        copy(xTR[0:HC, :, :], turned("route")).then_inc(act_route_done.sem, 1)
                    if soft:
                        if p == 5:
                            weighted_kept(turn, 1)
                        exponentials(turn, p)
                    if p == 0:
                        if embed:
                            act.wait_ge(dve_embed_done.sem, dve_embed_done.at(turn, "negmean"))
                            for t in (0, 1):
                                nc.scalar.activation(sqtmp[:, t, :], tok[:, t, :], ACT.Square, bias=negmean[:],
                                                     accum_out=sqs[:, t:t + 1]).then_inc(act_embed_done.sem, 1)
                    if p == 1:
                        if load:
                            patches_high(turn, 0)
                            patches_kept(turn, 1)
                    if p == 2:
                        if fixed:
                            weighted_rounded(turn, 0)
                        if load:
                            patches_high(turn, 1)
                    if p == 3:
                        if qkv:
                            act.wait_ge(pe_done["qkv"].sem, pe_done["qkv"].at(turn, "v"))
                            if turn.later("qkv"):
                                act.wait_ge(act_qkv_done.sem, act_qkv_done.at(turn, "vB", back=1))
                            copy(v16[:], G("qkv", "v")[0:T, 0:2 * W].rearrange("p (t d) -> p t d", t=2),
                                 scale=2.0 ** -16).then_inc(act_qkv_done.sem, 1)
                        if soft:
                            weighted_kept(turn, 0)
                        if fixed:
                            if route:
                                act.wait_ge(dve_route_done.sem, dve_route_done.at(turn, "kept"))
                            act.wait_ge(act_qkv_done.sem, act_qkv_done.at(turn.previous(), "kept"))
                            copy(H2[:], Hres[:]).then_inc(act_fixed_done.sem, 1)
                        if qkv:
                            if fixed:
                                act.wait_ge(act_fixed_done.sem, act_fixed_done.at(turn, "H2"))
                            act.wait_ge(pool_soft_done.sem, pool_soft_done.at(turn.previous(), "H0"))
                            copy(Hres[:], H[:]).then_inc(act_qkv_done.sem, 1)
                    if p == 4:
                        if fixed:
                            weighted_rounded(turn, 1)
                        if embed:
                            qk_kept(turn, 1)
                        if embed:
                            float_high_part(turn, 0)
                            float_high_part(turn, 1)
                if load:
                    patches_kept(turn, 2)
                if qkv:
                    fixed_high_part(turn, 0)
                    fixed_high_part(turn, 1)
                if fixed:
                    weighted_rounded(turn, 2)
                if soft:
                    weighted_kept(turn, 2)
                if embed:
                    act.wait_ge(pe_done["embed"].sem, pe_done["embed"].at(turn, "v"))
                    for t in (0, 1):
                        copy(vA[:, t, :, 0:DH],
                             S("embed", "v")[0:T, 0, t * W:(t + 1) * W].rearrange("p (h e) -> p h e", h=HEADS),
                             scale=(1.0 if t else not0[:])).then_inc(act_embed_done.sem, 1)
                if load:
                    patches_high(turn, 2)
                if qkv:
                    if fixed:
                        act.wait_ge(pe_done["fixed"].sem, pe_done["fixed"].at(turn, "z2"))
                    act.wait_ge(act_qkv_done.sem, act_qkv_done.at(turn, "v"))
                    copy(vB[:, :, :, 0:DH], v16[:].rearrange("p t (h e) -> p t h e", h=HEADS))\
                        .then_inc(act_qkv_done.sem, 1)

            run_turns(act, images, body)

        @block.vector
        def _(dve):
            v = nc.vector
            for stack in (stackA, stackB):
                v.memset(stack[:], 0.0).then_inc(stacks_zeroed, 1)
            dve.wait_ge(stacks_zeroed, 2)
            dve.wait_ge(weights_loaded, 16 * LOADS)
            v.tensor_tensor(addend[:], addend[:], base_sb[:], ALU.add).then_inc(quantised, 1)
            high_part(W_map_high[:], W_map[:]).then_inc(high_parts, 1)
            done = 1
            for w, bias_scale in ((Wb[0:HC, :, :], 1.0), (Wb[HC:HC + 1, :, :], 2.0 ** 16), (Wp[:], 1.0),
                                  (bp[:], 1.0)):
                v.tensor_scalar(w, w, 256.0, I16MAX, ALU.mult, ALU.min).then_inc(quantised, 1)
                done += 1
                dve.wait_ge(quantised, done)
                v.tensor_scalar(w, w, I16MIN, ROUND, ALU.max, ALU.add).then_inc(quantised, 1)
                done += 1
                dve.wait_ge(quantised, done)
                v.tensor_scalar(w, w, ROUND, bias_scale, ALU.subtract, ALU.mult).then_inc(quantised, 1)
                done += 1
            v.memset(acc[:], 0.0).then_inc(quantised, 1)
            dve.wait_ge(quantised, QUANTS)
            high_part(Wb_high[:], Wb[:]).then_inc(high_parts, 1)
            high_part(We_high[:], We[:]).then_inc(high_parts, 1)
            dve.wait_ge(consts_made, MEMSETS)

            def rows_read(rows, bn, steps):
                for t in (0, 1):
                    v.bn_stats(bn[:, t, :], rows[:, t, :]).then_inc(steps.sem, 1)

            def norm_stats(turn, bn, mv, var, steps):
                dve.wait_ge(steps.sem, steps.at(turn, "bn1"))
                dve_fence(0 if steps is dve_qkv_done else 1)
                for t in (0, 1):
                    v.bn_aggr(mv[:, t, :], bn[:, t, :]).then_inc(steps.sem, 1)
                dve.wait_ge(steps.sem, steps.at(turn, "mv1"))
                v.tensor_scalar(var[:], mv[:, :, 1], EPS, None, ALU.add).then_inc(steps.sem, 1)

            def operand_copied(turn, p):
                dve.wait_ge(pe_done["soft"].sem, pe_done["soft"].at(turn, f"st{p}"))
                v.tensor_copy(stA[0:SK, p % 3, :, :, :].rearrange("p s h r -> p (s h r)"),
                              R("soft", f"st{p}")[0:SK, 0:8 * TP]).then_inc(dve_soft_done.sem, 1)

            def float_scores(turn, p):
                dve.wait_ge(act_fixed_done.sem, act_fixed_done.at(turn, f"s{p}"))
                if p < 2 and turn.later("fixed"):
                    dve.wait_ge(pe_done["fixed"].sem, pe_done["fixed"].at(turn, "z2", back=1))
                if p >= 4:
                    dve.wait_ge(pe_done["fixed"].sem, pe_done["fixed"].at(turn, "z0"))
                v.tensor_copy(SB[:, p % 4, :, :, :].rearrange("p h c r -> p (h c r)"), S16[:, p % 2, :])\
                    .then_inc(dve_fixed_done.sem, 1)

            def float_weighted(turn, g):
                dve.wait_ge(act_fixed_done.sem, act_fixed_done.at(turn, f"z{g}"))
                v.tensor_copy(zB[:, g, :], z16[:, g % 2, :]).then_inc(dve_fixed_done.sem, 1)

            def row_maxima(turn, p):
                soft, slot = "soft" in turn.live, 4 * (p - 4)
                high, middle, low = (nms[0:T, p % 2, :, i] for i in range(3))
                if soft:
                    dve.wait_ge(pe_done["soft"].sem, pe_done["soft"].at(turn, f"mx{p}"))
                    v.tensor_reduce(nm[:, p % 2, :].rearrange("p (h t) -> p h t", h=2),
                                    S("soft", f"mx{p}")[0:T, :, 0:2 * ROWS].rearrange("p h (t r) -> p h t r", t=2),
                                    AX.X, ALU.max, negate=True).then_inc(dve_soft_done.sem, 1)
                if p >= 4:
                    gate_steps_here(turn, slot)
                if soft:
                    dve.wait_ge(dve_soft_done.sem, dve_soft_done.at(turn, f"mx{p}"))
                    v.tensor_copy(high, nm[:, p % 2, :]).then_inc(dve_soft_done.sem, 1)
                if p >= 4:
                    gate_steps_here(turn, slot + 1)
                if soft:
                    dve.wait_ge(dve_soft_done.sem, dve_soft_done.at(turn, f"n1_{p}"))
                    v.tensor_tensor(nmr[:, p % 2, :], nm[:, p % 2, :], high, ALU.subtract)\
                        .then_inc(dve_soft_done.sem, 1)
                if p >= 4:
                    gate_steps_here(turn, slot + 2)
                if soft:
                    dve.wait_ge(dve_soft_done.sem, dve_soft_done.at(turn, f"n2_{p}"))
                    v.tensor_copy(middle, nmr[:, p % 2, :]).then_inc(dve_soft_done.sem, 1)
                if p >= 4:
                    gate_steps_here(turn, slot + 3)
                if soft:
                    dve.wait_ge(dve_soft_done.sem, dve_soft_done.at(turn, f"n3_{p}"))
                    v.tensor_tensor(low, nmr[:, p % 2, :], middle, ALU.subtract).then_inc(dve_soft_done.sem, 1)

            def softmax_rows(turn, g):
                dve.wait_ge(pe_done["soft"].sem, pe_done["soft"].at(turn, f"zt{g}"))
                w = G("soft", f"zt{g}")[0:T, 0:256].rearrange("p (t j e) -> p t j e", t=2, j=4)
                v.reciprocal(rden[:, g, :, :], w[:, :, :, DH]).then_inc(dve_soft_done.sem, 1)
                dve.wait_ge(dve_soft_done.sem, dve_soft_done.at(turn, f"rden{g}"))
                v.tensor_tensor(hm[:, :, g * 64:(g + 1) * 64].rearrange("p t (j e) -> p t j e", j=4),
                                w[:, :, :, 0:DH], rden[:, g, :, :].unsqueeze(3).to_broadcast([T, 2, 4, DH]), ALU.mult)\
                    .then_inc(dve_soft_done.sem, 1)

            def experts_added(turn, u):
                dve.wait_ge(pe_done["experts"].sem, pe_done["experts"].at(turn, f"e{u}"))
                t, q = u % 2, u // 2
                for e in (0, 1):
                    if q or e:
                        dve.wait_ge(dve_experts_done.sem, dve_experts_done.at(turn, f"acc{u}0" if e else f"acc{u - 2}1"))
                    before = acc if q or e else H2res
                    v.scalar_tensor_tensor(acc[:, t, :], G("experts", f"e{u}")[0:T, e * W:(e + 1) * W],
                                           gate[:, t, 2 * q + e:2 * q + e + 1], before[:, t, :],
                                           ALU.mult, ALU.add).then_inc(dve_experts_done.sem, 1)

            def per_expert(ap):
                return ap[:].unsqueeze(2).to_broadcast([T, 2, NE])

            def router_read(turn):
                logits = G("route", "rt")[0:T, 0:2 * NE].rearrange("p (t e) -> p t e", t=2)
                dve.wait_ge(pe_done["route"].sem, pe_done["route"].at(turn, "rt"))
                v.tensor_reduce(top[:], logits, AX.X, ALU.max, negate=True).then_inc(dve_route_done.sem, 1)
                dve.wait_ge(dve_route_done.sem, dve_route_done.at(turn, "top"))
                if turn.later("route"):
                    dve.wait_ge(act_route_done.sem, act_route_done.at(turn, "exp", back=1))
                v.tensor_tensor(sc[:], logits, top[:].unsqueeze(2).to_broadcast([T, 2, NE]), ALU.add)\
                    .then_inc(dve_route_done.sem, 1)

            def per_expert(ap):
                return ap[:].unsqueeze(2).to_broadcast([T, 2, NE])

            def gate_step(turn, k):
                if k == 0:
                    dve.wait_ge(act_route_done.sem, act_route_done.at(turn, "exp"))
                    v.tensor_reduce(total[:], pr[:], AX.X, ALU.add).then_inc(dve_route_done.sem, 1)
                    return
                dve.wait_ge(dve_route_done.sem, dve_route_done.at(turn, gate_steps[k - 1]))
                if k == 1:
                    v.reciprocal(total[:], total[:]).then_inc(dve_route_done.sem, 1)
                if k == 2:
                    v.tensor_tensor(pr[:], pr[:], per_expert(total), ALU.mult).then_inc(dve_route_done.sem, 1)
                if k == 3:
                    v.tensor_reduce(first[:], pr[:], AX.X, ALU.max).then_inc(dve_route_done.sem, 1)
                if k == 4:
                    v.tensor_tensor(eq[:], pr[:], per_expert(first), ALU.is_equal).then_inc(dve_route_done.sem, 1)
                if k == 5:
                    v.tensor_tensor(eq[:], eq[:], rank[:], ALU.mult).then_inc(dve_route_done.sem, 1)
                if k == 6:
                    v.tensor_reduce(total[:], eq[:], AX.X, ALU.max).then_inc(dve_route_done.sem, 1)
                if k == 7:
                    v.tensor_tensor(sel1[:], eq[:], per_expert(total), ALU.is_equal).then_inc(dve_route_done.sem, 1)
                if k == 8:
                    v.scalar_tensor_tensor(rest[:], sel1[:], -2.0, pr[:], ALU.mult, ALU.add)\
                        .then_inc(dve_route_done.sem, 1)
                if k == 9:
                    v.tensor_reduce(second[:], rest[:], AX.X, ALU.max).then_inc(dve_route_done.sem, 1)
                if k == 10:
                    v.tensor_tensor(eq[:], rest[:], per_expert(second), ALU.is_equal).then_inc(dve_route_done.sem, 1)
                if k == 11:
                    v.tensor_tensor(eq[:], eq[:], rank[:], ALU.mult).then_inc(dve_route_done.sem, 1)
                if k == 12:
                    v.tensor_reduce(total[:], eq[:], AX.X, ALU.max).then_inc(dve_route_done.sem, 1)
                if k == 13:
                    v.tensor_tensor(eq[:], eq[:], per_expert(total), ALU.is_equal).then_inc(dve_route_done.sem, 1)
                if k == 14:
                    v.tensor_tensor(sel1[:], sel1[:], eq[:], ALU.add).then_inc(dve_route_done.sem, 1)
                if k == 15:
                    v.tensor_tensor(sel1[:], sel1[:], pr[:], ALU.mult).then_inc(dve_route_done.sem, 1)
                if k == 16:
                    v.tensor_tensor(den[:], first[:], second[:], ALU.add).then_inc(dve_route_done.sem, 1)
                if k == 17:
                    v.tensor_scalar(den[:], den[:], 1e-9, None, ALU.add).then_inc(dve_route_done.sem, 1)
                if k == 18:
                    v.reciprocal(den[:], den[:]).then_inc(dve_route_done.sem, 1)
                if k == 19:
                    v.tensor_tensor(newgate[:], sel1[:], per_expert(den), ALU.mult).then_inc(dve_route_done.sem, 1)

            def gate_steps_here(turn, *steps):
                if "route" in turn.live:
                    for k in steps:
                        gate_step(turn, k)

            def body(turn):
                load, embed, soft, qkv, fixed, route, experts = (s in turn.live for s in STAGES)
                if soft:
                    operand_copied(turn, 0)
                if experts:
                    if turn.later("experts"):
                        dve.wait_ge(out_stored, 16 * turn.image("experts"))
                    dve.wait_ge(dve_route_done.sem, dve_route_done.at(turn.previous(), "gate"))
                    v.tensor_copy(gate[:], newgate[:]).then_inc(dve_experts_done.sem, 1)
                    dve.wait_ge(dve_experts_done.sem, dve_experts_done.at(turn, "gate"))
                    experts_added(turn, 0)
                if soft:
                    row_maxima(turn, 0)
                if qkv:
                    dve.wait_ge(pool_soft_done.sem, pool_soft_done.at(turn.previous(), "H0"))
                    rows_read(H, bnB, dve_qkv_done)
                    norm_stats(turn, bnB, mvB, varB, dve_qkv_done)
                if experts:
                    experts_added(turn, 1)
                if qkv:
                    dve.wait_ge(pool_qkv_done.sem, pool_qkv_done.at(turn, "rstd"))
                    v.tensor_scalar(scaleB[:], rstdB[:], 2.0 ** 16, None, ALU.mult)\
                        .then_inc(dve_qkv_done.sem, 1)
                    dve.wait_ge(dve_qkv_done.sem, dve_qkv_done.at(turn, "scale"))
                    for t in (0, 1):
                        v.tensor_scalar(x2[:, t, :], H[:, t, :], mvB[:, t, 0:1], scaleB[:, t:t + 1],
                                        ALU.subtract, ALU.mult).then_inc(dve_qkv_done.sem, 1)
                    dve.wait_ge(dve_qkv_done.sem, dve_qkv_done.at(turn, "x2b"))
                    v.tensor_scalar(x2[:], x2[:], ROUND, ROUND, ALU.add, ALU.subtract)\
                        .then_inc(dve_qkv_done.sem, 1)
                for p in range(PAIRS):
                    if p == 2 and experts:
                        experts_added(turn, 3)
                    if soft:
                        dve.wait_ge(pe_done["soft"].sem, pe_done["soft"].at(turn, f"nm{p}"))
                        v.tensor_copy(stA[SK:SK + 3, p % 3, 0, :, :].rearrange("p h r -> p (h r)"),
                                      R("soft", f"nm{p}")[SK:SK + 3, 0:4 * TP]).then_inc(dve_soft_done.sem, 1)
                    if p == 1 and route:
                        norm_stats(turn, bnC, mvC, varC, dve_route_done)
                    if p in (1, 5) and experts:
                        experts_added(turn, 2 if p == 1 else 6)
                    if p == 1 and route:
                        dve.wait_ge(pool_route_done.sem, pool_route_done.at(turn, "rstd"))
                        for t in (0, 1):
                            v.tensor_scalar(x3[:, t, :], H2[:, t, :], mvC[:, t, 0:1], rstdC[:, t:t + 1],
                                            ALU.subtract, ALU.mult).then_inc(dve_route_done.sem, 1)
                    if p in (3, 4) and experts:
                        experts_added(turn, p + 1)
                    if soft and p + 2 < PAIRS:
                        operand_copied(turn, p + 2)
                    if p == 0 and embed:
                        dve.wait_ge(pe_done["embed"].sem, pe_done["embed"].at(turn, "tok"))
                        if soft:
                            dve.wait_ge(act_soft_done.sem, act_soft_done.at(turn, "tok"))
                        v.scalar_tensor_tensor(tok[:].rearrange("p t d -> p (t d)"), G("embed", "tok")[0:T, 0:2 * W],
                                               0.0, addend[:].rearrange("p t d -> p (t d)"), ALU.add, ALU.add,
                                               accum_out=rowsum[:]).then_inc(dve_embed_done.sem, 1)
                    if p == 0 and qkv:
                        dve.wait_ge(act_qkv_done.sem, act_qkv_done.at(turn, "xT"))
                        high_part(xTB_high[:], xTB[:]).then_inc(dve_qkv_done.sem, 1)
                    if p == 3 and fixed:
                        float_weighted(turn, 0)
                    if p == 5:
                        gate_steps_here(turn, 8)
                        if soft:
                            softmax_rows(turn, 0)
                        gate_steps_here(turn, 9)
                        if fixed:
                            float_weighted(turn, 1)
                        gate_steps_here(turn, 10)
                    if p == 2 and embed:
                        dve.wait_ge(pool_embed_done.sem, pool_embed_done.at(turn, "rstd"))
                        v.tensor_scalar(xn[:], tok[:], negmean[:], rstdA[:], ALU.add, ALU.mult)\
                            .then_inc(dve_embed_done.sem, 1)
                    if fixed and p > 0:
                        float_scores(turn, p - 1)
                    if p == 2 and route:
                        v.tensor_copy(H2res[:], H2[:]).then_inc(dve_route_done.sem, 1)
                    if p + 1 < PAIRS:
                        row_maxima(turn, p + 1)
                    if p == 1 and embed:
                        dve.wait_ge(pe_done["embed"].sem, pe_done["embed"].at(turn, "sq"))
                        v.tensor_scalar(varA[:], G("embed", "sq")[0:T, 0:1], 1.0 / NTOK, EPS, ALU.mult, ALU.add)\
                            .then_inc(dve_embed_done.sem, 1)
                    if p == 2 and route:
                        router_read(turn)
                    if p == 0 and embed:
                        dve.wait_ge(pe_done["embed"].sem, pe_done["embed"].at(turn, "sum"))
                        v.tensor_scalar(negmean[:], G("embed", "sum")[0:T, 0:1], -1.0 / NTOK, None, ALU.mult)\
                            .then_inc(dve_embed_done.sem, 1)
                    if p == 0 and route:
                        dve.wait_ge(dve_fixed_done.sem, dve_fixed_done.at(turn.previous(), "H2"))
                        rows_read(H2, bnC, dve_route_done)
                gate_steps_here(turn, 11)
                if fixed:
                    float_scores(turn, PAIRS - 1)
                if embed:
                    dve.wait_ge(act_embed_done.sem, act_embed_done.at(turn, "hk"))
                    v.tensor_tensor(all_heads(resid), all_heads(qkA), part(stackA, 1, 1), ALU.subtract)\
                        .then_inc(dve_embed_done.sem, 1)
                gate_steps_here(turn, 12)
                if embed:
                    dve.wait_ge(dve_embed_done.sem, dve_embed_done.at(turn, "resid"))
                    v.tensor_copy(part(stackA, 4, 4), all_heads(resid)).then_inc(dve_embed_done.sem, 1)
                if experts:
                    experts_added(turn, 7)
                if embed:
                    v.tensor_copy(part(stackA, 3, 2), all_heads(resid)).then_inc(dve_embed_done.sem, 1)
                if route:
                    if experts:
                        dve.wait_ge(pe_done["experts"].sem, pe_done["experts"].at(turn, "e7"))
                    dve.wait_ge(act_route_done.sem, act_route_done.at(turn, "xT"))
                    high_part(xTC_high[:], xTR[:]).then_inc(dve_route_done.sem, 1)
                gate_steps_here(turn, 13)
                if fixed:
                    float_weighted(turn, 2)
                gate_steps_here(turn, 14)
                if qkv:
                    dve.wait_ge(act_qkv_done.sem, act_qkv_done.at(turn, "hk"))
                    v.tensor_tensor(part(stackB, 2, 1), all_heads(qkB), part(stackB, 0, 0), ALU.subtract)\
                        .then_inc(dve_qkv_done.sem, 1)
                gate_steps_here(turn, 15)
                if soft:
                    softmax_rows(turn, 1)
                gate_steps_here(turn, 16)
                gate_steps_here(turn, 17)
                gate_steps_here(turn, 18)
                gate_steps_here(turn, 19)
                if fixed:
                    dve.wait_ge(pe_done["fixed"].sem, pe_done["fixed"].at(turn, "out"))
                    v.scalar_tensor_tensor(o32[:], G("fixed", "out")[0:T, 0:2 * W].rearrange("p (t d) -> p t d", t=2),
                                           2.0 ** -8, bp[:].unsqueeze(1).to_broadcast([T, 2, W]),
                                           ALU.mult, ALU.add).then_inc(dve_fixed_done.sem, 1)
                    dve.wait_ge(dve_fixed_done.sem, dve_fixed_done.at(turn, "o32"))
                    dve.wait_ge(act_fixed_done.sem, act_fixed_done.at(turn, "H2"))
                    v.scalar_tensor_tensor(H2[:], o32[:], 2.0 ** -8, H2[:], ALU.mult, ALU.add)\
                        .then_inc(dve_fixed_done.sem, 1)
                if soft:
                    softmax_rows(turn, 2)

            run_turns(dve, images, body)

        @block.gpsimd
        def _(pool):
            q = nc.gpsimd
            for made, (ap, value) in enumerate(fills):
                q.memset(ap, value).then_inc(consts_made, 1)
                pool.wait_ge(consts_made, made + 1)
            pool.wait_ge(weights_loaded, 16 * LOADS)
            q.tensor_copy(identb[:], ident[:]).then_inc(consts_made, 1)
            pool.wait_ge(consts_made, MEMSETS)
            pool.wait_ge(stacks_zeroed, 2)
            pool.wait_ge(high_parts, 1)
            low_part(W_map_low[:], W_map[:], W_map_high[:]).then_inc(low_parts, 1)

            def patches_low(turn, k):
                pool.wait_ge(act_load_done.sem, act_load_done.at(turn, f"xh{k}"))
                chunks = slice(2 * k, 2 * k + 2)
                low_part(XT_low[:, chunks, :], XT[:, chunks, :], XT_high[:, chunks, :])\
                    .then_inc(pool_load_done.sem, 1)

            def body(turn):
                load, embed, soft, qkv, fixed, route, experts = (s in turn.live for s in STAGES)
                if embed and not turn.later("embed"):
                    pool.wait_ge(high_parts, 3)
                    low_part(Wb_low[:], Wb[:], Wb_high[:]).then_inc(low_parts, 1)
                    low_part(We_low[:], We[:], We_high[:]).then_inc(low_parts, 1)
                if qkv:
                    pool.wait_ge(dve_qkv_done.sem, dve_qkv_done.at(turn, "var"))
                    q.tensor_tensor(rstdB[:], varB[:], halfneg[:], ALU.pow).then_inc(pool_qkv_done.sem, 1)
                if qkv:
                    pool.wait_ge(dve_qkv_done.sem, dve_qkv_done.at(turn, "xT"))
                    low_part(xTB_low[:], xTB[:], xTB_high[:]).then_inc(pool_qkv_done.sem, 1)
                if route:
                    pool.wait_ge(dve_route_done.sem, dve_route_done.at(turn, "var"))
                    q.tensor_tensor(rstdC[:], varC[:], halfneg[:], ALU.pow).then_inc(pool_route_done.sem, 1)
                if embed:
                    pool.wait_ge(dve_embed_done.sem, dve_embed_done.at(turn, "var"))
                    q.tensor_tensor(rstdA[:], varA[:], halfneg[:, 0:1], ALU.pow).then_inc(pool_embed_done.sem, 1)
                    pool.wait_ge(dve_embed_done.sem, dve_embed_done.at(turn, "xn"))
                    q.tensor_tensor(xn[:], xn[:], lnw[:], ALU.mult).then_inc(pool_embed_done.sem, 1)
                    pool.wait_ge(pool_embed_done.sem, pool_embed_done.at(turn, "xw"))
                    q.tensor_tensor(xn[:], xn[:], lnb[:], ALU.add).then_inc(pool_embed_done.sem, 1)
                if load:
                    patches_low(turn, 0)
                if load:
                    patches_low(turn, 1)
                if embed:
                    pool.wait_ge(dve_embed_done.sem, dve_embed_done.at(turn, "mid"))
                    q.tensor_tensor(part(stackA, 5, 0), all_heads(resid), part(stackA, 4, 4), ALU.subtract)\
                        .then_inc(pool_embed_done.sem, 1)
                if route:
                    pool.wait_ge(dve_route_done.sem, dve_route_done.at(turn, "xT"))
                    low_part(xTC_low[:], xTR[:], xTC_high[:]).then_inc(pool_route_done.sem, 1)
                if qkv:
                    pool.wait_ge(dve_qkv_done.sem, dve_qkv_done.at(turn, "mid"))
                    q.tensor_tensor(part(stackB, 3, 3), part(stackB, 2, 1), part(stackB, 4, 4), ALU.add)\
                        .then_inc(pool_qkv_done.sem, 1)
                if load:
                    patches_low(turn, 2)
                if soft:
                    pool.wait_ge(dve_soft_done.sem, dve_soft_done.at(turn, "hm2"))
                    if qkv:
                        pool.wait_ge(act_qkv_done.sem, act_qkv_done.at(turn, "kept"))
                    q.tensor_tensor(H[:], hm[:], tokres[:], ALU.add).then_inc(pool_soft_done.sem, 1)
                    pool.wait_ge(pool_soft_done.sem, pool_soft_done.at(turn, "H"))
                    q.tensor_tensor(H[0:1, 0, :], clsrow[:, 0, :], clsrow[:, 1, :], ALU.add).then_inc(pool_soft_done.sem, 1)

            run_turns(pool, images, body)


def positions():
    seq = ROWS - 1
    i = np.arange(seq, dtype=np.float32)[:, None]
    j = np.arange(W, dtype=np.float32)[None, :]
    even = (np.arange(W) % 2 == 0)[None, :]
    base = np.float32(10000.0)
    one = np.float32(1.0)
    angle = i / np.where(even, base ** (j / np.float32(W)), base ** ((j - one) / np.float32(W)))
    table = np.zeros((ROWS, W), np.float32)
    table[1:] = np.where(even, np.sin(angle), np.cos(angle))
    return table


def kernel(**inputs):
    import concourse.bacc as bacc
    from concourse.bass_utils import run_bass_kernel_spmd as run

    def get(name):
        return np.asarray(inputs[name])

    x = np.ascontiguousarray(get("x"))
    images = x.shape[0]
    arrays = {"x": x.reshape(images, 196, KD), "pos": positions()}
    base = np.zeros((ROWS, W), np.float32)
    base[1] = get("L0_tok_class_token")[0]
    base[2:] = get("L0_tok_b_map")
    arrays["base"] = base
    for name, key in (("ln_w", "L0_tok_ln_w"), ("ln_b", "L0_tok_ln_b")):
        arrays[name] = np.zeros((ROWS, W), np.float32)
        arrays[name][1:] = get(key)
    arrays["wmap"] = get("L0_tok_W_map").T.reshape(KC, 128, W).transpose(1, 0, 2)
    w_a = np.zeros((HC + 1, 2, 3, HC), np.float32)
    for s, (w, bias) in enumerate((("L0_tok_Wq", "L0_tok_bq"), ("L0_tok_Wk", "L0_tok_bk"),
                                   ("L0_tok_Wv", "L0_tok_bv"))):
        for h in range(HEADS):
            c, o = h // 6, (h % 6) * DH
            w_a[o:o + DH, c, s, o:o + DH] = get(w)[h].T
            w_a[HC, c, s, o:o + DH] = get(bias)[h]
    arrays["w_a"] = w_a
    w = get("L0_attn_wqkv").reshape(HEADS, 3, DH, W).transpose(3, 1, 0, 2).reshape(W, 3 * W)
    w_b = np.zeros((HC + 1, 2, 3 * W), np.float32)
    w_b[0:HC] = w.reshape(2, HC, 3 * W).transpose(1, 0, 2)
    w_b[HC, 0] = get("L0_attn_bqkv").reshape(HEADS, 3, DH).transpose(1, 0, 2).reshape(3 * W)
    arrays["w_b"] = w_b
    w_p = np.zeros((4, 32, GROUPS, W), np.float32)
    w_p[:, 0:DH] = get("L0_attn_wp").T.reshape(GROUPS, 4, DH, W).transpose(1, 2, 0, 3)
    arrays["w_p"] = w_p.reshape(128, GROUPS, W)
    arrays["b_p"] = np.broadcast_to(get("L0_attn_bp"), (T, W))
    w_r = np.zeros((HC + 1, 2, NE), np.float32)
    w_r[0:HC] = get("L0_ffn_router_w").T.reshape(2, HC, NE).transpose(1, 0, 2)
    w_r[HC, 0] = get("L0_ffn_router_b")
    arrays["w_r"] = w_r
    w_e = np.zeros((HC + 1, 2, NE * W), np.float32)
    w_e[0:HC] = get("L0_ffn_expert_w").transpose(2, 0, 1).reshape(2, HC, NE * W).transpose(1, 0, 2)
    w_e[HC, 0] = get("L0_ffn_expert_b").reshape(NE * W)
    arrays["w_e"] = w_e
    arrays["cls"] = get("cls_tok").reshape(1, W)
    arrays["eye"] = np.eye(128, dtype=np.float32)
    arrays = {f"{n}_dram": np.ascontiguousarray(a) for n, a in arrays.items()}

    nc = bacc.Bacc("TRN2", target_bir_lowering=False, num_devices=1)
    args = [nc.dram_tensor(n, a.shape, mybir.dt.from_np(a.dtype), kind="ExternalInput").ap()
            for n, a in arrays.items()]
    out = nc.dram_tensor("out_dram", (images, ROWS, W), F32, kind="ExternalOutput").ap()
    tower(nc, *args, out)
    r = run(nc, [arrays], core_ids=[0])
    return r.results[0]["out_dram"]
```
